# Optimizing a Trainium2 kernel written in Bass

```python
import numpy as np
import jax
import jax.numpy as jnp

def _softmax(x, axis=-1):
    return jax.nn.softmax(x, axis=axis)

def _gelu(x):
    return jax.nn.gelu(x, approximate=True)

def _silu(x):
    return jax.nn.silu(x)

def _sigmoid(x):
    return jax.nn.sigmoid(x)

def _layernorm(x, axis=-1, eps=1e-05):
    m = jnp.mean(x, axis=axis, keepdims=True)
    v = jnp.var(x, axis=axis, keepdims=True)
    return (x - m) / jnp.sqrt(v + eps)

def _scatter_add(tgt, idx, src, axis=0):
    return tgt.at[idx].add(src)

def _segment_sum(src, seg, n):
    return jax.ops.segment_sum(src, seg, n)
kernel_name = 'mk_conv_seq_d4_conv_nhwc256_r2_e030a0'

def setup_inputs(seed: int=0):
    np.random.seed(seed)
    _w = jnp.asarray

    def _rec_inputs():
        import jax
        import jax.numpy as jnp
        _gk = jax.random.key(seed)
        x = -0.000125 + 0.9999 * jax.random.normal(jax.random.fold_in(_gk, 1), (4, 64, 128, 128), jnp.float32)
        return x
    x = _rec_inputs()

    def _L0_conv_setup():
        import jax, jax.numpy as jnp
        import numpy as np
        B, C, NB, H, W = (4, 64, 4, 128, 128)
        BT = C // NB
        BN1_EPS, BN2_EPS = (1e-05, 0.001)

        def _bn(z, gamma, beta, mean, var, eps):
            inv = gamma / jnp.sqrt(var + eps)
            return z * inv[None, :, None, None] + (beta - mean * inv)[None, :, None, None]

        def _box_conv(z, x_min, x_max, y_min, y_max):
            S = jnp.pad(jnp.cumsum(jnp.cumsum(z, axis=2), axis=3), ((0, 0), (0, 0), (1, 0), (1, 0)))

            def sample(Sc, u, v):
                u = jnp.clip(u, 0.0, float(H))
                v = jnp.clip(v, 0.0, float(W))
                i0 = jnp.clip(jnp.floor(u), 0.0, float(H - 1)).astype(jnp.int32)
                j0 = jnp.clip(jnp.floor(v), 0.0, float(W - 1)).astype(jnp.int32)
                wu = u - i0
                wv = v - j0
                R = Sc[:, i0, :] * (1.0 - wu)[None, :, None] + Sc[:, i0 + 1, :] * wu[None, :, None]
                return R[:, :, j0] * (1.0 - wv)[None, None, :] + R[:, :, j0 + 1] * wv[None, None, :]

            def one_box(Sc, xmn, xmx, ymn, ymx):
                i = jnp.arange(H, dtype=z.dtype)
                j = jnp.arange(W, dtype=z.dtype)
                F11 = sample(Sc, i + xmx, j + ymx)
                F10 = sample(Sc, i + xmx, j + ymn)
                F01 = sample(Sc, i + xmn, j + ymx)
                F00 = sample(Sc, i + xmn, j + ymn)
                area = (xmx - xmn) * (ymx - ymn)
                return (F11 - F10 - F01 + F00) / area
            per_box = jax.vmap(one_box, in_axes=(None, 0, 0, 0, 0))
            per_chan = jax.vmap(per_box, in_axes=(1, 0, 0, 0, 0))
            out = per_chan(S, x_min, x_max, y_min, y_max)
            return out.transpose(2, 0, 1, 3, 4).reshape(z.shape[0], BT * NB, H, W)
        key = jax.random.key(seed)
        ks = jax.random.split(key, 16)
        x = jax.random.normal(ks[0], (B, C, H, W), dtype=jnp.float32)
        w1 = jax.random.normal(ks[1], (BT, C), dtype=jnp.float32) * 0.1
        bn1_gamma = 1.0 + 0.1 * jax.random.normal(ks[2], (BT,), dtype=jnp.float32)
        bn1_beta = 0.1 * jax.random.normal(ks[3], (BT,), dtype=jnp.float32)
        bn1_mean = 0.1 * jax.random.normal(ks[4], (BT,), dtype=jnp.float32)
        bn1_var = 0.5 + jax.random.uniform(ks[5], (BT,), dtype=jnp.float32)
        x_min = jax.random.uniform(ks[6], (BT, NB), minval=-100.0, maxval=-2.0)
        x_max = x_min + jax.random.uniform(ks[7], (BT, NB), minval=2.0, maxval=100.0)
        y_min = jax.random.uniform(ks[8], (BT, NB), minval=-100.0, maxval=-2.0)
        y_max = y_min + jax.random.uniform(ks[9], (BT, NB), minval=2.0, maxval=100.0)
        bn2_gamma = 1.0 + 0.1 * jax.random.normal(ks[10], (C,), dtype=jnp.float32)
        bn2_beta = 0.1 * jax.random.normal(ks[11], (C,), dtype=jnp.float32)
        bn2_mean = 0.1 * jax.random.normal(ks[12], (C,), dtype=jnp.float32)
        bn2_var = 0.5 + jax.random.uniform(ks[13], (C,), dtype=jnp.float32)
        return dict(x=x, w1=w1, bn1_gamma=bn1_gamma, bn1_beta=bn1_beta, bn1_mean=bn1_mean, bn1_var=bn1_var, x_min=x_min, x_max=x_max, y_min=y_min, y_max=y_max, bn2_gamma=bn2_gamma, bn2_beta=bn2_beta, bn2_mean=bn2_mean, bn2_var=bn2_var)
    _L0_conv_all = _L0_conv_setup()
    _L0_conv_in = {k: v for k, v in _L0_conv_all.items() if k in ('w1', 'bn1_gamma', 'bn1_beta', 'bn1_mean', 'bn1_var', 'x_min', 'x_max', 'y_min', 'y_max', 'bn2_gamma', 'bn2_beta', 'bn2_mean', 'bn2_var')}
    del _L0_conv_all

    def _L1_conv_setup():
        import jax, jax.numpy as jnp
        import numpy as np
        B, C, H, W = (4, 64, 128, 128)
        L = 4
        HID = 256
        THR = 0.01

        def _ln(x, w, b, eps=1e-05):
            mu = jnp.mean(x, axis=-1, keepdims=True)
            v = jnp.mean((x - mu) ** 2, axis=-1, keepdims=True)
            return (x - mu) * jax.lax.rsqrt(v + eps) * w + b

        def _block(x, ln1w, ln1b, ln2w, ln2b, w1, w2, b1, b2, mw1, mb1, mw2, mb2):
            residual = x
            xp = jnp.transpose(x, (0, 2, 3, 1))
            xn = _ln(xp, ln1w, ln1b)
            xf = jnp.fft.rfft2(xn, axes=(1, 2), norm='ortho')
            xr, xi = (xf.real, xf.imag)
            o1r = jnp.einsum('bhwc,cd->bhwd', xr, w1[0]) - jnp.einsum('bhwc,cd->bhwd', xi, w1[1]) + b1[0]
            o1i = jnp.einsum('bhwc,cd->bhwd', xr, w1[1]) + jnp.einsum('bhwc,cd->bhwd', xi, w1[0]) + b1[1]
            o1r = jax.nn.relu(o1r)
            o1i = jax.nn.relu(o1i)
            o2r = jnp.einsum('bhwc,cd->bhwd', o1r, w2[0]) - jnp.einsum('bhwc,cd->bhwd', o1i, w2[1]) + b2[0]
            o2i = jnp.einsum('bhwc,cd->bhwd', o1r, w2[1]) + jnp.einsum('bhwc,cd->bhwd', o1i, w2[0]) + b2[1]
            mask = ((jnp.abs(o2r) > THR) | (jnp.abs(o2i) > THR)).astype(o2r.dtype)
            o2r = o2r * mask
            o2i = o2i * mask
            xc = jax.lax.complex(o2r, o2i)
            xs = jnp.fft.irfft2(xc, s=(H, W), axes=(1, 2), norm='ortho')
            x = residual + jnp.transpose(xs, (0, 3, 1, 2))
            xp2 = _ln(jnp.transpose(x, (0, 2, 3, 1)), ln2w, ln2b)
            h = jax.nn.gelu(xp2 @ mw1 + mb1, approximate=False)
            m = h @ mw2 + mb2
            return x + jnp.transpose(m, (0, 3, 1, 2))
        key = jax.random.key(seed)
        ks = jax.random.split(key, 5)
        x = jax.random.normal(ks[0], (B, C, H, W), jnp.float32)
        w1 = jax.random.normal(ks[1], (L, 2, C, C), jnp.float32) * 0.02
        w2 = jax.random.normal(ks[2], (L, 2, C, C), jnp.float32) * 0.02
        b1 = jnp.zeros((L, 2, C), jnp.float32)
        b2 = jnp.zeros((L, 2, C), jnp.float32)
        ln1_w = jnp.ones((L, C), jnp.float32)
        ln1_b = jnp.zeros((L, C), jnp.float32)
        ln2_w = jnp.ones((L, C), jnp.float32)
        ln2_b = jnp.zeros((L, C), jnp.float32)
        mlp_w1 = jax.random.normal(ks[3], (L, C, HID), jnp.float32) * 0.02
        mlp_b1 = jnp.zeros((L, HID), jnp.float32)
        mlp_w2 = jax.random.normal(ks[4], (L, HID, C), jnp.float32) * 0.02
        mlp_b2 = jnp.zeros((L, C), jnp.float32)
        return dict(x=x, ln1_w=ln1_w, ln1_b=ln1_b, ln2_w=ln2_w, ln2_b=ln2_b, w1=w1, w2=w2, b1=b1, b2=b2, mlp_w1=mlp_w1, mlp_b1=mlp_b1, mlp_w2=mlp_w2, mlp_b2=mlp_b2)
    _L1_conv_all = _L1_conv_setup()
    _L1_conv_in = {k: v for k, v in _L1_conv_all.items() if k in ('ln1_w', 'ln1_b', 'ln2_w', 'ln2_b', 'w1', 'w2', 'b1', 'b2', 'mlp_w1', 'mlp_b1', 'mlp_w2', 'mlp_b2')}
    del _L1_conv_all

    def _L2_conv_setup():
        import jax, jax.numpy as jnp
        import numpy as np
        B, C, NB, H, W = (4, 64, 4, 128, 128)
        BT = C // NB
        BN1_EPS, BN2_EPS = (1e-05, 0.001)

        def _bn(z, gamma, beta, mean, var, eps):
            inv = gamma / jnp.sqrt(var + eps)
            return z * inv[None, :, None, None] + (beta - mean * inv)[None, :, None, None]

        def _box_conv(z, x_min, x_max, y_min, y_max):
            S = jnp.pad(jnp.cumsum(jnp.cumsum(z, axis=2), axis=3), ((0, 0), (0, 0), (1, 0), (1, 0)))

            def sample(Sc, u, v):
                u = jnp.clip(u, 0.0, float(H))
                v = jnp.clip(v, 0.0, float(W))
                i0 = jnp.clip(jnp.floor(u), 0.0, float(H - 1)).astype(jnp.int32)
                j0 = jnp.clip(jnp.floor(v), 0.0, float(W - 1)).astype(jnp.int32)
                wu = u - i0
                wv = v - j0
                R = Sc[:, i0, :] * (1.0 - wu)[None, :, None] + Sc[:, i0 + 1, :] * wu[None, :, None]
                return R[:, :, j0] * (1.0 - wv)[None, None, :] + R[:, :, j0 + 1] * wv[None, None, :]

            def one_box(Sc, xmn, xmx, ymn, ymx):
                i = jnp.arange(H, dtype=z.dtype)
                j = jnp.arange(W, dtype=z.dtype)
                F11 = sample(Sc, i + xmx, j + ymx)
                F10 = sample(Sc, i + xmx, j + ymn)
                F01 = sample(Sc, i + xmn, j + ymx)
                F00 = sample(Sc, i + xmn, j + ymn)
                area = (xmx - xmn) * (ymx - ymn)
                return (F11 - F10 - F01 + F00) / area
            per_box = jax.vmap(one_box, in_axes=(None, 0, 0, 0, 0))
            per_chan = jax.vmap(per_box, in_axes=(1, 0, 0, 0, 0))
            out = per_chan(S, x_min, x_max, y_min, y_max)
            return out.transpose(2, 0, 1, 3, 4).reshape(z.shape[0], BT * NB, H, W)
        key = jax.random.key(seed)
        ks = jax.random.split(key, 16)
        x = jax.random.normal(ks[0], (B, C, H, W), dtype=jnp.float32)
        w1 = jax.random.normal(ks[1], (BT, C), dtype=jnp.float32) * 0.1
        bn1_gamma = 1.0 + 0.1 * jax.random.normal(ks[2], (BT,), dtype=jnp.float32)
        bn1_beta = 0.1 * jax.random.normal(ks[3], (BT,), dtype=jnp.float32)
        bn1_mean = 0.1 * jax.random.normal(ks[4], (BT,), dtype=jnp.float32)
        bn1_var = 0.5 + jax.random.uniform(ks[5], (BT,), dtype=jnp.float32)
        x_min = jax.random.uniform(ks[6], (BT, NB), minval=-100.0, maxval=-2.0)
        x_max = x_min + jax.random.uniform(ks[7], (BT, NB), minval=2.0, maxval=100.0)
        y_min = jax.random.uniform(ks[8], (BT, NB), minval=-100.0, maxval=-2.0)
        y_max = y_min + jax.random.uniform(ks[9], (BT, NB), minval=2.0, maxval=100.0)
        bn2_gamma = 1.0 + 0.1 * jax.random.normal(ks[10], (C,), dtype=jnp.float32)
        bn2_beta = 0.1 * jax.random.normal(ks[11], (C,), dtype=jnp.float32)
        bn2_mean = 0.1 * jax.random.normal(ks[12], (C,), dtype=jnp.float32)
        bn2_var = 0.5 + jax.random.uniform(ks[13], (C,), dtype=jnp.float32)
        return dict(x=x, w1=w1, bn1_gamma=bn1_gamma, bn1_beta=bn1_beta, bn1_mean=bn1_mean, bn1_var=bn1_var, x_min=x_min, x_max=x_max, y_min=y_min, y_max=y_max, bn2_gamma=bn2_gamma, bn2_beta=bn2_beta, bn2_mean=bn2_mean, bn2_var=bn2_var)
    _L2_conv_all = _L2_conv_setup()
    _L2_conv_in = {k: v for k, v in _L2_conv_all.items() if k in ('w1', 'bn1_gamma', 'bn1_beta', 'bn1_mean', 'bn1_var', 'x_min', 'x_max', 'y_min', 'y_max', 'bn2_gamma', 'bn2_beta', 'bn2_mean', 'bn2_var')}
    del _L2_conv_all

    def _L3_conv_setup():
        import jax, jax.numpy as jnp
        import numpy as np
        B, C, NB, H, W = (4, 64, 4, 128, 128)
        BT = C // NB
        BN1_EPS, BN2_EPS = (1e-05, 0.001)

        def _bn(z, gamma, beta, mean, var, eps):
            inv = gamma / jnp.sqrt(var + eps)
            return z * inv[None, :, None, None] + (beta - mean * inv)[None, :, None, None]

        def _box_conv(z, x_min, x_max, y_min, y_max):
            S = jnp.pad(jnp.cumsum(jnp.cumsum(z, axis=2), axis=3), ((0, 0), (0, 0), (1, 0), (1, 0)))

            def sample(Sc, u, v):
                u = jnp.clip(u, 0.0, float(H))
                v = jnp.clip(v, 0.0, float(W))
                i0 = jnp.clip(jnp.floor(u), 0.0, float(H - 1)).astype(jnp.int32)
                j0 = jnp.clip(jnp.floor(v), 0.0, float(W - 1)).astype(jnp.int32)
                wu = u - i0
                wv = v - j0
                R = Sc[:, i0, :] * (1.0 - wu)[None, :, None] + Sc[:, i0 + 1, :] * wu[None, :, None]
                return R[:, :, j0] * (1.0 - wv)[None, None, :] + R[:, :, j0 + 1] * wv[None, None, :]

            def one_box(Sc, xmn, xmx, ymn, ymx):
                i = jnp.arange(H, dtype=z.dtype)
                j = jnp.arange(W, dtype=z.dtype)
                F11 = sample(Sc, i + xmx, j + ymx)
                F10 = sample(Sc, i + xmx, j + ymn)
                F01 = sample(Sc, i + xmn, j + ymx)
                F00 = sample(Sc, i + xmn, j + ymn)
                area = (xmx - xmn) * (ymx - ymn)
                return (F11 - F10 - F01 + F00) / area
            per_box = jax.vmap(one_box, in_axes=(None, 0, 0, 0, 0))
            per_chan = jax.vmap(per_box, in_axes=(1, 0, 0, 0, 0))
            out = per_chan(S, x_min, x_max, y_min, y_max)
            return out.transpose(2, 0, 1, 3, 4).reshape(z.shape[0], BT * NB, H, W)
        key = jax.random.key(seed)
        ks = jax.random.split(key, 16)
        x = jax.random.normal(ks[0], (B, C, H, W), dtype=jnp.float32)
        w1 = jax.random.normal(ks[1], (BT, C), dtype=jnp.float32) * 0.1
        bn1_gamma = 1.0 + 0.1 * jax.random.normal(ks[2], (BT,), dtype=jnp.float32)
        bn1_beta = 0.1 * jax.random.normal(ks[3], (BT,), dtype=jnp.float32)
        bn1_mean = 0.1 * jax.random.normal(ks[4], (BT,), dtype=jnp.float32)
        bn1_var = 0.5 + jax.random.uniform(ks[5], (BT,), dtype=jnp.float32)
        x_min = jax.random.uniform(ks[6], (BT, NB), minval=-100.0, maxval=-2.0)
        x_max = x_min + jax.random.uniform(ks[7], (BT, NB), minval=2.0, maxval=100.0)
        y_min = jax.random.uniform(ks[8], (BT, NB), minval=-100.0, maxval=-2.0)
        y_max = y_min + jax.random.uniform(ks[9], (BT, NB), minval=2.0, maxval=100.0)
        bn2_gamma = 1.0 + 0.1 * jax.random.normal(ks[10], (C,), dtype=jnp.float32)
        bn2_beta = 0.1 * jax.random.normal(ks[11], (C,), dtype=jnp.float32)
        bn2_mean = 0.1 * jax.random.normal(ks[12], (C,), dtype=jnp.float32)
        bn2_var = 0.5 + jax.random.uniform(ks[13], (C,), dtype=jnp.float32)
        return dict(x=x, w1=w1, bn1_gamma=bn1_gamma, bn1_beta=bn1_beta, bn1_mean=bn1_mean, bn1_var=bn1_var, x_min=x_min, x_max=x_max, y_min=y_min, y_max=y_max, bn2_gamma=bn2_gamma, bn2_beta=bn2_beta, bn2_mean=bn2_mean, bn2_var=bn2_var)
    _L3_conv_all = _L3_conv_setup()
    _L3_conv_in = {k: v for k, v in _L3_conv_all.items() if k in ('w1', 'bn1_gamma', 'bn1_beta', 'bn1_mean', 'bn1_var', 'x_min', 'x_max', 'y_min', 'y_max', 'bn2_gamma', 'bn2_beta', 'bn2_mean', 'bn2_var')}
    del _L3_conv_all
    return {'x': x, 'L0_conv_w1': _L0_conv_in['w1'], 'L0_conv_bn1_gamma': _L0_conv_in['bn1_gamma'], 'L0_conv_bn1_beta': _L0_conv_in['bn1_beta'], 'L0_conv_bn1_mean': _L0_conv_in['bn1_mean'], 'L0_conv_bn1_var': _L0_conv_in['bn1_var'], 'L0_conv_x_min': _L0_conv_in['x_min'], 'L0_conv_x_max': _L0_conv_in['x_max'], 'L0_conv_y_min': _L0_conv_in['y_min'], 'L0_conv_y_max': _L0_conv_in['y_max'], 'L0_conv_bn2_gamma': _L0_conv_in['bn2_gamma'], 'L0_conv_bn2_beta': _L0_conv_in['bn2_beta'], 'L0_conv_bn2_mean': _L0_conv_in['bn2_mean'], 'L0_conv_bn2_var': _L0_conv_in['bn2_var'], 'L1_conv_ln1_w': _L1_conv_in['ln1_w'], 'L1_conv_ln1_b': _L1_conv_in['ln1_b'], 'L1_conv_ln2_w': _L1_conv_in['ln2_w'], 'L1_conv_ln2_b': _L1_conv_in['ln2_b'], 'L1_conv_w1': _L1_conv_in['w1'], 'L1_conv_w2': _L1_conv_in['w2'], 'L1_conv_b1': _L1_conv_in['b1'], 'L1_conv_b2': _L1_conv_in['b2'], 'L1_conv_mlp_w1': _L1_conv_in['mlp_w1'], 'L1_conv_mlp_b1': _L1_conv_in['mlp_b1'], 'L1_conv_mlp_w2': _L1_conv_in['mlp_w2'], 'L1_conv_mlp_b2': _L1_conv_in['mlp_b2'], 'L2_conv_w1': _L2_conv_in['w1'], 'L2_conv_bn1_gamma': _L2_conv_in['bn1_gamma'], 'L2_conv_bn1_beta': _L2_conv_in['bn1_beta'], 'L2_conv_bn1_mean': _L2_conv_in['bn1_mean'], 'L2_conv_bn1_var': _L2_conv_in['bn1_var'], 'L2_conv_x_min': _L2_conv_in['x_min'], 'L2_conv_x_max': _L2_conv_in['x_max'], 'L2_conv_y_min': _L2_conv_in['y_min'], 'L2_conv_y_max': _L2_conv_in['y_max'], 'L2_conv_bn2_gamma': _L2_conv_in['bn2_gamma'], 'L2_conv_bn2_beta': _L2_conv_in['bn2_beta'], 'L2_conv_bn2_mean': _L2_conv_in['bn2_mean'], 'L2_conv_bn2_var': _L2_conv_in['bn2_var'], 'L3_conv_w1': _L3_conv_in['w1'], 'L3_conv_bn1_gamma': _L3_conv_in['bn1_gamma'], 'L3_conv_bn1_beta': _L3_conv_in['bn1_beta'], 'L3_conv_bn1_mean': _L3_conv_in['bn1_mean'], 'L3_conv_bn1_var': _L3_conv_in['bn1_var'], 'L3_conv_x_min': _L3_conv_in['x_min'], 'L3_conv_x_max': _L3_conv_in['x_max'], 'L3_conv_y_min': _L3_conv_in['y_min'], 'L3_conv_y_max': _L3_conv_in['y_max'], 'L3_conv_bn2_gamma': _L3_conv_in['bn2_gamma'], 'L3_conv_bn2_beta': _L3_conv_in['bn2_beta'], 'L3_conv_bn2_mean': _L3_conv_in['bn2_mean'], 'L3_conv_bn2_var': _L3_conv_in['bn2_var']}

def reference(x, L0_conv_w1, L0_conv_bn1_gamma, L0_conv_bn1_beta, L0_conv_bn1_mean, L0_conv_bn1_var, L0_conv_x_min, L0_conv_x_max, L0_conv_y_min, L0_conv_y_max, L0_conv_bn2_gamma, L0_conv_bn2_beta, L0_conv_bn2_mean, L0_conv_bn2_var, L1_conv_ln1_w, L1_conv_ln1_b, L1_conv_ln2_w, L1_conv_ln2_b, L1_conv_w1, L1_conv_w2, L1_conv_b1, L1_conv_b2, L1_conv_mlp_w1, L1_conv_mlp_b1, L1_conv_mlp_w2, L1_conv_mlp_b2, L2_conv_w1, L2_conv_bn1_gamma, L2_conv_bn1_beta, L2_conv_bn1_mean, L2_conv_bn1_var, L2_conv_x_min, L2_conv_x_max, L2_conv_y_min, L2_conv_y_max, L2_conv_bn2_gamma, L2_conv_bn2_beta, L2_conv_bn2_mean, L2_conv_bn2_var, L3_conv_w1, L3_conv_bn1_gamma, L3_conv_bn1_beta, L3_conv_bn1_mean, L3_conv_bn1_var, L3_conv_x_min, L3_conv_x_max, L3_conv_y_min, L3_conv_y_max, L3_conv_bn2_gamma, L3_conv_bn2_beta, L3_conv_bn2_mean, L3_conv_bn2_var):
    import jax
    import jax.numpy as jnp

    def _L0_conv_ref(x, w1, bn1_gamma, bn1_beta, bn1_mean, bn1_var, x_min, x_max, y_min, y_max, bn2_gamma, bn2_beta, bn2_mean, bn2_var):
        import jax, jax.numpy as jnp
        import numpy as np
        B, C, NB, H, W = (4, 64, 4, 128, 128)
        BT = C // NB
        BN1_EPS, BN2_EPS = (1e-05, 0.001)

        def _bn(z, gamma, beta, mean, var, eps):
            inv = gamma / jnp.sqrt(var + eps)
            return z * inv[None, :, None, None] + (beta - mean * inv)[None, :, None, None]

        def _box_conv(z, x_min, x_max, y_min, y_max):
            S = jnp.pad(jnp.cumsum(jnp.cumsum(z, axis=2), axis=3), ((0, 0), (0, 0), (1, 0), (1, 0)))

            def sample(Sc, u, v):
                u = jnp.clip(u, 0.0, float(H))
                v = jnp.clip(v, 0.0, float(W))
                i0 = jnp.clip(jnp.floor(u), 0.0, float(H - 1)).astype(jnp.int32)
                j0 = jnp.clip(jnp.floor(v), 0.0, float(W - 1)).astype(jnp.int32)
                wu = u - i0
                wv = v - j0
                R = Sc[:, i0, :] * (1.0 - wu)[None, :, None] + Sc[:, i0 + 1, :] * wu[None, :, None]
                return R[:, :, j0] * (1.0 - wv)[None, None, :] + R[:, :, j0 + 1] * wv[None, None, :]

            def one_box(Sc, xmn, xmx, ymn, ymx):
                i = jnp.arange(H, dtype=z.dtype)
                j = jnp.arange(W, dtype=z.dtype)
                F11 = sample(Sc, i + xmx, j + ymx)
                F10 = sample(Sc, i + xmx, j + ymn)
                F01 = sample(Sc, i + xmn, j + ymx)
                F00 = sample(Sc, i + xmn, j + ymn)
                area = (xmx - xmn) * (ymx - ymn)
                return (F11 - F10 - F01 + F00) / area
            per_box = jax.vmap(one_box, in_axes=(None, 0, 0, 0, 0))
            per_chan = jax.vmap(per_box, in_axes=(1, 0, 0, 0, 0))
            out = per_chan(S, x_min, x_max, y_min, y_max)
            return out.transpose(2, 0, 1, 3, 4).reshape(z.shape[0], BT * NB, H, W)
        h = jnp.einsum('bchw,kc->bkhw', x, w1)
        h = _bn(h, bn1_gamma, bn1_beta, bn1_mean, bn1_var, BN1_EPS)
        h = _box_conv(h, x_min, x_max, y_min, y_max)
        h = _bn(h, bn2_gamma, bn2_beta, bn2_mean, bn2_var, BN2_EPS)
        h = jax.nn.relu(h)
        return jax.nn.relu(x + h)

    def _L1_conv_ref(x, ln1_w, ln1_b, ln2_w, ln2_b, w1, w2, b1, b2, mlp_w1, mlp_b1, mlp_w2, mlp_b2):
        import jax, jax.numpy as jnp
        import numpy as np
        B, C, H, W = (4, 64, 128, 128)
        L = 4
        HID = 256
        THR = 0.01

        def _ln(x, w, b, eps=1e-05):
            mu = jnp.mean(x, axis=-1, keepdims=True)
            v = jnp.mean((x - mu) ** 2, axis=-1, keepdims=True)
            return (x - mu) * jax.lax.rsqrt(v + eps) * w + b

        def _block(x, ln1w, ln1b, ln2w, ln2b, w1, w2, b1, b2, mw1, mb1, mw2, mb2):
            residual = x
            xp = jnp.transpose(x, (0, 2, 3, 1))
            xn = _ln(xp, ln1w, ln1b)
            xf = jnp.fft.rfft2(xn, axes=(1, 2), norm='ortho')
            xr, xi = (xf.real, xf.imag)
            o1r = jnp.einsum('bhwc,cd->bhwd', xr, w1[0]) - jnp.einsum('bhwc,cd->bhwd', xi, w1[1]) + b1[0]
            o1i = jnp.einsum('bhwc,cd->bhwd', xr, w1[1]) + jnp.einsum('bhwc,cd->bhwd', xi, w1[0]) + b1[1]
            o1r = jax.nn.relu(o1r)
            o1i = jax.nn.relu(o1i)
            o2r = jnp.einsum('bhwc,cd->bhwd', o1r, w2[0]) - jnp.einsum('bhwc,cd->bhwd', o1i, w2[1]) + b2[0]
            o2i = jnp.einsum('bhwc,cd->bhwd', o1r, w2[1]) + jnp.einsum('bhwc,cd->bhwd', o1i, w2[0]) + b2[1]
            mask = ((jnp.abs(o2r) > THR) | (jnp.abs(o2i) > THR)).astype(o2r.dtype)
            o2r = o2r * mask
            o2i = o2i * mask
            xc = jax.lax.complex(o2r, o2i)
            xs = jnp.fft.irfft2(xc, s=(H, W), axes=(1, 2), norm='ortho')
            x = residual + jnp.transpose(xs, (0, 3, 1, 2))
            xp2 = _ln(jnp.transpose(x, (0, 2, 3, 1)), ln2w, ln2b)
            h = jax.nn.gelu(xp2 @ mw1 + mb1, approximate=False)
            m = h @ mw2 + mb2
            return x + jnp.transpose(m, (0, 3, 1, 2))
        for i in range(L):
            x = _block(x, ln1_w[i], ln1_b[i], ln2_w[i], ln2_b[i], w1[i], w2[i], b1[i][:, None, None, :], b2[i][:, None, None, :], mlp_w1[i], mlp_b1[i], mlp_w2[i], mlp_b2[i])
        return x

    def _L2_conv_ref(x, w1, bn1_gamma, bn1_beta, bn1_mean, bn1_var, x_min, x_max, y_min, y_max, bn2_gamma, bn2_beta, bn2_mean, bn2_var):
        import jax, jax.numpy as jnp
        import numpy as np
        B, C, NB, H, W = (4, 64, 4, 128, 128)
        BT = C // NB
        BN1_EPS, BN2_EPS = (1e-05, 0.001)

        def _bn(z, gamma, beta, mean, var, eps):
            inv = gamma / jnp.sqrt(var + eps)
            return z * inv[None, :, None, None] + (beta - mean * inv)[None, :, None, None]

        def _box_conv(z, x_min, x_max, y_min, y_max):
            S = jnp.pad(jnp.cumsum(jnp.cumsum(z, axis=2), axis=3), ((0, 0), (0, 0), (1, 0), (1, 0)))

            def sample(Sc, u, v):
                u = jnp.clip(u, 0.0, float(H))
                v = jnp.clip(v, 0.0, float(W))
                i0 = jnp.clip(jnp.floor(u), 0.0, float(H - 1)).astype(jnp.int32)
                j0 = jnp.clip(jnp.floor(v), 0.0, float(W - 1)).astype(jnp.int32)
                wu = u - i0
                wv = v - j0
                R = Sc[:, i0, :] * (1.0 - wu)[None, :, None] + Sc[:, i0 + 1, :] * wu[None, :, None]
                return R[:, :, j0] * (1.0 - wv)[None, None, :] + R[:, :, j0 + 1] * wv[None, None, :]

            def one_box(Sc, xmn, xmx, ymn, ymx):
                i = jnp.arange(H, dtype=z.dtype)
                j = jnp.arange(W, dtype=z.dtype)
                F11 = sample(Sc, i + xmx, j + ymx)
                F10 = sample(Sc, i + xmx, j + ymn)
                F01 = sample(Sc, i + xmn, j + ymx)
                F00 = sample(Sc, i + xmn, j + ymn)
                area = (xmx - xmn) * (ymx - ymn)
                return (F11 - F10 - F01 + F00) / area
            per_box = jax.vmap(one_box, in_axes=(None, 0, 0, 0, 0))
            per_chan = jax.vmap(per_box, in_axes=(1, 0, 0, 0, 0))
            out = per_chan(S, x_min, x_max, y_min, y_max)
            return out.transpose(2, 0, 1, 3, 4).reshape(z.shape[0], BT * NB, H, W)
        h = jnp.einsum('bchw,kc->bkhw', x, w1)
        h = _bn(h, bn1_gamma, bn1_beta, bn1_mean, bn1_var, BN1_EPS)
        h = _box_conv(h, x_min, x_max, y_min, y_max)
        h = _bn(h, bn2_gamma, bn2_beta, bn2_mean, bn2_var, BN2_EPS)
        h = jax.nn.relu(h)
        return jax.nn.relu(x + h)

    def _L3_conv_ref(x, w1, bn1_gamma, bn1_beta, bn1_mean, bn1_var, x_min, x_max, y_min, y_max, bn2_gamma, bn2_beta, bn2_mean, bn2_var):
        import jax, jax.numpy as jnp
        import numpy as np
        B, C, NB, H, W = (4, 64, 4, 128, 128)
        BT = C // NB
        BN1_EPS, BN2_EPS = (1e-05, 0.001)

        def _bn(z, gamma, beta, mean, var, eps):
            inv = gamma / jnp.sqrt(var + eps)
            return z * inv[None, :, None, None] + (beta - mean * inv)[None, :, None, None]

        def _box_conv(z, x_min, x_max, y_min, y_max):
            S = jnp.pad(jnp.cumsum(jnp.cumsum(z, axis=2), axis=3), ((0, 0), (0, 0), (1, 0), (1, 0)))

            def sample(Sc, u, v):
                u = jnp.clip(u, 0.0, float(H))
                v = jnp.clip(v, 0.0, float(W))
                i0 = jnp.clip(jnp.floor(u), 0.0, float(H - 1)).astype(jnp.int32)
                j0 = jnp.clip(jnp.floor(v), 0.0, float(W - 1)).astype(jnp.int32)
                wu = u - i0
                wv = v - j0
                R = Sc[:, i0, :] * (1.0 - wu)[None, :, None] + Sc[:, i0 + 1, :] * wu[None, :, None]
                return R[:, :, j0] * (1.0 - wv)[None, None, :] + R[:, :, j0 + 1] * wv[None, None, :]

            def one_box(Sc, xmn, xmx, ymn, ymx):
                i = jnp.arange(H, dtype=z.dtype)
                j = jnp.arange(W, dtype=z.dtype)
                F11 = sample(Sc, i + xmx, j + ymx)
                F10 = sample(Sc, i + xmx, j + ymn)
                F01 = sample(Sc, i + xmn, j + ymx)
                F00 = sample(Sc, i + xmn, j + ymn)
                area = (xmx - xmn) * (ymx - ymn)
                return (F11 - F10 - F01 + F00) / area
            per_box = jax.vmap(one_box, in_axes=(None, 0, 0, 0, 0))
            per_chan = jax.vmap(per_box, in_axes=(1, 0, 0, 0, 0))
            out = per_chan(S, x_min, x_max, y_min, y_max)
            return out.transpose(2, 0, 1, 3, 4).reshape(z.shape[0], BT * NB, H, W)
        h = jnp.einsum('bchw,kc->bkhw', x, w1)
        h = _bn(h, bn1_gamma, bn1_beta, bn1_mean, bn1_var, BN1_EPS)
        h = _box_conv(h, x_min, x_max, y_min, y_max)
        h = _bn(h, bn2_gamma, bn2_beta, bn2_mean, bn2_var, BN2_EPS)
        h = jax.nn.relu(h)
        return jax.nn.relu(x + h)

    def _gn(v, G=32, eps=1e-05):
        B_, H_, W_, C_ = v.shape
        g = v.reshape(B_, H_, W_, G, C_ // G)
        m = jnp.mean(g, axis=(1, 2, 4), keepdims=True)
        s = jnp.var(g, axis=(1, 2, 4), keepdims=True)
        return ((g - m) / jnp.sqrt(s + eps)).reshape(v.shape)

    def _ln_c(v, eps=1e-06):
        m = jnp.mean(v, axis=-1, keepdims=True)
        s = jnp.var(v, axis=-1, keepdims=True)
        return (v - m) / jnp.sqrt(s + eps)

    def _ln_t(v, eps=1e-05):
        m = jnp.mean(v, axis=-1, keepdims=True)
        s = jnp.var(v, axis=-1, keepdims=True)
        return (v - m) / jnp.sqrt(s + eps)

    def _to_tokens(v):
        B_, H_, W_, C_ = v.shape
        return v.reshape(B_, H_ * W_, C_)

    def _from_tokens(t, like):
        return t.reshape(like.shape)
    x = _L0_conv_ref(x, L0_conv_w1, L0_conv_bn1_gamma, L0_conv_bn1_beta, L0_conv_bn1_mean, L0_conv_bn1_var, L0_conv_x_min, L0_conv_x_max, L0_conv_y_min, L0_conv_y_max, L0_conv_bn2_gamma, L0_conv_bn2_beta, L0_conv_bn2_mean, L0_conv_bn2_var)
    x = _L1_conv_ref(x, L1_conv_ln1_w, L1_conv_ln1_b, L1_conv_ln2_w, L1_conv_ln2_b, L1_conv_w1, L1_conv_w2, L1_conv_b1, L1_conv_b2, L1_conv_mlp_w1, L1_conv_mlp_b1, L1_conv_mlp_w2, L1_conv_mlp_b2)
    x = _L2_conv_ref(x, L2_conv_w1, L2_conv_bn1_gamma, L2_conv_bn1_beta, L2_conv_bn1_mean, L2_conv_bn1_var, L2_conv_x_min, L2_conv_x_max, L2_conv_y_min, L2_conv_y_max, L2_conv_bn2_gamma, L2_conv_bn2_beta, L2_conv_bn2_mean, L2_conv_bn2_var)
    x = _L3_conv_ref(x, L3_conv_w1, L3_conv_bn1_gamma, L3_conv_bn1_beta, L3_conv_bn1_mean, L3_conv_bn1_var, L3_conv_x_min, L3_conv_x_max, L3_conv_y_min, L3_conv_y_max, L3_conv_bn2_gamma, L3_conv_bn2_beta, L3_conv_bn2_mean, L3_conv_bn2_var)
    return x

_drawn_inputs = setup_inputs


def setup_inputs(seed=0):
    import zlib

    import numpy as np

    out = dict(_drawn_inputs(seed))
    spreads = {'L1_conv_ln1_w': (1.0, 0.6),
     'L1_conv_ln1_b': (0.0, 0.8),
     'L1_conv_ln2_w': (1.0, 0.6),
     'L1_conv_ln2_b': (0.0, 0.8),
     'L1_conv_b1': (0.0, 0.37),
     'L1_conv_b2': (0.0, 0.1),
     'L1_conv_mlp_b1': (0.0, 0.1),
     'L1_conv_mlp_b2': (0.0, 0.1)}
    factors = {'L0_conv_w1': 5.051,
     'L0_conv_bn1_gamma': 26.212,
     'L0_conv_bn1_var': 26.302,
     'L0_conv_x_min': 2.853,
     'L0_conv_x_max': 2.671,
     'L0_conv_y_min': 3.513,
     'L0_conv_y_max': 2.686,
     'L0_conv_bn2_gamma': 6.216,
     'L0_conv_bn2_var': 3.944,
     'L2_conv_bn1_gamma': 2.93,
     'L2_conv_bn1_var': 3.172,
     'L3_conv_bn1_gamma': 3.343}
    for name, (base, spread) in spreads.items():
        noise = np.random.default_rng([zlib.crc32(name.encode()), seed]).standard_normal(out[name].shape)
        drawn = base * np.exp(spread * noise) if base else spread * noise
        out[name] = jnp.asarray(drawn.astype(out[name].dtype))
    for name, factor in factors.items():
        out[name] = (out[name] * factor).astype(out[name].dtype)
    return out
```

```python
from contextlib import ExitStack

import numpy as np

import concourse.bass as bass
from concourse import mybir

F32 = mybir.dt.float32
ALU = mybir.AluOpType
ACT = mybir.ActivationFunctionType
AX = mybir.AxisListType

P = 128
B, C = 4, 64
NB = 4
K = C // NB
HALF = P // 2
L = 4
HID = 256
HC = HID // P
KW = P // 2 + 1
THR = 0.01
BANK = 512

BN1_EPS, BN2_EPS, LN_EPS = 1e-5, 1e-3, 1e-5

DELTA, IDENT, DFT_W, COS, SIN, IDFT_W, CENTRE, N_CONST = range(8)


def constants():
    n = np.arange(P)
    out = np.zeros((N_CONST, P, P))
    out[DELTA] = n[None, :] - n[:, None]
    out[IDENT] = np.eye(P)
    turn = 2 * np.pi * (np.outer(n, n) % P) / P
    out[COS], out[SIN] = np.cos(turn), np.sin(turn)
    out[DFT_W][:, :KW] = np.cos(turn[:, :KW]) / P
    out[DFT_W][:, KW:] = -np.sin(turn[:, 1:KW - 1]) / P
    out[IDFT_W][:HALF] = 2 * np.cos(turn[:HALF]) / P
    out[IDFT_W][0] = 1 / P
    out[IDFT_W][HALF] = np.cos(turn[HALF]) / P
    out[IDFT_W][HALF + 1:] = -2 * np.sin(turn[1:HALF]) / P
    for h in range(2):
        out[CENTRE][h * C:(h + 1) * C, h * C:(h + 1) * C] = np.eye(C) - 1 / C
    return out.astype(np.float32)


def chain(eng, sem, count, ins):
    count[0] += 1
    ins.then_inc(sem, 1)
    eng.wait_ge(sem, count[0])


def box_layer(nc, tag, const, w, turns, src, dst, zd, K_UNROLL=4):
    CH8 = HALF * P // BANK
    with ExitStack() as ctx:
        def sb(name, shape):
            return ctx.enter_context(nc.sbuf_tensor(f"{tag}_{name}", shape, F32))

        def psum(name):
            return ctx.enter_context(nc.psum_tensor(f"{tag}_{name}", [P, BANK], F32))

        def sem(name):
            return ctx.enter_context(nc.semaphore(f"{tag}_{name}"))

        banks = [psum(f"bank{i}") for i in range(8)]
        delta, ident = sb("delta", [P, P]), sb("ident", [P, P])
        edges = sb("edges", [P, 2, 2, C])
        bn2 = sb("bn2", [P, 4, C])
        scale2, bias2, t2 = sb("scale2", [P, C]), sb("bias2", [P, C]), sb("t2", [P, 3, C])
        bn1r = sb("bn1r", [P, 2, K])
        bn1c = sb("bn1c", [2 * K, 4])
        inv1 = sb("inv1", [P, K])
        inv1c, bias1 = sb("inv1c", [2 * K, 1]), sb("bias1", [2 * K, 2])
        w1t = sb("w1t", [P, K])
        w1bd = sb("w1bd", [P, 2 * K])

        s_par, s_step, s_sqrt, s_var, s_w1 = (sem(x) for x in ("par", "step", "sqrt", "var", "w1"))
        s_act0 = sem("act0")
        s_x = [sem("x0"), sem("x1")]
        s_z_mm, s_z_dve, s_z_act = sem("z_mm"), sem("z_dve"), sem("z_act")
        s_z_out = [sem("z_out0"), sem("z_out1")]

        def bc(a):
            return a.partition_broadcast(P)

        with ExitStack() as zctx:
            xc = zctx.enter_context(nc.sbuf_tensor(f"{tag}_xc", [P, 2, HALF * P], F32))
            zs = zctx.enter_context(nc.sbuf_tensor(f"{tag}_zs", [2 * K, 2, HALF * P], F32))
            with nc.Block() as block:
                @block.sync
                def _(sp):
                    par = [(delta[:], const[DELTA]), (ident[:], const[IDENT])]
                    for ax, (hi, lo) in enumerate((("p_max", "p_min"), ("q_max", "q_min"))):
                        for m, n in enumerate((hi, lo)):
                            par.append((edges[:, ax, m, :], bc(w[n].rearrange("k n -> (k n)"))))
                    for i, n in enumerate(("bn2_gamma", "bn2_beta", "bn2_mean", "bn2_var")):
                        par.append((bn2[:, i, :], bc(w[n])))
                    for i, n in enumerate(("bn1_gamma", "bn1_var")):
                        par.append((bn1r[:, i, :], bc(w[n])))
                    for i, n in enumerate(("bn1_gamma", "bn1_beta", "bn1_mean", "bn1_var")):
                        for h in range(2):
                            par.append((bn1c[h * K:(h + 1) * K, i:i + 1], w[n].rearrange("(k a) -> k a", a=1)))
                    for h in range(2):
                        par.append((w1t[h * C:(h + 1) * C, :], w["w1"].rearrange("k c -> c k")))
                    with nc.allow_non_contiguous_dma("small parameters"):
                        for o, i in par:
                            sp.dma_start(o, i).then_inc(s_par, 16)
                    assert len(par) == N_PAR
                    for b in range(B):
                        if b >= 2:
                            sp.wait_ge(s_z_mm, CH8 * (b - 1))
                        for h in range(2):
                            sp.dma_start(xc[h * C:(h + 1) * C, b % 2, :].rearrange("c (p q) -> c p q", q=P),
                                         src["half"](b, h)).then_inc(s_x[b % 2], 16)

                @block.vector
                def _(dve):
                    n = [0]
                    V = nc.vector
                    dve.wait_ge(s_par, 16 * N_PAR)
                    V.tensor_scalar(t2[:, 0, :], bn2[:, 3, :], BN2_EPS, None, ALU.add)
                    V.tensor_scalar(inv1[:], bn1r[:, 1, :], BN1_EPS, None, ALU.add)
                    V.tensor_scalar(inv1c[:], bn1c[:, 3:4], BN1_EPS, None, ALU.add)
                    V.memset(w1bd[:], 0.0).then_inc(s_var, 1)
                    dve.wait_ge(s_sqrt, 3)
                    V.reciprocal(t2[:, 0, :], t2[:, 0, :])
                    V.reciprocal(inv1[:], inv1[:])
                    chain(dve, s_step, n, V.reciprocal(inv1c[:], inv1c[:]))
                    V.tensor_tensor(t2[:, 0, :], t2[:, 0, :], bn2[:, 0, :], ALU.mult)
                    V.tensor_tensor(inv1[:], inv1[:], bn1r[:, 0, :], ALU.mult)
                    chain(dve, s_step, n, V.tensor_tensor(inv1c[:], inv1c[:], bn1c[:, 0:1], ALU.mult))
                    for h in range(2):
                        V.tensor_tensor(w1bd[h * C:(h + 1) * C, h * K:(h + 1) * K], w1t[h * C:(h + 1) * C, :],
                                        inv1[h * C:(h + 1) * C, :], ALU.mult).then_inc(s_w1, 1)
                    chain(dve, s_step, n, V.tensor_tensor(bias1[:, 0:1], inv1c[:], bn1c[:, 2:3], ALU.mult))
                    V.tensor_tensor(bias1[:, 1:2], bn1c[:, 1:2], bias1[:, 0:1], ALU.subtract).then_inc(s_w1, 1)
                    V.tensor_tensor(bias2[:], t2[:, 0, :], bn2[:, 2, :], ALU.mult)
                    V.tensor_tensor(t2[:, 1, :], edges[:, 0, 0, :], edges[:, 0, 1, :], ALU.subtract)
                    chain(dve, s_step, n, V.tensor_tensor(t2[:, 2, :], edges[:, 1, 0, :], edges[:, 1, 1, :],
                                                          ALU.subtract))
                    V.tensor_tensor(bias2[:], bn2[:, 1, :], bias2[:], ALU.subtract)
                    chain(dve, s_step, n, V.tensor_tensor(t2[:, 1, :], t2[:, 1, :], t2[:, 2, :], ALU.mult))
                    chain(dve, s_step, n, V.reciprocal(t2[:, 2, :], t2[:, 1, :]))
                    V.tensor_tensor(scale2[:], t2[:, 0, :], t2[:, 2, :], ALU.mult)
                    dve.wait_ge(s_w1, 3)
                    for b in range(B):
                        for j in range(0, CH8, 2):
                            t = b * CH8 + j
                            dve.wait_ge(s_z_mm, t + 1)
                            if b >= 2 and j == 0:
                                dve.wait_ge(s_z_out[b % 2], 32)
                            V.tensor_scalar(zs[:, b % 2, j * BANK:(j + 1) * BANK], banks[t % 4][0:2 * K, :],
                                            bias1[:, 1:2], None, ALU.add).then_inc(s_z_dve, 1)

                @block.scalar
                def _(act):
                    act.wait_ge(s_var, 1)
                    for a in (t2[:, 0, :], inv1[:], inv1c[:]):
                        nc.scalar.activation(a, a, ACT.Sqrt).then_inc(s_sqrt, 1)
                    act.wait_ge(s_w1, 3)
                    for b in range(B):
                        for j in range(1, CH8, 2):
                            t = b * CH8 + j
                            act.wait_ge(s_z_mm, t + 1)
                            if b >= 2 and j == 1:
                                act.wait_ge(s_z_out[b % 2], 32)
                            nc.scalar.activation(zs[:, b % 2, j * BANK:(j + 1) * BANK], banks[t % 4][0:2 * K, :],
                                                 ACT.Identity, bias=bias1[:, 1:2]).then_inc(s_z_act, 1)

                @block.tensor
                def _(pe):
                    pe.wait_ge(s_w1, 3)
                    for b in range(B):
                        pe.wait_ge(s_x[b % 2], 32 * (b // 2 + 1))
                        for j in range(CH8):
                            t = b * CH8 + j
                            if t >= 4:
                                pe.wait_ge((s_z_dve, s_z_act)[j % 2], t // 2 - 1)
                            nc.tensor.matmul(banks[t % 4][0:2 * K, :], w1bd[:], xc[:, b % 2, j * BANK:(j + 1) * BANK],
                                             start=True, stop=True).then_inc(s_z_mm, 1)

                @block.gpsimd
                def _(pool):
                    for b in range(B):
                        pool.wait_ge(s_z_dve, CH8 // 2 * (b + 1))
                        pool.wait_ge(s_z_act, CH8 // 2 * (b + 1))
                        for h in range(2):
                            pool.dma_start(zd[b, :, h * HALF:(h + 1) * HALF, :].rearrange("k p q -> k (p q)"),
                                           zs[h * K:(h + 1) * K, b % 2, :]).then_inc(s_z_out[b % 2], 16)
                    for i in range(2):
                        pool.wait_ge(s_z_out[i], 32 * B // 2)

        STEPS = K_UNROLL * B
        z = sb("z", [P, 2, B, P])
        x = sb("x", [P, 2, B, NB, P])
        raw = sb("raw", [P, 2, 4, NB, P])
        taps = sb("taps", [P, 2, 2, NB, P])
        half1 = sb("half1", [P, 2, NB, P])
        pre = sb("pre", [P, 2, NB, P])
        summed = sb("summed", [P, 2, NB, P])
        o = sb("o", [P, 4, NB, P])
        s_ld = [sem("ld0"), sem("ld1")]
        s_raw, s_taps, s_clip = sem("raw"), sem("taps"), sem("clip")
        s_f1, s_h1, s_f2, s_pre, s_sum, s_relu = (sem(n) for n in ("f1", "h1", "f2", "pre", "sum", "relu"))
        s_out = [sem(f"out{i}") for i in range(4)]
        all_sems = s_ld + [s_raw, s_taps, s_clip, s_f1, s_h1, s_f2, s_pre, s_sum, s_relu] + s_out
        with nc.Fori(0, K // K_UNROLL) as kk:
            with nc.Block() as block:
                @block.sync
                def _(sp):
                    def load(u):
                        k = kk * K_UNROLL + u
                        if u >= 2:
                            sp.wait_ge(s_sum, B * (u - 1))
                        sp.dma_start(z[:, u % 2], zd[:, k].rearrange("b p q -> p b q")).then_inc(s_ld[u % 2], 16)
                        for b in range(B):
                            sp.dma_start(x[:, u % 2, b], src["pcq"](b)[:, bass.ds(k * NB, NB), :]
                                         ).then_inc(s_ld[u % 2], 16)
                    load(0)
                    for s in range(STEPS):
                        u, b = divmod(s, B)
                        if b == 0 and u + 1 < K_UNROLL:
                            load(u + 1)
                        k = kk * K_UNROLL + u
                        sp.wait_ge(s_relu, s + 1)
                        sp.dma_start(dst(b)[:, bass.ds(k * NB, NB), :], o[:, s % 4]).then_inc(s_out[s % 4], 16)
                    for i in range(4):
                        sp.wait_ge(s_out[i], 16 * (STEPS // 4))

                @block.gpsimd
                def _(pool):
                    for u in range(K_UNROLL):
                        k = kk * K_UNROLL + u
                        if u >= 2:
                            pool.wait_ge(s_taps, u - 1)
                        e = edges[:].rearrange("p a m c -> p (a m) c")[:, :, bass.ds(k * NB, NB)]
                        nc.gpsimd.tensor_tensor(raw[:, u % 2], delta[:, None, None, :].broadcast_to([P, 4, NB, P]),
                                                e[:, :, :, None].broadcast_to([P, 4, NB, P]), ALU.add
                                                ).then_inc(s_raw, 1)

                @block.vector
                def _(dve):
                    n = [0]
                    V = nc.vector

                    def make_taps(u):
                        k = kk * K_UNROLL + u
                        dve.wait_ge(s_raw, u + 1)
                        r = raw[:, u % 2].rearrange("p (a m) n i -> p a m (n i)", a=2)
                        chain(dve, s_clip, n, V.tensor_scalar(raw[:, u % 2], raw[:, u % 2], 0.0, 1.0, ALU.max, ALU.min))
                        if u >= 2:
                            dve.wait_ge(s_f2, B * (u - 1))
                        chain(dve, s_clip, n, V.tensor_tensor(taps[:, u % 2].rearrange("p a n i -> p a (n i)"),
                                                              r[:, :, 0], r[:, :, 1], ALU.subtract))
                        V.tensor_tensor(taps[:, u % 2, 1], taps[:, u % 2, 1],
                                        scale2[:, bass.ds(k * NB, NB)][:, :, None].broadcast_to([P, NB, P]),
                                        ALU.mult).then_inc(s_taps, 1)

                    make_taps(0)
                    for s in range(STEPS):
                        u, b = divmod(s, B)
                        k = kk * K_UNROLL + u
                        if b == 0 and u + 1 < K_UNROLL:
                            make_taps(u + 1)
                        dve.wait_ge(s_f2, s + 1)
                        if not turns and b == 0:
                            dve.wait_ge(s_ld[u % 2], 16 * (B + 1) * (u // 2 + 1))
                        V.tensor_tensor(pre[:, s % 2], banks[2 + s % 2].rearrange("p (n i) -> p n i", n=NB),
                                        bias2[:, bass.ds(k * NB, NB)][:, :, None].broadcast_to([P, NB, P]),
                                        ALU.add).then_inc(s_pre, 1)
                        dve.wait_ge(s_pre, s + 1)
                        if s >= 2:
                            dve.wait_ge(s_relu, s - 1)
                        res = (banks[4 + s % 2].rearrange("p (n i) -> p n i", n=NB) if turns
                               else x[:, u % 2, b])
                        V.scalar_tensor_tensor(out=summed[:, s % 2], in0=pre[:, s % 2], scalar=0.0, in1=res,
                                               op0=ALU.max, op1=ALU.add).then_inc(s_sum, 1)

                @block.scalar
                def _(act):
                    def relu(s):
                        act.wait_ge(s_sum, s + 1)
                        if s >= 4:
                            act.wait_ge(s_out[s % 4], 16 * (s // 4))
                        nc.scalar.activation(o[:, s % 4], summed[:, s % 2], ACT.Relu).then_inc(s_relu, 1)

                    for s in range(STEPS):
                        act.wait_ge(s_f1, s + 1)
                        if s >= 2:
                            act.wait_ge(s_f2, s - 1)
                        nc.scalar.activation(half1[:, s % 2], banks[s % 2].rearrange("p (n i) -> p n i", n=NB),
                                             ACT.Copy).then_inc(s_h1, 1)
                        if s >= 1:
                            relu(s - 1)
                    relu(STEPS - 1)

                @block.tensor
                def _(pe):
                    def first(s):
                        u, b = divmod(s, B)
                        if b == 0:
                            pe.wait_ge(s_ld[u % 2], 16 * (B + 1) * (u // 2 + 1))
                            pe.wait_ge(s_taps, u + 1)
                        if s >= 2:
                            pe.wait_ge(s_h1, s - 1)
                        nc.tensor.matmul(banks[s % 2][:], z[:, u % 2, b, :],
                                         taps[:, u % 2, 0].rearrange("p n i -> p (n i)"),
                                         start=True, stop=True).then_inc(s_f1, 1)

                    def second(s):
                        u, b = divmod(s, B)
                        if s >= 2:
                            pe.wait_ge(s_sum, s - 1)
                        if turns:
                            for j in range(NB):
                                nc.tensor.transpose(banks[4 + s % 2][:, j * P:(j + 1) * P], x[:, u % 2, b, j, :],
                                                    ident[:])
                        pe.wait_ge(s_h1, s + 1)
                        for j in range(NB):
                            h, t = half1[:, s % 2, j, :], taps[:, u % 2, 1, j, :]
                            mm = nc.tensor.matmul(banks[2 + s % 2][:, j * P:(j + 1) * P], t if turns else h,
                                                  h if turns else t, start=True, stop=True)
                        mm.then_inc(s_f2, 1)

                    first(0)
                    for s in range(STEPS):
                        if s + 1 < STEPS:
                            first(s + 1)
                        second(s)
            for q in all_sems:
                nc.gpsimd.sem_clear(q)
            nc.all_engine_barrier()



N_PAR = 2 + 4 + 4 + 2 + 8 + 2
N_CHUNK = 17
N_WLOAD = 21
GROUPS = C // 4
HB = 8
BLOCKS = P // HB
QUARTER = 4
QH = HB * QUARTER


def chunk(i):
    return 4 if i < N_CHUNK - 1 else 1


def afno_layers(nc, const, w, src, dst):
    with ExitStack() as ctx:
        def sb(name, shape):
            return ctx.enter_context(nc.sbuf_tensor(f"a_{name}", shape, F32))

        def sem(name):
            s = ctx.enter_context(nc.semaphore(f"a_{name}"))
            sems.append(s)
            return s

        sems = []
        bank = [ctx.enter_context(nc.psum_tensor(f"a_bank{i}", [P, BANK], F32)) for i in range(8)]

        x = sb("x", [P, C, P])
        y = sb("y", [P, C, P])
        m1 = y
        m2 = sb("m2", [P, C, P])
        hidden = m2[:].rearrange("p c h -> p (c h)")[:, 0:8 * BANK].rearrange("p (r i n) -> p r i n", r=2, i=4)
        g = sb("g", [P, KW, 3, C])
        iy = g[:].rearrange("p k r c -> p (k r c)")[:, 0:C * P].rearrange("p (c h) -> p c h", c=C)
        xf = sb("xf", [P, 2, BANK])
        o1 = sb("o1", [P, 2, BANK])
        o2 = sb("o2", [P, 2, 4, 2, C])
        mag = sb("mag", [P, 2, 4, 2, C])
        top = sb("top", [P, 2, 4, C])
        im = sb("im", [P, 2, 4, C])
        sq = sb("sq", [P, C, QH])
        y2 = sb("y2", [P, 2, HB, C])
        yc = sb("yc", [P, 2, BANK])
        stat = sb("stat", [P, 4, P])
        ident, dft_w, cos, sin, idft_w, centre = (sb(n, [P, P]) for n in
                                                  ("ident", "dft_w", "cos", "sin", "idft_w", "centre"))
        mix1, mix1_s, mix1_fold, mix2 = (sb(n, [P, P]) for n in ("mix1", "mix1_s", "mix1_fold", "mix2"))
        mix1_b, mix1_b0 = sb("mix1_b", [P, 1]), sb("mix1_b0", [P, 1])
        mix2_b = sb("mix2_b", [P, 2, C])
        ln1 = sb("ln1", [P, 2])
        ln2 = sb("ln2", [P, 2])
        up, up_s = sb("up", [P, HID]), sb("up_s", [P, HID])
        up_fold = sb("up_fold", [P, 2, HID])
        up_b = sb("up_b", [P, 2 * HC])
        down = sb("down", [P, HC, C])
        down_b = sb("down_b", [P, C])

        s_const, s_w, s_img, s_store = sem("const"), sem("w"), sem("img"), sem("store")
        s_step = sem("step")
        s_sq, s_stat, s_var, s_std, s_y = sem("sq"), sem("stat"), sem("var"), sem("std"), sem("y")
        s_wscaled, s_wfold, s_wready = sem("wscaled"), sem("wfold"), sem("wready")
        s_zero = sem("zero")
        s_fw, s_g_dve, s_g_act = sem("fw"), sem("g_dve"), sem("g_act")
        s_fh, s_xf, s_mix1, s_o1, s_mix2, s_o2 = (sem(n) for n in ("fh", "xf", "mix1", "o1", "mix2", "o2"))
        s_mag, s_top, s_masked, s_m = sem("mag"), sem("top"), sem("masked"), sem("m")
        s_ih, s_iy = sem("ih"), [sem("iy_dve"), sem("iy_act")]
        s_iw, s_x = sem("iw"), sem("x")
        s_sq2, s_stat2, s_var2, s_std2 = sem("sq2"), sem("stat2"), sem("var2"), sem("std2")
        s_y2, s_tr, s_yc, s_up, s_hid, s_down, s_xb, s_res = (
            sem(n) for n in ("y2", "tr", "yc", "up", "hid", "down", "xb", "res"))

        def four(a):
            return a.rearrange("p (a b) -> p a b", a=4)

        with nc.Block() as block:
            @block.sync
            def _(sp):
                for t, i in ((ident, IDENT), (dft_w, DFT_W), (cos, COS), (sin, SIN), (idft_w, IDFT_W), (centre, CENTRE)):
                    sp.dma_start(t[:], const[i]).then_inc(s_const, 16)
                sp.wait_ge(s_const, 16 * 6)

            @block.vector
            def _(dve):
                nc.vector.memset(up_fold[:], 0.0).then_inc(s_zero, 1)
                dve.wait_ge(s_zero, 1)
        for q in (s_const, s_zero):
            nc.gpsimd.sem_clear(q)
        nc.all_engine_barrier()

        with nc.Fori(0, B) as b:
            with nc.Block() as block:
                @block.sync
                def _(sp):
                    sp.dma_start(x[:], src[b]).then_inc(s_img, 16)
                    sp.wait_ge(s_img, 16)
            nc.gpsimd.sem_clear(s_img)
            nc.all_engine_barrier()
            with nc.Fori(0, L) as l:
                with nc.Block() as block:
                    @block.sync
                    def _(sp):
                        with nc.allow_non_contiguous_dma("small weights"):
                            loads = []
                            for t, n in ((mix1, "w1"), (mix2, "w2")):
                                for rows in range(2):
                                    for cols in range(2):
                                        loads.append((t[rows * C:(rows + 1) * C, cols * C:(cols + 1) * C],
                                                      w[n][l, (rows + cols) % 2]))
                            loads.append((mix1_b[:], w["b1"][l].rearrange("r (c a) -> (r c) a", a=1)))
                            loads.append((mix2_b[:].rearrange("p r c -> p (r c)"),
                                          w["b2"][l].rearrange("r c -> (r c)").partition_broadcast(P)))
                            for t, n in ((ln1, "ln1"), (ln2, "ln2")):
                                for i in range(2):
                                    loads.append((t[i * C:(i + 1) * C, 0:1],
                                                  w[n + "_w"][l].rearrange("(c a) -> c a", a=1)))
                                loads.append((t[0:C, 1:2], w[n + "_b"][l].rearrange("(c a) -> c a", a=1)))
                            for i in range(2):
                                loads.append((up[i * C:(i + 1) * C, :], w["mlp_w1"][l]))
                            loads.append((up_b[:, 0:HC], w["mlp_b1"][l].rearrange("(j p) -> p j", p=P)))
                            loads.append((down[:], w["mlp_w2"][l].rearrange("(j p) c -> p j c", p=P)))
                            loads.append((down_b[:], w["mlp_b2"][l].partition_broadcast(P)))
                            assert len(loads) == N_WLOAD
                            for o, i in loads:
                                sp.dma_start(o, i).then_inc(s_w, 16)

                    @block.gpsimd
                    def _(pool):
                        nc.gpsimd.memset(g[:, 0, 1, :], 0.0)
                        nc.gpsimd.memset(g[:, KW - 1, 1, :], 0.0).then_inc(s_zero, 1)
                        pool.wait_ge(s_w, 16 * N_WLOAD)
                        for i in range(BLOCKS):
                            xb = x[:, :, i * HB:(i + 1) * HB]
                            pool.wait_ge(s_y2, i + 1)
                            nc.gpsimd.tensor_tensor(xb, xb, down_b[:, :, None].broadcast_to([P, C, HB]), ALU.add
                                                    ).then_inc(s_xb, 1)

                    @block.vector
                    def _(dve):
                        n = [0]
                        V = nc.vector

                        def stats(q, s_squares, s_read, s_ready):
                            hs = slice(q * QH, (q + 1) * QH)
                            V.tensor_reduce(stat[:, 0, hs], x[:, :, hs].rearrange("p c h -> p h c"), AX.X, ALU.add)
                            dve.wait_ge(s_squares, q + 1)
                            V.tensor_reduce(stat[:, 1, hs], sq[:].rearrange("p c h -> p h c"), AX.X, ALU.add
                                            ).then_inc(s_read, 1)
                            dve.wait_ge(s_read, q + 1)
                            chain(dve, s_step, n, V.scalar_tensor_tensor(
                                out=stat[:, 2, hs], in0=stat[:, 0, hs], scalar=-1.0 / (C * C), in1=stat[:, 0, hs],
                                op0=ALU.mult, op1=ALU.mult))
                            chain(dve, s_step, n, V.scalar_tensor_tensor(
                                out=stat[:, 2, hs], in0=stat[:, 1, hs], scalar=1.0 / C, in1=stat[:, 2, hs],
                                op0=ALU.mult, op1=ALU.add))
                            V.tensor_scalar(stat[:, 2, hs], stat[:, 2, hs], 0.0, LN_EPS, ALU.max, ALU.add
                                            ).then_inc(s_ready, 1)

                        def scale(q, s_root):
                            hs = slice(q * QH, (q + 1) * QH)
                            dve.wait_ge(s_root, q + 1)
                            chain(dve, s_step, n, V.reciprocal(stat[:, 3, hs], stat[:, 2, hs]))

                        for q in range(5):
                            if q < 4:
                                stats(q, s_sq, s_stat, s_var)
                            if q >= 1:
                                hs = slice((q - 1) * QH, q * QH)
                                scale(q - 1, s_std)
                                V.tensor_tensor(y[:, :, hs], x[:, :, hs],
                                                stat[:, 3, None, hs].broadcast_to([P, C, QH]), ALU.mult
                                                ).then_inc(s_y, 1)
                        dve.wait_ge(s_w, 16 * N_WLOAD)
                        V.tensor_scalar(mix2[C:P, 0:C], mix2[C:P, 0:C], -1.0, None, ALU.mult)
                        chain(dve, s_step, n, V.tensor_scalar(mix1[C:P, 0:C], mix1[C:P, 0:C], -1.0, None, ALU.mult))
                        V.tensor_scalar(mix1_s[:], mix1[:], ln1[:, 0:1], None, ALU.mult)
                        V.tensor_scalar(up_s[:], up[:], ln2[:, 0:1], None, ALU.mult).then_inc(s_wscaled, 1)
                        for i in range(GROUPS):
                            dve.wait_ge(s_fw, i + 1)
                            ps, cs = four(bank[i % 2][:]), slice(4 * i, 4 * i + 4)
                            V.tensor_copy(g[:, :, 0, cs], ps[:, :, 0:KW].rearrange("p c k -> p k c"))
                            V.tensor_copy(g[:, 1:KW - 1, 1, cs], ps[:, :, KW:P].rearrange("p c k -> p k c")
                                          ).then_inc(s_g_dve, 1)
                        dve.wait_ge(s_wfold, 1)
                        V.tensor_copy(mix1_fold[:], bank[7][:, 0:P])
                        V.tensor_copy(up_fold[0:C, 0, :], bank[6][0:C, 0:HID])
                        V.tensor_copy(up_fold[C:P, 1, :], bank[6][C:P, 0:HID])
                        V.scalar_tensor_tensor(out=mix1_b0[:], in0=bank[5][:, 0:1], scalar=float(P), in1=mix1_b[:],
                                               op0=ALU.mult, op1=ALU.add)
                        V.tensor_tensor(up_b[:, HC:2 * HC], bank[5][:, 1:1 + HC], up_b[:, 0:HC], ALU.add
                                        ).then_inc(s_wready, 1)
                        for t in range(N_CHUNK + 3):
                            if t < N_CHUNK:
                                k = chunk(t)
                                dve.wait_ge(s_fh, t + 1)
                                if t >= 2:
                                    dve.wait_ge(s_mix1, t - 1)
                                V.tensor_copy(xf[:, t % 2, 0:k * P], bank[2 + t % 2][:, 0:k * P]).then_inc(s_xf, 1)
                            j = t - 2
                            if 0 <= j < N_CHUNK:
                                k = chunk(j)
                                dve.wait_ge(s_mix2, j + 1)
                                if j >= 2:
                                    dve.wait_ge(s_masked, j - 1)
                                    dve.wait_ge(s_mag, j - 1)
                                V.tensor_tensor(o2[:, j % 2, 0:k].rearrange("p k r c -> p k (r c)"),
                                                four(bank[6 + j % 2][:])[:, 0:k],
                                                mix2_b[:].rearrange("p r c -> p (r c)")[:, None, :
                                                ].broadcast_to([P, k, P]), ALU.add).then_inc(s_o2, 1)
                            j = t - 3
                            if 0 <= j < N_CHUNK:
                                k = chunk(j)
                                dve.wait_ge(s_mag, j + 1)
                                V.tensor_tensor(top[:, j % 2, 0:k], mag[:, j % 2, 0:k, 0], mag[:, j % 2, 0:k, 1],
                                                ALU.max).then_inc(s_top, 1)
                                dve.wait_ge(s_top, j + 1)
                                col = 4 * j
                                V.scalar_tensor_tensor(
                                    out=m1[:, :, col:col + k].rearrange("p c k -> p k c"),
                                    in0=top[:, j % 2, 0:k], scalar=THR, in1=o2[:, j % 2, 0:k, 0],
                                    op0=ALU.is_gt, op1=ALU.mult)
                                if j >= 2:
                                    dve.wait_ge(s_m, j - 1)
                                V.scalar_tensor_tensor(
                                    out=im[:, j % 2, 0:k], in0=top[:, j % 2, 0:k], scalar=THR,
                                    in1=o2[:, j % 2, 0:k, 1], op0=ALU.is_gt, op1=ALU.mult).then_inc(s_masked, 1)
                        for i in range(0, GROUPS, 2):
                            dve.wait_ge(s_ih, i + 1)
                            V.tensor_copy(iy[:, 4 * i:4 * i + 4, :], four(bank[0][:])).then_inc(s_iy[0], 1)

                        def first_residual(q):
                            for i in range(q * QUARTER, (q + 1) * QUARTER):
                                xb = x[:, :, i * HB:(i + 1) * HB]
                                dve.wait_ge(s_iw, i + 1)
                                ins = V.tensor_tensor(xb, bank[i % 2].rearrange("p (c h) -> p c h", h=HB), xb,
                                                      ALU.add).then_inc(s_x, 1)
                            dve.wait_ge(s_x, (q + 1) * QUARTER)

                        def normalise(i):
                            hs = slice(i * HB, (i + 1) * HB)
                            if i >= 2:
                                dve.wait_ge(s_tr, i - 1)
                            V.tensor_tensor(y2[:, i % 2].rearrange("p h c -> p c h"), x[:, :, hs],
                                            stat[:, 3, None, hs].broadcast_to([P, C, HB]), ALU.mult
                                            ).then_inc(s_y2, 1)

                        def second_residual(i):
                            xb = x[:, :, i * HB:(i + 1) * HB].rearrange("p c h -> p h c")
                            dve.wait_ge(s_down, i + 1)
                            dve.wait_ge(s_xb, i + 1)
                            V.tensor_tensor(xb, bank[3].rearrange("p (h c) -> p h c", c=C), xb, ALU.add
                                            ).then_inc(s_res, 1)

                        first_residual(0)
                        stats(0, s_sq2, s_stat2, s_var2)
                        for q in range(4):
                            if q + 1 < 4:
                                first_residual(q + 1)
                                stats(q + 1, s_sq2, s_stat2, s_var2)
                            scale(q, s_std2)
                            for i in range(q * QUARTER, (q + 1) * QUARTER):
                                normalise(i)
                                if i >= 1:
                                    second_residual(i - 1)
                        second_residual(BLOCKS - 1)

                    @block.scalar
                    def _(act):
                        A = nc.scalar.activation

                        def root(q, s_ready, s_root):
                            hs = slice(q * QH, (q + 1) * QH)
                            act.wait_ge(s_ready, q + 1)
                            A(stat[:, 2, hs], stat[:, 2, hs], ACT.Sqrt).then_inc(s_root, 1)

                        for q in range(4):
                            if q >= 1:
                                act.wait_ge(s_stat, q)
                            A(sq[:], x[:, :, q * QH:(q + 1) * QH], ACT.Square).then_inc(s_sq, 1)
                            if q >= 1:
                                root(q - 1, s_var, s_std)
                        root(3, s_var, s_std)
                        for i in range(GROUPS):
                            act.wait_ge(s_g_dve, i + 1)
                            A(g[:, :, 2, 4 * i:4 * i + 4], g[:, :, 0, 4 * i:4 * i + 4], ACT.Copy, scale=-1.0
                              ).then_inc(s_g_act, 1)
                        act.wait_ge(s_wready, 1)
                        for t in range(1, N_CHUNK + 3):
                            j = t - 1
                            if j < N_CHUNK:
                                cols = chunk(j) * P
                                act.wait_ge(s_mix1, j + 1)
                                if j >= 2:
                                    act.wait_ge(s_mix2, j - 1)
                                first = 0
                                if j == 0:
                                    A(o1[:, 0, 0:1], bank[4][:, 0:1], ACT.Relu, bias=mix1_b0[:])
                                    first = 1
                                A(o1[:, j % 2, first:cols], bank[4 + j % 2][:, first:cols], ACT.Relu, bias=mix1_b[:]
                                  ).then_inc(s_o1, 1)
                            j = t - 2
                            if 0 <= j < N_CHUNK:
                                k = chunk(j)
                                act.wait_ge(s_o2, j + 1)
                                if j >= 2:
                                    act.wait_ge(s_top, j - 1)
                                A(mag[:, j % 2, 0:k], o2[:, j % 2, 0:k], ACT.Abs).then_inc(s_mag, 1)
                            j = t - 3
                            if 0 <= j < N_CHUNK:
                                k, col = chunk(j), 4 * j
                                act.wait_ge(s_masked, j + 1)
                                ins = A(m2[:, :, col:col + k].rearrange("p c k -> p k c"), im[:, j % 2, 0:k],
                                        ACT.Copy, scale=-1.0)
                                if j < N_CHUNK - 1:
                                    lo = 1 if j == 0 else 0
                                    to = slice(HALF + col + lo, HALF + col + 4)
                                    A(m1[:, :, to].rearrange("p c k -> p k c"), im[:, j % 2, lo:4], ACT.Copy)
                                    ins = A(m2[:, :, to], m1[:, :, col + lo:col + 4], ACT.Copy)
                                ins.then_inc(s_m, 1)
                        for i in range(1, GROUPS, 2):
                            act.wait_ge(s_ih, i + 1)
                            A(iy[:, 4 * i:4 * i + 4, :], four(bank[1][:]), ACT.Copy).then_inc(s_iy[1], 1)

                        def squares(q):
                            act.wait_ge(s_x, (q + 1) * QUARTER)
                            if q >= 1:
                                act.wait_ge(s_stat2, q)
                            A(sq[:], x[:, :, q * QH:(q + 1) * QH], ACT.Square).then_inc(s_sq2, 1)
                            root(q, s_var2, s_std2)

                        squares(0)
                        for q in range(4):
                            if q + 1 < 4:
                                squares(q + 1)
                            for i in range(q * QUARTER, (q + 1) * QUARTER):
                                act.wait_ge(s_tr, i + 1)
                                if i >= 2:
                                    act.wait_ge(s_up, 4 * (i - 1))
                                A(yc[:, i % 2, :], bank[2][:], ACT.Copy).then_inc(s_yc, 1)
                                for j in range(4):
                                    act.wait_ge(s_up, 4 * i + j + 1)
                                    if i >= 2 and j == 0:
                                        act.wait_ge(s_down, i - 1)
                                    A(hidden[:, i % 2, j, :], bank[4 + j][:], ACT.Gelu,
                                      bias=up_b[:, HC + j % HC:HC + j % HC + 1]).then_inc(s_hid, 1)

                    @block.tensor
                    def _(pe):
                        M = nc.tensor.matmul
                        pe.wait_ge(s_y, 4)
                        for i in range(GROUPS):
                            if i >= 2:
                                pe.wait_ge(s_g_dve, i - 1)
                            for c in range(4):
                                mm = M(bank[i % 2][:, c * P:(c + 1) * P], y[:, 4 * i + c, :], dft_w[:], start=True,
                                       stop=True)
                            mm.then_inc(s_fw, 1)
                        pe.wait_ge(s_wscaled, 1)
                        M(bank[7][:, 0:P], centre[:], mix1_s[:], start=True, stop=True)
                        M(bank[6][:, 0:HID], centre[:], up_s[:], start=True, stop=True)
                        M(bank[5][:, 0:1], mix1[0:C, :], ln1[0:C, 1:2], start=True, stop=True)
                        for j in range(HC):
                            mm = M(bank[5][:, 1 + j:2 + j], up[0:C, j * P:(j + 1) * P], ln2[0:C, 1:2], start=True,
                                   stop=True)
                        mm.then_inc(s_wfold, 1)
                        for i in range(N_CHUNK + 2):
                            if i < N_CHUNK:
                                if i == 0:
                                    pe.wait_ge(s_g_dve, GROUPS)
                                    pe.wait_ge(s_g_act, GROUPS)
                                    pe.wait_ge(s_zero, 1)
                                if i >= 2:
                                    pe.wait_ge(s_xf, i - 1)
                                for k in range(chunk(i)):
                                    kw = 4 * i + k
                                    to = bank[2 + i % 2][:, k * P:(k + 1) * P]
                                    M(to, g[:, kw, 0:2, :].rearrange("p r c -> p (r c)"), cos[:], start=True, stop=False)
                                    mm = M(to, g[:, kw, 1:3, :].rearrange("p r c -> p (r c)"), sin[:], start=False,
                                           stop=True)
                                mm.then_inc(s_fh, 1)
                            j = i - 1
                            if 0 <= j < N_CHUNK:
                                if j == 0:
                                    pe.wait_ge(s_wready, 1)
                                pe.wait_ge(s_xf, j + 1)
                                if j >= 2:
                                    pe.wait_ge(s_o1, j - 1)
                                cols = chunk(j) * P
                                M(bank[4 + j % 2][:, 0:cols], mix1_fold[:], xf[:, j % 2, 0:cols], start=True, stop=True
                                  ).then_inc(s_mix1, 1)
                            j = i - 2
                            if 0 <= j < N_CHUNK:
                                pe.wait_ge(s_o1, j + 1)
                                if j >= 2:
                                    pe.wait_ge(s_o2, j - 1)
                                for k in range(chunk(j)):
                                    mm = M(bank[6 + j % 2][:, k * P:(k + 1) * P], o1[:, j % 2, k * P:(k + 1) * P],
                                           mix2[:], start=True, stop=True)
                                mm.then_inc(s_mix2, 1)
                        pe.wait_ge(s_m, N_CHUNK)
                        for i in range(GROUPS):
                            if i >= 2:
                                pe.wait_ge(s_iy[i % 2], i // 2)
                            for c in range(4):
                                to = bank[i % 2][:, c * P:(c + 1) * P]
                                M(to, m1[:, 4 * i + c, :], cos[:], start=True, stop=False)
                                mm = M(to, m2[:, 4 * i + c, :], sin[:], start=False, stop=True)
                            mm.then_inc(s_ih, 1)
                        pe.wait_ge(s_iy[0], GROUPS // 2)
                        pe.wait_ge(s_iy[1], GROUPS // 2)

                        def inverse(q):
                            for i in range(q * QUARTER, (q + 1) * QUARTER):
                                if i >= 2:
                                    pe.wait_ge(s_x, i - 1)
                                M(bank[i % 2][:], idft_w[:], iy[:, :, i * HB:(i + 1) * HB], start=True, stop=True
                                  ).then_inc(s_iw, 1)

                        def mlp_down(i):
                            pe.wait_ge(s_hid, 4 * (i + 1))
                            if i >= 1:
                                pe.wait_ge(s_res, i)
                            for h in range(HB):
                                for j in range(HC):
                                    mm = M(bank[3][:, h * C:(h + 1) * C],
                                           hidden[:, i % 2, h % 2 * HC + j, h // 2 * P:(h // 2 + 1) * P],
                                           down[:, j, :], start=j == 0, stop=j == HC - 1)
                            mm.then_inc(s_down, 1)

                        inverse(0)
                        for q in range(4):
                            if q + 1 < 4:
                                inverse(q + 1)
                            for i in range(q * QUARTER, (q + 1) * QUARTER):
                                pe.wait_ge(s_y2, i + 1)
                                if i >= 1:
                                    pe.wait_ge(s_yc, i)
                                for k in range(HB // 2):
                                    mm = nc.tensor.transpose(bank[2][:, k * P:(k + 1) * P],
                                                             y2[:, i % 2, 2 * k:2 * k + 2, :].rearrange(
                                                                 "p h c -> p (h c)"), ident[:])
                                mm.then_inc(s_tr, 1)
                                pe.wait_ge(s_yc, i + 1)
                                for j in range(4):
                                    if i >= 1:
                                        pe.wait_ge(s_hid, 4 * (i - 1) + j + 1)
                                    M(bank[4 + j][:], up_fold[:, j // HC, j % HC * P:(j % HC + 1) * P], yc[:, i % 2, :],
                                      start=True, stop=True).then_inc(s_up, 1)
                                if i >= 1:
                                    mlp_down(i - 1)
                        mlp_down(BLOCKS - 1)
                for q in sems:
                    nc.gpsimd.sem_clear(q)
                nc.all_engine_barrier()
            with nc.Block() as block:
                @block.sync
                def _(sp):
                    sp.dma_start(dst[b], x[:]).then_inc(s_store, 16)
                    sp.wait_ge(s_store, 16)
            nc.gpsimd.sem_clear(s_store)
            nc.all_engine_barrier()


LAYER_INPUTS = {
    "L0_conv": ["w1", "bn1_gamma", "bn1_beta", "bn1_mean", "bn1_var", "x_min", "x_max", "y_min", "y_max",
                "bn2_gamma", "bn2_beta", "bn2_mean", "bn2_var"],
    "L1_conv": ["ln1_w", "ln1_b", "ln2_w", "ln2_b", "w1", "w2", "b1", "b2", "mlp_w1", "mlp_b1", "mlp_w2", "mlp_b2"],
}
LAYER_INPUTS["L2_conv"] = LAYER_INPUTS["L3_conv"] = LAYER_INPUTS["L0_conv"]


def build(nc, ins, out):
    const = ins["constants"]
    part = {t: {n: ins[f"{t}_{n}"] for n in names} for t, names in LAYER_INPUTS.items()}

    def scratch(name, shape):
        return nc.dram_tensor(name, shape, F32, kind="Internal").ap()

    turned = [scratch(f"turned{i}", [B, P, C, P]) for i in range(3)]
    z = [scratch(f"z{i}", [B, K, P, P]) for i in range(3)]
    x = ins["x"]

    def edges(w, p, q):
        return w | {"p_max": w[p + "_max"], "p_min": w[p + "_min"], "q_max": w[q + "_max"], "q_min": w[q + "_min"]}

    def from_turned(t):
        return {"pcq": lambda b: t[b], "half": lambda b, h: t[b, h * HALF:(h + 1) * HALF].rearrange("w c h -> c w h")}

    box_layer(nc, "L0", const, edges(part["L0_conv"], "x", "y"), True,
              {"pcq": lambda b: x[b].rearrange("c h w -> h c w"), "half": lambda b, h: x[b, :, h * HALF:(h + 1) * HALF]},
              lambda b: turned[0][b], z[0])
    afno_layers(nc, const, part["L1_conv"], turned[0], turned[1])
    box_layer(nc, "L2", const, edges(part["L2_conv"], "y", "x"), False, from_turned(turned[1]),
              lambda b: turned[2][b], z[1])
    box_layer(nc, "L3", const, edges(part["L3_conv"], "y", "x"), True, from_turned(turned[2]),
              lambda b: out[b].rearrange("c h w -> h c w"), z[2])


def kernel(**inputs):
    import concourse.bacc as bacc
    from concourse.bass_utils import run_bass_kernel_spmd

    nc = bacc.Bacc("TRN2", target_bir_lowering=False, num_devices=1)
    names = ["x"] + [f"{t}_{n}" for t, ns in LAYER_INPUTS.items() for n in ns]
    arrays = {n: np.ascontiguousarray(inputs[n]) for n in names}
    arrays["constants"] = constants()
    aps = {n: nc.dram_tensor(f"in_{n}", a.shape, mybir.dt.from_np(a.dtype), kind="ExternalInput").ap()
           for n, a in arrays.items()}
    out = nc.dram_tensor("out", (B, C, P, P), F32, kind="ExternalOutput").ap()
    build(nc, aps, out)
    r = run_bass_kernel_spmd(nc, [{f"in_{n}": a for n, a in arrays.items()}], core_ids=[0])
    return r.results[0]["out"]
```

```python
from contextlib import ExitStack

import numpy as np

import concourse.bass as bass
from concourse import mybir

F32 = mybir.dt.float32
F16 = mybir.dt.float16
I32 = mybir.dt.int32
ALU = mybir.AluOpType
ACT = mybir.ActivationFunctionType
AX = mybir.AxisListType

P = 128
B, C = 4, 64
NB = 4
K = C // NB
HALF = P // 2
L = 4
HID = 256
HC = HID // P
KW = P // 2 + 1
THR = 0.01
BANK = 512

BN1_EPS, BN2_EPS, LN_EPS = 1e-5, 1e-3, 1e-5

DELTA, IDENT, DFT_W, COS, SIN, IDFT_W, CENTRE, N_CONST = range(8)


def constants():
    n = np.arange(P)
    out = np.zeros((N_CONST, P, P))
    out[DELTA] = n[None, :] - n[:, None]
    out[IDENT] = np.eye(P)
    turn = 2 * np.pi * (np.outer(n, n) % P) / P
    out[COS], out[SIN] = np.cos(turn), np.sin(turn)
    out[DFT_W][:, :KW] = np.cos(turn[:, :KW]) / P
    out[DFT_W][:, KW:] = -np.sin(turn[:, 1:KW - 1]) / P
    out[IDFT_W][:HALF] = 2 * np.cos(turn[:HALF]) / P
    out[IDFT_W][0] = 1 / P
    out[IDFT_W][HALF] = np.cos(turn[HALF]) / P
    out[IDFT_W][HALF + 1:] = -2 * np.sin(turn[1:HALF]) / P
    for h in range(2):
        out[CENTRE][h * C:(h + 1) * C, h * C:(h + 1) * C] = np.eye(C) - 1 / C
    return out.astype(np.float32)


def chain(eng, sem, count, ins):
    count[0] += 1
    ins.then_inc(sem, 1)
    eng.wait_ge(sem, count[0])


def box_layer(nc, tag, const, w, turns, src, dst, zd, K_UNROLL=8):
    CH8 = HALF * P // BANK
    with ExitStack() as ctx:
        def sb(name, shape):
            return ctx.enter_context(nc.sbuf_tensor(f"{tag}_{name}", shape, F32))

        def psum(name):
            return ctx.enter_context(nc.psum_tensor(f"{tag}_{name}", [P, BANK], F32))

        def sem(name):
            return ctx.enter_context(nc.semaphore(f"{tag}_{name}"))

        banks = [psum(f"bank{i}") for i in range(8)]
        delta, ident = sb("delta", [P, P]), sb("ident", [P, P])
        edges = sb("edges", [P, 2, 2, C])
        bn2 = sb("bn2", [P, 4, C])
        scale2, bias2, t2 = sb("scale2", [P, C]), sb("bias2", [P, C]), sb("t2", [P, 3, C])
        bn1r = sb("bn1r", [P, 2, K])
        bn1c = sb("bn1c", [2 * K, 4])
        inv1 = sb("inv1", [P, K])
        inv1c, bias1 = sb("inv1c", [2 * K, 1]), sb("bias1", [2 * K, 2])
        w1t = sb("w1t", [P, K])
        w1bd = sb("w1bd", [P, 2 * K])

        s_par, s_step, s_sqrt, s_var, s_w1 = (sem(x) for x in ("par", "step", "sqrt", "var", "w1"))
        s_act0 = sem("act0")
        s_x = [sem("x0"), sem("x1")]
        s_z_mm, s_z_dve, s_z_act = sem("z_mm"), sem("z_dve"), sem("z_act")
        s_z_out = [sem("z_out0"), sem("z_out1")]

        def bc(a):
            return a.partition_broadcast(P)

        with ExitStack() as zctx:
            xc = zctx.enter_context(nc.sbuf_tensor(f"{tag}_xc", [P, 2, HALF * P], F32))
            zs = zctx.enter_context(nc.sbuf_tensor(f"{tag}_zs", [2 * K, 2, HALF * P], F32))
            with nc.Block() as block:
                @block.sync
                def _(sp):
                    par = [(delta[:], const[DELTA]), (ident[:], const[IDENT])]
                    for ax, (hi, lo) in enumerate((("p_max", "p_min"), ("q_max", "q_min"))):
                        for m, n in enumerate((hi, lo)):
                            par.append((edges[:, ax, m, :], bc(w[n].rearrange("k n -> (k n)"))))
                    for i, n in enumerate(("bn2_gamma", "bn2_beta", "bn2_mean", "bn2_var")):
                        par.append((bn2[:, i, :], bc(w[n])))
                    for i, n in enumerate(("bn1_gamma", "bn1_var")):
                        par.append((bn1r[:, i, :], bc(w[n])))
                    for i, n in enumerate(("bn1_gamma", "bn1_beta", "bn1_mean", "bn1_var")):
                        for h in range(2):
                            par.append((bn1c[h * K:(h + 1) * K, i:i + 1], w[n].rearrange("(k a) -> k a", a=1)))
                    for h in range(2):
                        par.append((w1t[h * C:(h + 1) * C, :], w["w1"].rearrange("k c -> c k")))
                    assert len(par) == N_PAR

                    def load(b):
                        if b >= 2:
                            sp.wait_ge(s_z_mm, CH8 * (b - 1))
                        for h in range(2):
                            sp.dma_start(xc[h * C:(h + 1) * C, b % 2, :].rearrange("c (p q) -> c p q", q=P),
                                         src["half"](b, h)).then_inc(s_x[b % 2], 16)

                    with nc.allow_non_contiguous_dma("small parameters"):
                        for i, (o, j) in enumerate(par):
                            sp.dma_start(o, j).then_inc(s_par, 16)
                            if i == 11:
                                load(0)
                    for b in range(1, B):
                        load(b)

                @block.vector
                def _(dve):
                    n = [0]
                    V = nc.vector
                    dve.wait_ge(s_par, 16 * N_PAR)
                    V.tensor_scalar(t2[:, 0, :], bn2[:, 3, :], BN2_EPS, None, ALU.add)
                    V.tensor_scalar(inv1[:], bn1r[:, 1, :], BN1_EPS, None, ALU.add)
                    V.tensor_scalar(inv1c[:], bn1c[:, 3:4], BN1_EPS, None, ALU.add)
                    V.memset(w1bd[:], 0.0).then_inc(s_var, 1)
                    dve.wait_ge(s_sqrt, 3)
                    V.reciprocal(t2[:, 0, :], t2[:, 0, :])
                    V.reciprocal(inv1[:], inv1[:])
                    chain(dve, s_step, n, V.reciprocal(inv1c[:], inv1c[:]))
                    V.tensor_tensor(t2[:, 0, :], t2[:, 0, :], bn2[:, 0, :], ALU.mult)
                    V.tensor_tensor(inv1[:], inv1[:], bn1r[:, 0, :], ALU.mult)
                    chain(dve, s_step, n, V.tensor_tensor(inv1c[:], inv1c[:], bn1c[:, 0:1], ALU.mult))
                    for h in range(2):
                        V.tensor_tensor(w1bd[h * C:(h + 1) * C, h * K:(h + 1) * K], w1t[h * C:(h + 1) * C, :],
                                        inv1[h * C:(h + 1) * C, :], ALU.mult).then_inc(s_w1, 1)
                    chain(dve, s_step, n, V.tensor_tensor(bias1[:, 0:1], inv1c[:], bn1c[:, 2:3], ALU.mult))
                    V.tensor_tensor(bias1[:, 1:2], bn1c[:, 1:2], bias1[:, 0:1], ALU.subtract).then_inc(s_w1, 1)
                    V.tensor_tensor(bias2[:], t2[:, 0, :], bn2[:, 2, :], ALU.mult)
                    V.tensor_tensor(t2[:, 1, :], edges[:, 0, 0, :], edges[:, 0, 1, :], ALU.subtract)
                    chain(dve, s_step, n, V.tensor_tensor(t2[:, 2, :], edges[:, 1, 0, :], edges[:, 1, 1, :],
                                                          ALU.subtract))
                    V.tensor_tensor(bias2[:], bn2[:, 1, :], bias2[:], ALU.subtract)
                    chain(dve, s_step, n, V.tensor_tensor(t2[:, 1, :], t2[:, 1, :], t2[:, 2, :], ALU.mult))
                    chain(dve, s_step, n, V.reciprocal(t2[:, 2, :], t2[:, 1, :]))
                    V.tensor_tensor(scale2[:], t2[:, 0, :], t2[:, 2, :], ALU.mult)
                    dve.wait_ge(s_w1, 3)
                    for b in range(B):
                        for j in range(0, CH8, 2):
                            t = b * CH8 + j
                            dve.wait_ge(s_z_mm, t + 1)
                            if b >= 2 and j == 0:
                                dve.wait_ge(s_z_out[b % 2], 32)
                            V.tensor_scalar(zs[:, b % 2, j * BANK:(j + 1) * BANK], banks[t % 4][0:2 * K, :],
                                            bias1[:, 1:2], None, ALU.add).then_inc(s_z_dve, 1)

                @block.scalar
                def _(act):
                    act.wait_ge(s_var, 1)
                    for a in (t2[:, 0, :], inv1[:], inv1c[:]):
                        nc.scalar.activation(a, a, ACT.Sqrt).then_inc(s_sqrt, 1)
                    act.wait_ge(s_w1, 3)
                    for b in range(B):
                        for j in range(1, CH8, 2):
                            t = b * CH8 + j
                            act.wait_ge(s_z_mm, t + 1)
                            if b >= 2 and j == 1:
                                act.wait_ge(s_z_out[b % 2], 32)
                            nc.scalar.activation(zs[:, b % 2, j * BANK:(j + 1) * BANK], banks[t % 4][0:2 * K, :],
                                                 ACT.Identity, bias=bias1[:, 1:2]).then_inc(s_z_act, 1)

                @block.tensor
                def _(pe):
                    pe.wait_ge(s_w1, 3)
                    for b in range(B):
                        pe.wait_ge(s_x[b % 2], 32 * (b // 2 + 1))
                        for j in range(CH8):
                            t = b * CH8 + j
                            if t >= 4:
                                pe.wait_ge((s_z_dve, s_z_act)[j % 2], t // 2 - 1)
                            nc.tensor.matmul(banks[t % 4][0:2 * K, :], w1bd[:], xc[:, b % 2, j * BANK:(j + 1) * BANK],
                                             start=True, stop=True).then_inc(s_z_mm, 1)

                @block.gpsimd
                def _(pool):
                    for b in range(B):
                        pool.wait_ge(s_z_dve, CH8 // 2 * (b + 1))
                        pool.wait_ge(s_z_act, CH8 // 2 * (b + 1))
                        for h in range(2):
                            pool.dma_start(zd[b, :, h * HALF:(h + 1) * HALF, :].rearrange("k p q -> k (p q)"),
                                           zs[h * K:(h + 1) * K, b % 2, :]).then_inc(s_z_out[b % 2], 16)
                    for i in range(2):
                        pool.wait_ge(s_z_out[i], 32 * B // 2)

        STEPS = K_UNROLL * B
        z = sb("z", [P, 2, B, P])
        x = sb("x", [P, 2, B, NB, P])
        raw = sb("raw", [P, 2, 4, NB, P])
        taps = sb("taps", [P, 2, 2, NB, P])
        half1 = sb("half1", [P, 2, NB, P])
        pre = sb("pre", [P, 2, NB, P])
        summed = sb("summed", [P, 2, NB, P])
        o = sb("o", [P, 4, NB, P])
        s_ld = [sem("ld0"), sem("ld1")]
        s_raw, s_taps, s_clip = sem("raw"), sem("taps"), sem("clip")
        s_f1, s_h1, s_f2, s_pre, s_sum, s_relu = (sem(n) for n in ("f1", "h1", "f2", "pre", "sum", "relu"))
        s_out = [sem(f"out{i}") for i in range(4)]
        all_sems = s_ld + [s_raw, s_taps, s_clip, s_f1, s_h1, s_f2, s_pre, s_sum, s_relu] + s_out
        with nc.Fori(0, K // K_UNROLL) as kk:
            with nc.Block() as block:
                @block.sync
                def _(sp):
                    def load(u):
                        k = kk * K_UNROLL + u
                        if u >= 2:
                            sp.wait_ge(s_sum, B * (u - 1))
                        sp.dma_start(z[:, u % 2], zd[:, k].rearrange("b p q -> p b q")).then_inc(s_ld[u % 2], 16)
                        for b in range(B):
                            sp.dma_start(x[:, u % 2, b], src["pcq"](b)[:, bass.ds(k * NB, NB), :]
                                         ).then_inc(s_ld[u % 2], 16)
                    load(0)
                    for s in range(STEPS):
                        u, b = divmod(s, B)
                        if b == 0 and u + 1 < K_UNROLL:
                            load(u + 1)
                        k = kk * K_UNROLL + u
                        sp.wait_ge(s_relu, s + 1)
                        sp.dma_start(dst(b)[:, bass.ds(k * NB, NB), :], o[:, s % 4]).then_inc(s_out[s % 4], 16)
                    for i in range(4):
                        sp.wait_ge(s_out[i], 16 * (STEPS // 4))

                @block.gpsimd
                def _(pool):
                    for u in range(K_UNROLL):
                        k = kk * K_UNROLL + u
                        if u >= 2:
                            pool.wait_ge(s_taps, u - 1)
                        e = edges[:].rearrange("p a m c -> p (a m) c")[:, :, bass.ds(k * NB, NB)]
                        nc.gpsimd.tensor_tensor(raw[:, u % 2], delta[:, None, None, :].broadcast_to([P, 4, NB, P]),
                                                e[:, :, :, None].broadcast_to([P, 4, NB, P]), ALU.add
                                                ).then_inc(s_raw, 1)

                @block.vector
                def _(dve):
                    n = [0]
                    V = nc.vector

                    def make_taps(u):
                        k = kk * K_UNROLL + u
                        dve.wait_ge(s_raw, u + 1)
                        r = raw[:, u % 2].rearrange("p (a m) n i -> p a m (n i)", a=2)
                        chain(dve, s_clip, n, V.tensor_scalar(raw[:, u % 2], raw[:, u % 2], 0.0, 1.0, ALU.max, ALU.min))
                        if u >= 2:
                            dve.wait_ge(s_f2, B * (u - 1))
                        chain(dve, s_clip, n, V.tensor_tensor(taps[:, u % 2].rearrange("p a n i -> p a (n i)"),
                                                              r[:, :, 0], r[:, :, 1], ALU.subtract))
                        V.tensor_tensor(taps[:, u % 2, 1], taps[:, u % 2, 1],
                                        scale2[:, bass.ds(k * NB, NB)][:, :, None].broadcast_to([P, NB, P]),
                                        ALU.mult).then_inc(s_taps, 1)

                    make_taps(0)
                    for s in range(STEPS):
                        u, b = divmod(s, B)
                        k = kk * K_UNROLL + u
                        if b == 0 and u + 1 < K_UNROLL:
                            make_taps(u + 1)
                        dve.wait_ge(s_f2, s + 1)
                        if not turns and b == 0:
                            dve.wait_ge(s_ld[u % 2], 16 * (B + 1) * (u // 2 + 1))
                        V.tensor_tensor(pre[:, s % 2], banks[2 + s % 2].rearrange("p (n i) -> p n i", n=NB),
                                        bias2[:, bass.ds(k * NB, NB)][:, :, None].broadcast_to([P, NB, P]),
                                        ALU.add).then_inc(s_pre, 1)
                        dve.wait_ge(s_pre, s + 1)
                        if s >= 2:
                            dve.wait_ge(s_relu, s - 1)
                        res = (banks[4 + s % 2].rearrange("p (n i) -> p n i", n=NB) if turns
                               else x[:, u % 2, b])
                        V.scalar_tensor_tensor(out=summed[:, s % 2], in0=pre[:, s % 2], scalar=0.0, in1=res,
                                               op0=ALU.max, op1=ALU.add).then_inc(s_sum, 1)

                @block.scalar
                def _(act):
                    def relu(s):
                        act.wait_ge(s_sum, s + 1)
                        if s >= 4:
                            act.wait_ge(s_out[s % 4], 16 * (s // 4))
                        nc.scalar.activation(o[:, s % 4], summed[:, s % 2], ACT.Relu).then_inc(s_relu, 1)

                    for s in range(STEPS):
                        act.wait_ge(s_f1, s + 1)
                        if s >= 2:
                            act.wait_ge(s_f2, s - 1)
                        nc.scalar.activation(half1[:, s % 2], banks[s % 2].rearrange("p (n i) -> p n i", n=NB),
                                             ACT.Copy).then_inc(s_h1, 1)
                        if s >= 1:
                            relu(s - 1)
                    relu(STEPS - 1)

                @block.tensor
                def _(pe):
                    def first(s):
                        u, b = divmod(s, B)
                        if b == 0:
                            pe.wait_ge(s_ld[u % 2], 16 * (B + 1) * (u // 2 + 1))
                            pe.wait_ge(s_taps, u + 1)
                        if s >= 2:
                            pe.wait_ge(s_h1, s - 1)
                        nc.tensor.matmul(banks[s % 2][:], z[:, u % 2, b, :],
                                         taps[:, u % 2, 0].rearrange("p n i -> p (n i)"),
                                         start=True, stop=True).then_inc(s_f1, 1)

                    def second(s):
                        u, b = divmod(s, B)
                        if s >= 2:
                            pe.wait_ge(s_sum, s - 1)
                        if turns:
                            for j in range(NB):
                                nc.tensor.transpose(banks[4 + s % 2][:, j * P:(j + 1) * P], x[:, u % 2, b, j, :],
                                                    ident[:])
                        pe.wait_ge(s_h1, s + 1)
                        for j in range(NB):
                            h, t = half1[:, s % 2, j, :], taps[:, u % 2, 1, j, :]
                            mm = nc.tensor.matmul(banks[2 + s % 2][:, j * P:(j + 1) * P], t if turns else h,
                                                  h if turns else t, start=True, stop=True)
                        mm.then_inc(s_f2, 1)

                    first(0)
                    for s in range(STEPS):
                        if s + 1 < STEPS:
                            first(s + 1)
                        second(s)
            for q in all_sems:
                nc.gpsimd.sem_clear(q)
            nc.all_engine_barrier()



PAIRS = 10
N_PAR = 2 + 4 + 4 + 2 + 8 + 2
N_CHUNK = 17
N_WLOAD = 22
GROUPS = C // 4
HB = 8
BLOCKS = P // HB
STRIP = 2
SH = HB * STRIP
STRIPS = BLOCKS // STRIP
LOADS = 4
AHEAD = 3 * STRIP
W_SCALE = 64.0
ROOT_STEPS = 14
RSQRT_GUESS = 0x5F3759DF


def chunk(i):
    return 4 if i < N_CHUNK - 1 else 1


def inverse_bank(i):
    return i % 2 if i < AHEAD else 0


def inverse_before(i):
    return i - 2 if i <= AHEAD else i - 1


def root_step(nc, dve, step, n, view, j):
    V = nc.vector
    total, total_sq, v, r, mean = (view(q) for q in range(5))
    if j:
        dve.wait_ge(step, n[0])
    if j == 0:
        V.tensor_scalar(mean, total, 1.0 / C, None, ALU.mult)
        ins = V.scalar_tensor_tensor(out=v, in0=total, scalar=-1.0 / (C * C), in1=total, op0=ALU.mult, op1=ALU.mult)
    elif j == 1:
        ins = V.scalar_tensor_tensor(out=v, in0=total_sq, scalar=1.0 / C, in1=v, op0=ALU.mult, op1=ALU.add)
    elif j == 2:
        ins = V.tensor_scalar(v, v, 0.0, LN_EPS, ALU.max, ALU.add)
    elif j == 3:
        ins = V.tensor_scalar(r.bitcast(I32), v.bitcast(I32), 1, None, ALU.logical_shift_right)
    elif j == 4:
        ins = V.tensor_scalar(r.bitcast(I32), r.bitcast(I32), -1.0, float(RSQRT_GUESS), ALU.mult, ALU.add)
    elif j % 3 == 2:
        ins = V.tensor_tensor(total, r, r, ALU.mult)
    elif j % 3 == 0:
        ins = V.scalar_tensor_tensor(out=total, in0=total, scalar=-0.5, in1=v, op0=ALU.mult, op1=ALU.mult)
    else:
        ins = V.scalar_tensor_tensor(out=r, in0=total, scalar=1.5, in1=r, op0=ALU.add, op1=ALU.mult)
    n[0] += 1
    return ins.then_inc(step, 1)


def inverse_std(nc, dve, step, n, view):
    for j in range(ROOT_STEPS):
        root_step(nc, dve, step, n, view, j)
    dve.wait_ge(step, n[0])


def root_count(kind, t):
    return (min(t + 1, 2) if t < 3 else t) if kind == 1 else t + 4


def square_count(kind, t):
    if kind == 2:
        return t + 2
    return {0: 1, 1: 1, 2: 2}.get(t, t)


def afno_layers(nc, const, w, src, dst):
    with ExitStack() as ctx:
        def sb(name, shape, dtype=F32):
            return ctx.enter_context(nc.sbuf_tensor(f"a_{name}", shape, dtype))

        def sem(name):
            s = ctx.enter_context(nc.semaphore(f"a_{name}"))
            sems.append(s)
            return s

        sems = []
        bank = [ctx.enter_context(nc.psum_tensor(f"a_bank{i}", [P, BANK], F32)) for i in range(8)]

        x = sb("x", [P, C, P])
        y = sb("y", [P, C, P])
        m1 = y
        m2 = sb("m2", [P, C, P])
        m2_flat = m2[:].rearrange("p c h -> p (c h)")
        hidden = m2_flat[:, 0:8 * BANK].rearrange("p (r i n) -> p r i n", r=2, i=4)
        delta = m2_flat[:, 8 * BANK:10 * BANK].rearrange("p (r n) -> p r n", r=2)
        sq = m2_flat[:, 10 * BANK:10 * BANK + 2 * C * SH].rearrange("p (k c h) -> p k c h", k=2, c=C)
        g = sb("g", [P, KW, 3, C])
        iy = g[:].rearrange("p k r c -> p (k r c)")[:, 0:C * P].rearrange("p (c h) -> p c h", c=C)
        xf = sb("xf", [P, 2, BANK])
        o1 = sb("o1", [P, 2, BANK])
        o2 = sb("o2", [P, 2, 4, 2, C])
        mag = sb("mag", [P, 2, 4, 2, C])
        top = sb("top", [P, 2, 4, C])
        im = sb("im", [P, 2, 4, C])
        xc = sb("xc", [P, 2, C, HB])
        y2 = sb("y2", [P, 2, HB, C])
        y2s = sb("y2s", [P, 2, HB, 2, C], F16)
        yc = sb("yc", [P, 2, HB * P], F16)
        sums = sb("sums", [P, 2, P, LOADS])
        whole = sb("whole", [P, 5, P])
        stat = sb("stat", [P, 5, 3, 2, SH])
        ident, dft_w, cos, sin, idft_w, centre = (sb(n, [P, P]) for n in
                                                  ("ident", "dft_w", "cos", "sin", "idft_w", "centre"))
        mix1, mix1_s, mix1_fold, mix2 = (sb(n, [P, P]) for n in ("mix1", "mix1_s", "mix1_fold", "mix2"))
        mix1_b, mix1_b0 = sb("mix1_b", [P, 1]), sb("mix1_b0", [P, 1])
        mix2_b = sb("mix2_b", [P, 2, C])
        ln1 = sb("ln1", [P, 2])
        ln2 = sb("ln2", [P, 2])
        up, up_s = sb("up", [P, HID]), sb("up_s", [P, HID])
        up_w = sb("up_w", [P, 2, HID], F16)
        ident16 = sb("ident16", [P, P], F16)
        up_b = sb("up_b", [P, 2 * HC])
        down = sb("down", [P, 2, HC, P])
        down_b = sb("down_b", [P, C])

        s_const, s_w, s_store, s_sums = sem("const"), sem("w"), sem("store"), sem("sums")
        s_part = [sem(f"part{i}") for i in range(LOADS)]
        s_step = sem("step")
        s_sq, s_sq_read, s_y = [sem("sq0"), sem("sq1")], [sem("sq_read0"), sem("sq_read1")], sem("y")
        s_wscaled, s_wfold, s_wready = sem("wscaled"), sem("wfold"), sem("wready")
        s_zero = sem("zero")
        s_fw, s_g_dve, s_g_act = sem("fw"), sem("g_dve"), sem("g_act")
        s_fh, s_xf, s_mix1, s_o1, s_mix2, s_o2 = (sem(n) for n in ("fh", "xf", "mix1", "o1", "mix2", "o2"))
        s_mag, s_top, s_masked, s_m = sem("mag"), sem("top"), sem("masked"), sem("m")
        s_ih, s_iy = sem("ih"), [sem("iy_dve"), sem("iy_act")]
        s_iw, s_x = sem("iw"), sem("x")
        s_root, s_xc, s_high, s_low = sem("root"), sem("xc"), sem("high"), sem("low")
        s_y2, s_tr, s_yc, s_up, s_hid, s_down, s_delta, s_back, s_xb, s_res = (
            sem(n) for n in ("y2", "tr", "yc", "up", "hid", "down", "delta", "back", "xb", "res"))

        def four(a):
            return a.rearrange("p (a b) -> p a b", a=4)

        with nc.Block() as block:
            @block.sync
            def _(sp):
                for t, i in ((ident, IDENT), (dft_w, DFT_W), (cos, COS), (sin, SIN), (idft_w, IDFT_W), (centre, CENTRE)):
                    sp.dma_start(t[:], const[i]).then_inc(s_const, 16)
                sp.wait_ge(s_const, 16 * 6)

            @block.vector
            def _(dve):
                dve.wait_ge(s_const, 16 * 6)
                nc.vector.tensor_copy(ident16[:], ident[:])
                nc.vector.memset(down[:], 0.0).then_inc(s_zero, 1)
                dve.wait_ge(s_zero, 1)
        for q in (s_const, s_zero):
            nc.gpsimd.sem_clear(q)
        nc.all_engine_barrier()

        with nc.Fori(0, B) as b:
            with nc.Block() as block:
                parts = [slice(i * C // LOADS, (i + 1) * C // LOADS) for i in range(LOADS)]

                @block.sync
                def _(sp):
                    for i, cs in enumerate(parts):
                        sp.dma_start(x[:, cs, :], src[b][:, cs, :]).then_inc(s_part[i], 16)

                @block.scalar
                def _(act):
                    for i, cs in enumerate(parts):
                        act.wait_ge(s_part[i], 16)
                        nc.scalar.activation(y[:, cs, :], x[:, cs, :], ACT.Square).then_inc(s_sq[0], 1)

                @block.vector
                def _(dve):
                    n = [0]
                    V = nc.vector
                    for i, cs in enumerate(parts):
                        dve.wait_ge(s_part[i], 16)
                        V.tensor_reduce(sums[:, 0, :, i], x[:, cs, :].rearrange("p c h -> p h c"), AX.X, ALU.add)
                        dve.wait_ge(s_sq[0], i + 1)
                        V.tensor_reduce(sums[:, 1, :, i], y[:, cs, :].rearrange("p c h -> p h c"), AX.X, ALU.add
                                        ).then_inc(s_sums, 1)
                    dve.wait_ge(s_sums, LOADS)
                    chain(dve, s_step, n, V.tensor_reduce(whole[:, 0:2, :], sums[:], AX.X, ALU.add))
                    inverse_std(nc, dve, s_step, n, lambda q: whole[:, q, :])
                    V.tensor_tensor(y[:], x[:], whole[:, 3, None, :].broadcast_to([P, C, P]), ALU.mult)
            for q in (*s_part, s_sq[0], s_sums, s_step):
                nc.gpsimd.sem_clear(q)
            nc.all_engine_barrier()
            with nc.Fori(0, L) as l:
                with nc.Block() as block:
                    @block.sync
                    def _(sp):
                        with nc.allow_non_contiguous_dma("small weights"):
                            loads = []
                            for t, n in ((mix1, "w1"), (mix2, "w2")):
                                for rows in range(2):
                                    for cols in range(2):
                                        loads.append((t[rows * C:(rows + 1) * C, cols * C:(cols + 1) * C],
                                                      w[n][l, (rows + cols) % 2]))
                            loads.append((mix1_b[:], w["b1"][l].rearrange("r (c a) -> (r c) a", a=1)))
                            loads.append((mix2_b[:].rearrange("p r c -> p (r c)"),
                                          w["b2"][l].rearrange("r c -> (r c)").partition_broadcast(P)))
                            for t, n in ((ln1, "ln1"), (ln2, "ln2")):
                                for i in range(2):
                                    loads.append((t[i * C:(i + 1) * C, 0:1],
                                                  w[n + "_w"][l].rearrange("(c a) -> c a", a=1)))
                                loads.append((t[0:C, 1:2], w[n + "_b"][l].rearrange("(c a) -> c a", a=1)))
                            for i in range(2):
                                loads.append((up[i * C:(i + 1) * C, :], w["mlp_w1"][l]))
                            loads.append((up_b[:, 0:HC], w["mlp_b1"][l].rearrange("(j p) -> p j", p=P)))
                            for i in range(2):
                                loads.append((down[:, i, :, i * C:(i + 1) * C],
                                              w["mlp_w2"][l].rearrange("(j p) c -> p j c", p=P)))
                            loads.append((down_b[:], w["mlp_b2"][l].partition_broadcast(P)))
                            assert len(loads) == N_WLOAD
                            for o, i in loads:
                                sp.dma_start(o, i).then_inc(s_w, 16)

                    @block.gpsimd
                    def _(pool):
                        nc.gpsimd.memset(g[:, 0, 1, :], 0.0)
                        nc.gpsimd.memset(g[:, KW - 1, 1, :], 0.0).then_inc(s_zero, 1)
                        pool.wait_ge(s_w, 16 * N_WLOAD)
                        def centre_block(i):
                            hs, t = slice(i * HB, (i + 1) * HB), i // STRIP
                            pool.wait_ge(s_root, root_count(1, t))
                            if i >= 2:
                                pool.wait_ge(s_y2, i - 1)
                            mean = stat[:, 4, t % 3, 0, i % STRIP * HB:(i % STRIP + 1) * HB]
                            nc.gpsimd.tensor_tensor(xc[:, i % 2], x[:, :, hs], mean[:, None, :].broadcast_to([P, C, HB]),
                                                    ALU.subtract).then_inc(s_xc, 1)
                            pool.wait_ge(s_xc, i + 1)
                            nc.gpsimd.tensor_tensor(x[:, :, hs], x[:, :, hs],
                                                    down_b[:, :, None].broadcast_to([P, C, HB]), ALU.add
                                                    ).then_inc(s_xb, 1)

                        def next_y(t):
                            hs = slice(t * SH, (t + 1) * SH)
                            pool.wait_ge(s_root, root_count(2, t))
                            nc.gpsimd.tensor_tensor(y[:, :, hs], x[:, :, hs],
                                                    stat[:, 3, (t + 1) % 3, 1, :][:, None, :].broadcast_to([P, C, SH]),
                                                    ALU.mult).then_inc(s_y, 1)

                        for i in range(3):
                            centre_block(i)
                        for p in range(PAIRS):
                            for i in (2 * p + 3, 2 * p + 4):
                                if i < BLOCKS:
                                    centre_block(i)
                            if 3 <= p < STRIPS + 2:
                                next_y(p - 3)

                    @block.vector
                    def _(dve):
                        n = [0]
                        V = nc.vector

                        for i in range(GROUPS):
                            if i == GROUPS - 2:
                                dve.wait_ge(s_w, 16 * N_WLOAD)
                                V.tensor_scalar(mix2[C:P, 0:C], mix2[C:P, 0:C], -1.0, None, ALU.mult)
                                chain(dve, s_step, n, V.tensor_scalar(mix1[C:P, 0:C], mix1[C:P, 0:C], -1.0, None, ALU.mult))
                                V.tensor_scalar(mix1_s[:], mix1[:], ln1[:, 0:1], None, ALU.mult)
                                chain(dve, s_step, n, V.tensor_scalar(up_s[:], up[:], ln2[:, 0:1], W_SCALE, ALU.mult,
                                                                      ALU.mult))
                                chain(dve, s_step, n, V.tensor_copy(up_w[:, 0, :], up_s[:]))
                                V.tensor_tensor(up_w[:, 1, :], up_s[:], up_w[:, 0, :], ALU.subtract
                                                ).then_inc(s_wscaled, 1)
                            dve.wait_ge(s_fw, i + 1)
                            ps, cs = four(bank[i % 2][:]), slice(4 * i, 4 * i + 4)
                            V.tensor_copy(g[:, :, 0, cs], ps[:, :, 0:KW].rearrange("p c k -> p k c"))
                            V.tensor_copy(g[:, 1:KW - 1, 1, cs], ps[:, :, KW:P].rearrange("p c k -> p k c")
                                          ).then_inc(s_g_dve, 1)
                        dve.wait_ge(s_wfold, 1)
                        V.tensor_copy(mix1_fold[:], bank[7][:, 0:P])
                        V.scalar_tensor_tensor(out=mix1_b0[:], in0=bank[5][:, 0:1], scalar=float(P), in1=mix1_b[:],
                                               op0=ALU.mult, op1=ALU.add)
                        V.tensor_tensor(up_b[:, HC:2 * HC], bank[5][:, 1:1 + HC], up_b[:, 0:HC], ALU.add
                                        ).then_inc(s_wready, 1)
                        for t in range(N_CHUNK + 3):
                            if t < N_CHUNK:
                                k = chunk(t)
                                dve.wait_ge(s_fh, t + 1)
                                if t >= 2:
                                    dve.wait_ge(s_mix1, t - 1)
                                V.tensor_copy(xf[:, t % 2, 0:k * P], bank[2 + t % 2][:, 0:k * P]).then_inc(s_xf, 1)
                            j = t - 2
                            if 0 <= j < N_CHUNK:
                                k = chunk(j)
                                dve.wait_ge(s_mix2, j + 1)
                                if j >= 2:
                                    dve.wait_ge(s_masked, j - 1)
                                    dve.wait_ge(s_mag, j - 1)
                                V.tensor_tensor(o2[:, j % 2, 0:k].rearrange("p k r c -> p k (r c)"),
                                                four(bank[6 + j % 2][:])[:, 0:k],
                                                mix2_b[:].rearrange("p r c -> p (r c)")[:, None, :
                                                ].broadcast_to([P, k, P]), ALU.add).then_inc(s_o2, 1)
                            j = t - 3
                            if 0 <= j < N_CHUNK:
                                k = chunk(j)
                                dve.wait_ge(s_mag, j + 1)
                                V.tensor_tensor(top[:, j % 2, 0:k], mag[:, j % 2, 0:k, 0], mag[:, j % 2, 0:k, 1],
                                                ALU.max).then_inc(s_top, 1)
                                dve.wait_ge(s_top, j + 1)
                                col = 4 * j
                                V.scalar_tensor_tensor(
                                    out=m1[:, :, col:col + k].rearrange("p c k -> p k c"),
                                    in0=top[:, j % 2, 0:k], scalar=THR, in1=o2[:, j % 2, 0:k, 0],
                                    op0=ALU.is_gt, op1=ALU.mult)
                                if j >= 2:
                                    dve.wait_ge(s_m, j - 1)
                                V.scalar_tensor_tensor(
                                    out=im[:, j % 2, 0:k], in0=top[:, j % 2, 0:k], scalar=THR,
                                    in1=o2[:, j % 2, 0:k, 1], op0=ALU.is_gt, op1=ALU.mult).then_inc(s_masked, 1)
                        for i in range(0, GROUPS, 2):
                            dve.wait_ge(s_ih, i + 1)
                            V.tensor_copy(iy[:, 4 * i:4 * i + 4, :], four(bank[0][:])).then_inc(s_iy[0], 1)

                        def first_residual(i):
                            xb = x[:, :, i * HB:(i + 1) * HB]
                            dve.wait_ge(s_iw, i + 1)
                            V.tensor_tensor(xb, bank[inverse_bank(i)].rearrange("p (c h) -> p c h", h=HB), xb,
                                            ALU.add).then_inc(s_x, 1)

                        def normalise(i):
                            t = i // STRIP
                            dve.wait_ge(s_xc, i + 1)
                            if i >= 2:
                                dve.wait_ge(s_high, i - 1)
                                dve.wait_ge(s_low, i - 1)
                            r = stat[:, 3, t % 3, 0, i % STRIP * HB:(i % STRIP + 1) * HB]
                            V.tensor_tensor(y2[:, i % 2].rearrange("p h c -> p c h"), xc[:, i % 2],
                                            r[:, None, :].broadcast_to([P, C, HB]), ALU.mult).then_inc(s_y2, 1)

                        def low_part(i):
                            dve.wait_ge(s_high, i + 1)
                            V.tensor_tensor(y2s[:, i % 2, :, 1, :], y2[:, i % 2], y2s[:, i % 2, :, 0, :],
                                            ALU.subtract).then_inc(s_low, 1)

                        def second_residual(i):
                            xb = x[:, :, i * HB:(i + 1) * HB].rearrange("p c (q k) -> p k q c", q=2)
                            dve.wait_ge(s_back, i + 1)
                            dve.wait_ge(s_xb, i + 1)
                            V.tensor_tensor(xb, bank[1].rearrange("p (k q c) -> p k q c", q=2, c=C), xb, ALU.add
                                            ).then_inc(s_res, 1)

                        def sum_up(kind, t, slot):
                            dve.wait_ge((s_x, s_res)[kind - 1], (t + 1) * STRIP)
                            if kind == 2 and t >= 3:
                                dve.wait_ge(s_y, t - 2)
                            V.tensor_reduce(stat[:, 0, slot, kind - 1], x[:, :, t * SH:(t + 1) * SH].rearrange(
                                "p c h -> p h c"), AX.X, ALU.add)

                        def sum_squares(kind, t, slot, buffer):
                            dve.wait_ge(s_sq[buffer], square_count(kind, t))
                            V.tensor_reduce(stat[:, 1, slot, kind - 1], sq[:, buffer].rearrange("p c h -> p h c"), AX.X,
                                            ALU.add).then_inc(s_sq_read[buffer], 1)
                            dve.wait_ge(s_sq_read[buffer], square_count(kind, t))

                        first_residual(0)
                        first_residual(1)
                        sum_up(1, 0, 0)
                        sum_squares(1, 0, 0, 0)
                        inverse_std(nc, dve, s_step, n, lambda q: stat[:, q, 0, 0, :])
                        dve.sem_inc(s_root, 1)
                        for i in range(STRIP, AHEAD):
                            first_residual(i)
                        normalise(0)
                        sum_up(1, 1, 1)
                        normalise(1)
                        low_part(0)
                        sum_up(1, 2, 2)
                        sum_squares(1, 1, 1, 1)
                        sum_squares(1, 2, 2, 0)
                        inverse_std(nc, dve, s_step, n, lambda q: stat[:, q, 1:3, 0, :])
                        dve.sem_inc(s_root, 1)
                        for p in range(PAIRS):
                            mine = [(kind, t) for kind, t in ((1, p + 2), (2, p - 2)) if p and 0 <= t < STRIPS]
                            slot = (p + 2) % 3
                            kinds = slice(mine[0][0] - 1, mine[-1][0]) if mine else None

                            def root(lo, hi):
                                for j in range(lo, hi):
                                    if mine:
                                        root_step(nc, dve, s_step, n, lambda q: stat[:, q, slot, kinds, :], j)

                            for odd in range(2):
                                i = 2 * p + odd
                                if i + 2 < BLOCKS:
                                    normalise(i + 2)
                                if odd:
                                    root(5, 7)
                                if i + 1 < BLOCKS:
                                    low_part(i + 1)
                                if odd:
                                    root(7, 9)
                                else:
                                    for kind, t in mine:
                                        sum_squares(kind, t, slot, kind - 1)
                                    root(0, 1)
                                if 0 <= i - 2 < BLOCKS:
                                    second_residual(i - 2)
                                root(9, 11) if odd else root(1, 3)
                                if i + AHEAD < BLOCKS:
                                    first_residual(i + AHEAD)
                                root(11, ROOT_STEPS) if odd else root(3, 5)
                            if mine:
                                dve.wait_ge(s_step, n[0])
                                dve.sem_inc(s_root, 1)
                            for kind, t in ((1, p + 3), (2, p - 1)):
                                if 0 <= t < STRIPS:
                                    sum_up(kind, t, (p + 3) % 3)
                        hs = slice((STRIPS - 1) * SH, P)
                        V.tensor_tensor(y[:, :, hs], x[:, :, hs], stat[:, 3, STRIPS % 3, 1, :][:, None, :].broadcast_to(
                            [P, C, SH]), ALU.mult)

                    @block.scalar
                    def _(act):
                        A = nc.scalar.activation

                        for i in range(GROUPS):
                            act.wait_ge(s_g_dve, i + 1)
                            A(g[:, :, 2, 4 * i:4 * i + 4], g[:, :, 0, 4 * i:4 * i + 4], ACT.Copy, scale=-1.0
                              ).then_inc(s_g_act, 1)
                        act.wait_ge(s_wready, 1)
                        for t in range(1, N_CHUNK + 3):
                            j = t - 1
                            if j < N_CHUNK:
                                cols = chunk(j) * P
                                act.wait_ge(s_mix1, j + 1)
                                if j >= 2:
                                    act.wait_ge(s_mix2, j - 1)
                                first = 0
                                if j == 0:
                                    A(o1[:, 0, 0:1], bank[4][:, 0:1], ACT.Relu, bias=mix1_b0[:])
                                    first = 1
                                A(o1[:, j % 2, first:cols], bank[4 + j % 2][:, first:cols], ACT.Relu, bias=mix1_b[:]
                                  ).then_inc(s_o1, 1)
                            j = t - 2
                            if 0 <= j < N_CHUNK:
                                k = chunk(j)
                                act.wait_ge(s_o2, j + 1)
                                if j >= 2:
                                    act.wait_ge(s_top, j - 1)
                                A(mag[:, j % 2, 0:k], o2[:, j % 2, 0:k], ACT.Abs).then_inc(s_mag, 1)
                            j = t - 3
                            if 0 <= j < N_CHUNK:
                                k, col = chunk(j), 4 * j
                                act.wait_ge(s_masked, j + 1)
                                ins = A(m2[:, :, col:col + k].rearrange("p c k -> p k c"), im[:, j % 2, 0:k],
                                        ACT.Copy, scale=-1.0)
                                if j < N_CHUNK - 1:
                                    lo = 1 if j == 0 else 0
                                    to = slice(HALF + col + lo, HALF + col + 4)
                                    A(m1[:, :, to].rearrange("p c k -> p k c"), im[:, j % 2, lo:4], ACT.Copy)
                                    ins = A(m2[:, :, to], m1[:, :, col + lo:col + 4], ACT.Copy)
                                ins.then_inc(s_m, 1)
                        for i in range(1, GROUPS, 2):
                            act.wait_ge(s_ih, i + 1)
                            A(iy[:, 4 * i:4 * i + 4, :], four(bank[1][:]), ACT.Copy).then_inc(s_iy[1], 1)

                        def square(kind, t, buffer):
                            act.wait_ge((s_x, s_res)[kind - 1], (t + 1) * STRIP)
                            if square_count(kind, t) > 1:
                                act.wait_ge(s_sq_read[buffer], square_count(kind, t) - 1)
                            A(sq[:, buffer], x[:, :, t * SH:(t + 1) * SH], ACT.Square).then_inc(s_sq[buffer], 1)

                        def transposed(i):
                            act.wait_ge(s_tr, i + 1)
                            if i >= 2:
                                act.wait_ge(s_up, 4 * (i - 1))
                            A(yc[:, i % 2, :], bank[2][:].bitcast(F16), ACT.Copy).then_inc(s_yc, 1)

                        def high_part(i):
                            act.wait_ge(s_y2, i + 1)
                            if i >= 2:
                                act.wait_ge(s_tr, i - 1)
                            A(y2s[:, i % 2, :, 0, :], y2[:, i % 2], ACT.Copy).then_inc(s_high, 1)

                        square(1, 0, 0)
                        square(1, 1, 1)
                        square(1, 2, 0)
                        high_part(0)
                        high_part(1)
                        transposed(0)
                        for i in range(2 * PAIRS):
                            if i < BLOCKS:
                                for j in range(4):
                                    act.wait_ge(s_up, 4 * i + j + 1)
                                    if i >= 2 and j == 0:
                                        act.wait_ge(s_down, i - 1)
                                    A(hidden[:, i % 2, j, :], bank[4 + j][:], ACT.Gelu, scale=1.0 / W_SCALE,
                                      bias=up_b[:, HC + j % HC:HC + j % HC + 1]).then_inc(s_hid, 1)
                            if i + 1 < BLOCKS:
                                transposed(i + 1)
                            if i + 2 < BLOCKS:
                                high_part(i + 2)
                            if 0 <= i - 1 < BLOCKS:
                                act.wait_ge(s_down, i)
                                if i >= 3:
                                    act.wait_ge(s_back, i - 2)
                                A(delta[:, (i - 1) % 2, :], bank[3][:], ACT.Copy).then_inc(s_delta, 1)
                            if i % 2:
                                for kind, t in ((1, i // 2 + 3), (2, i // 2 - 1)):
                                    if 0 <= t < STRIPS:
                                        square(kind, t, kind - 1)

                    @block.tensor
                    def _(pe):
                        M = nc.tensor.matmul
                        for i in range(GROUPS):
                            if i >= 2:
                                pe.wait_ge(s_g_dve, i - 1)
                            for c in range(4):
                                mm = M(bank[i % 2][:, c * P:(c + 1) * P], y[:, 4 * i + c, :], dft_w[:], start=True,
                                       stop=True)
                            mm.then_inc(s_fw, 1)
                        pe.wait_ge(s_wscaled, 1)
                        M(bank[7][:, 0:P], centre[:], mix1_s[:], start=True, stop=True)
                        M(bank[5][:, 0:1], mix1[0:C, :], ln1[0:C, 1:2], start=True, stop=True)
                        for j in range(HC):
                            mm = M(bank[5][:, 1 + j:2 + j], up[0:C, j * P:(j + 1) * P], ln2[0:C, 1:2], start=True,
                                   stop=True)
                        mm.then_inc(s_wfold, 1)
                        for i in range(N_CHUNK + 2):
                            if i < N_CHUNK:
                                if i == 0:
                                    pe.wait_ge(s_g_dve, GROUPS)
                                    pe.wait_ge(s_g_act, GROUPS)
                                    pe.wait_ge(s_zero, 1)
                                if i >= 2:
                                    pe.wait_ge(s_xf, i - 1)
                                for k in range(chunk(i)):
                                    kw = 4 * i + k
                                    to = bank[2 + i % 2][:, k * P:(k + 1) * P]
                                    M(to, g[:, kw, 0:2, :].rearrange("p r c -> p (r c)"), cos[:], start=True, stop=False)
                                    mm = M(to, g[:, kw, 1:3, :].rearrange("p r c -> p (r c)"), sin[:], start=False,
                                           stop=True)
                                mm.then_inc(s_fh, 1)
                            j = i - 1
                            if 0 <= j < N_CHUNK:
                                if j == 0:
                                    pe.wait_ge(s_wready, 1)
                                pe.wait_ge(s_xf, j + 1)
                                if j >= 2:
                                    pe.wait_ge(s_o1, j - 1)
                                cols = chunk(j) * P
                                M(bank[4 + j % 2][:, 0:cols], mix1_fold[:], xf[:, j % 2, 0:cols], start=True, stop=True
                                  ).then_inc(s_mix1, 1)
                            j = i - 2
                            if 0 <= j < N_CHUNK:
                                pe.wait_ge(s_o1, j + 1)
                                if j >= 2:
                                    pe.wait_ge(s_o2, j - 1)
                                for k in range(chunk(j)):
                                    mm = M(bank[6 + j % 2][:, k * P:(k + 1) * P], o1[:, j % 2, k * P:(k + 1) * P],
                                           mix2[:], start=True, stop=True)
                                mm.then_inc(s_mix2, 1)
                        pe.wait_ge(s_m, N_CHUNK)
                        for i in range(GROUPS):
                            if i >= 2:
                                pe.wait_ge(s_iy[i % 2], i // 2)
                            for c in range(4):
                                to = bank[i % 2][:, c * P:(c + 1) * P]
                                M(to, m1[:, 4 * i + c, :], cos[:], start=True, stop=False)
                                mm = M(to, m2[:, 4 * i + c, :], sin[:], start=False, stop=True)
                            mm.then_inc(s_ih, 1)
                        pe.wait_ge(s_iy[0], GROUPS // 2)
                        pe.wait_ge(s_iy[1], GROUPS // 2)

                        def inverse(i):
                            if i >= 2:
                                pe.wait_ge(s_x, inverse_before(i) + 1)
                            M(bank[inverse_bank(i)][:], idft_w[:], iy[:, :, i * HB:(i + 1) * HB], start=True, stop=True
                              ).then_inc(s_iw, 1)

                        def turn(i):
                            pe.wait_ge(s_low, i + 1)
                            if i >= 1:
                                pe.wait_ge(s_yc, i)
                            for h in range(HB):
                                mm = nc.tensor.transpose(bank[2][:].bitcast(F16)[:, h * P:(h + 1) * P],
                                                         y2s[:, i % 2, h].rearrange("p r c -> p (r c)"), ident16[:])
                            mm.then_inc(s_tr, 1)

                        def mlp_up(i):
                            pe.wait_ge(s_yc, i + 1)
                            for j in range(4):
                                if i >= 1:
                                    pe.wait_ge(s_hid, 4 * (i - 1) + j + 1)
                                for part in range(2):
                                    mm = M(bank[4 + j][:], up_w[:, part, j % HC * P:(j % HC + 1) * P],
                                           yc[:, i % 2, j // HC * BANK:(j // HC + 1) * BANK], start=part == 0,
                                           stop=part == 1)
                                mm.then_inc(s_up, 1)

                        def mlp_down(i):
                            pe.wait_ge(s_hid, 4 * (i + 1))
                            if i >= 1:
                                pe.wait_ge(s_delta, i)
                            for j in range(4):
                                mm = M(bank[3][:], down[:, j // HC, j % HC, :], hidden[:, i % 2, j, :], start=j == 0,
                                       stop=j == 3)
                            mm.then_inc(s_down, 1)

                        def turn_back(i):
                            pe.wait_ge(s_delta, i + 1)
                            pe.wait_ge(s_x, AHEAD)
                            if i >= 1:
                                pe.wait_ge(s_res, i)
                            for k in range(HB // 2):
                                mm = nc.tensor.transpose(bank[1][:, k * P:(k + 1) * P],
                                                         delta[:, i % 2, k * P:(k + 1) * P], ident[:])
                            mm.then_inc(s_back, 1)

                        for i in range(AHEAD):
                            inverse(i)
                        turn(0)
                        for i in range(BLOCKS + 2):
                            if i < BLOCKS:
                                mlp_up(i)
                            if 0 <= i - 2 < BLOCKS:
                                turn_back(i - 2)
                            if i + AHEAD < BLOCKS:
                                inverse(i + AHEAD)
                            if i + 1 < BLOCKS:
                                turn(i + 1)
                            if 0 <= i - 1 < BLOCKS:
                                mlp_down(i - 1)
                for q in sems:
                    nc.gpsimd.sem_clear(q)
                nc.all_engine_barrier()
            with nc.Block() as block:
                @block.sync
                def _(sp):
                    sp.dma_start(dst[b], x[:]).then_inc(s_store, 16)
                    sp.wait_ge(s_store, 16)
            nc.gpsimd.sem_clear(s_store)
            nc.all_engine_barrier()


LAYER_INPUTS = {
    "L0_conv": ["w1", "bn1_gamma", "bn1_beta", "bn1_mean", "bn1_var", "x_min", "x_max", "y_min", "y_max",
                "bn2_gamma", "bn2_beta", "bn2_mean", "bn2_var"],
    "L1_conv": ["ln1_w", "ln1_b", "ln2_w", "ln2_b", "w1", "w2", "b1", "b2", "mlp_w1", "mlp_b1", "mlp_w2", "mlp_b2"],
}
LAYER_INPUTS["L2_conv"] = LAYER_INPUTS["L3_conv"] = LAYER_INPUTS["L0_conv"]


def build(nc, ins, out):
    const = ins["constants"]
    part = {t: {n: ins[f"{t}_{n}"] for n in names} for t, names in LAYER_INPUTS.items()}

    def scratch(name, shape):
        return nc.dram_tensor(name, shape, F32, kind="Internal").ap()

    turned = [scratch(f"turned{i}", [B, P, C, P]) for i in range(3)]
    z = [scratch(f"z{i}", [B, K, P, P]) for i in range(3)]
    x = ins["x"]

    def edges(w, p, q):
        return w | {"p_max": w[p + "_max"], "p_min": w[p + "_min"], "q_max": w[q + "_max"], "q_min": w[q + "_min"]}

    def from_turned(t):
        return {"pcq": lambda b: t[b], "half": lambda b, h: t[b, h * HALF:(h + 1) * HALF].rearrange("w c h -> c w h")}

    box_layer(nc, "L0", const, edges(part["L0_conv"], "x", "y"), True,
              {"pcq": lambda b: x[b].rearrange("c h w -> h c w"), "half": lambda b, h: x[b, :, h * HALF:(h + 1) * HALF]},
              lambda b: turned[0][b], z[0])
    afno_layers(nc, const, part["L1_conv"], turned[0], turned[1])
    box_layer(nc, "L2", const, edges(part["L2_conv"], "y", "x"), False, from_turned(turned[1]),
              lambda b: turned[2][b], z[1])
    box_layer(nc, "L3", const, edges(part["L3_conv"], "y", "x"), True, from_turned(turned[2]),
              lambda b: out[b].rearrange("c h w -> h c w"), z[2])


def kernel(**inputs):
    import concourse.bacc as bacc
    from concourse.bass_utils import run_bass_kernel_spmd

    nc = bacc.Bacc("TRN2", target_bir_lowering=False, num_devices=1)
    names = ["x"] + [f"{t}_{n}" for t, ns in LAYER_INPUTS.items() for n in ns]
    arrays = {n: np.ascontiguousarray(inputs[n]) for n in names}
    arrays["constants"] = constants()
    aps = {n: nc.dram_tensor(f"in_{n}", a.shape, mybir.dt.from_np(a.dtype), kind="ExternalInput").ap()
           for n, a in arrays.items()}
    out = nc.dram_tensor("out", (B, C, P, P), F32, kind="ExternalOutput").ap()
    build(nc, aps, out)
    r = run_bass_kernel_spmd(nc, [{f"in_{n}": a for n, a in arrays.items()}], core_ids=[0])
    return r.results[0]["out"]
```

```python
from contextlib import ExitStack

import numpy as np

import concourse.bass as bass
from concourse import mybir

F32 = mybir.dt.float32
F16 = mybir.dt.float16
I32 = mybir.dt.int32
ALU = mybir.AluOpType
ACT = mybir.ActivationFunctionType
AX = mybir.AxisListType

P = 128
B, C = 4, 64
NB = 4
K = C // NB
HALF = P // 2
L = 4
HID = 256
HC = HID // P
KW = P // 2 + 1
THR = 0.01
BANK = 512

UNITS = 4 * B
RING = 8
U_ROWS = HALF // 4
U_CHUNKS = U_ROWS * P // BANK

BN1_EPS, BN2_EPS, LN_EPS = 1e-5, 1e-3, 1e-5

DELTA_Z, DELTA, IDENT, DFT_W, DFT_H, COS, SIN, IDFT_W, CENTRE, N_CONST = range(10)


def z_rows():
    return np.arange(P).reshape(2, UNITS // B, U_CHUNKS, -1).transpose(1, 2, 0, 3).reshape(-1)


def constants():
    n = np.arange(P)
    out = np.zeros((N_CONST, P, P))
    out[DELTA] = n[None, :] - n[:, None]
    out[DELTA_Z] = n[None, :] - z_rows()[:, None]
    out[IDENT] = np.eye(P)
    turn = 2 * np.pi * (np.outer(n, n) % P) / P
    out[COS], out[SIN] = np.cos(turn), np.sin(turn)
    out[DFT_H] = np.cos(turn)
    out[DFT_H][HALF + 1:] = -np.sin(turn[HALF + 1:])
    out[DFT_W][:, :KW] = np.cos(turn[:, :KW]) / P
    out[DFT_W][:, KW:] = -np.sin(turn[:, 1:KW - 1]) / P
    out[IDFT_W][:HALF] = 2 * np.cos(turn[:HALF]) / P
    out[IDFT_W][0] = 1 / P
    out[IDFT_W][HALF] = np.cos(turn[HALF]) / P
    out[IDFT_W][HALF + 1:] = -2 * np.sin(turn[1:HALF]) / P
    for h in range(2):
        out[CENTRE][h * C:(h + 1) * C, h * C:(h + 1) * C] = np.eye(C) - 1 / C
    return out.astype(np.float32)


def chain(eng, sem, count, ins):
    count[0] += 1
    ins.then_inc(sem, 1)
    eng.wait_ge(sem, count[0])


def clear(nc, sems):
    nums = sorted(s.num for s in sems)
    starts = [n for n in nums if n - 1 not in nums]
    for a in starts:
        b = a
        while b in nums:
            b += 1
        nc.gpsimd.sem_clear(range(a, b))


def box_layer(nc, layer, const, w, turns, src, dst, zd, s_par, s_z_out):
    tag = f"box{layer}"
    par_before, z_before = layer * 16 * N_PAR, layer * 16 * UNITS // 4
    with ExitStack() as ctx:
        def sb(name, shape):
            return ctx.enter_context(nc.sbuf_tensor(f"{tag}_{name}", shape, F32))

        def psum(name):
            return ctx.enter_context(nc.psum_tensor(f"{tag}_{name}", [P, BANK], F32))

        def sem(name):
            return ctx.enter_context(nc.semaphore(f"{tag}_{name}"))

        banks = [psum(f"bank{i}") for i in range(8)]
        z_banks = (3, 4, 6, 7)
        delta, ident = sb("delta", [P, 2, P]), sb("ident", [P, P])
        edges = sb("edges", [P, 2, 2, C])
        bn2 = sb("bn2", [P, 4, C])
        affine, t2 = sb("affine", [P, 2, C]), sb("t2", [P, 3, C])
        scale2, bias2 = affine[:, 0, :], affine[:, 1, :]
        bn1r = sb("bn1r", [P, 2, K])
        bn1c = sb("bn1c", [P, 4])
        inv1 = sb("inv1", [P, K])
        inv1c, bias1 = sb("inv1c", [P, 1]), sb("bias1", [P, 2])
        w1t = sb("w1t", [P, K])
        w1bd = sb("w1bd", [P, 2 * K])
        xc = sb("xc", [P, RING, U_ROWS * P])
        zs = sb("zs", [P, 4, BANK])
        z = sb("z", [P, 3, B, P])
        x = sb("x", [P, 3, B, NB, P])
        raw = sb("raw", [P, 3, 4, NB, P])
        taps = sb("taps", [P, 3, 2, NB, P])
        affine_k = sb("affine_k", [P, 3, 2, NB])
        half1 = sb("half1", [P, 2, NB, P])
        pre = sb("pre", [P, 2, NB, P])
        summed = sb("summed", [P, 2, NB, P])
        o = sb("o", [P, 4, NB, P])

        s_par1, s_var1, s_sqrt1, s_w1, s_bias1 = (sem(x) for x in ("par1", "var1", "sqrt1", "w1", "bias1"))
        s_par_c = sem("par_c")
        s_step, s_sqrt, s_var = (sem(x) for x in ("step", "sqrt", "var"))
        s_unit = [sem(f"unit{i}") for i in range(RING)]
        s_z_mm, s_z_dve, s_z_act = sem("z_mm"), sem("z_dve"), sem("z_act")
        s_z_first = [sem(f"z_first{b}") for b in range(B)]
        s_z_ld, s_x_ld = [sem(f"z_ld{i}") for i in range(3)], [sem(f"x_ld{i}") for i in range(3)]
        s_raw, s_clip, s_taps, s_bn2 = sem("raw"), sem("clip"), sem("taps"), sem("bn2")
        s_f1, s_h1, s_f2, s_pre, s_sum, s_relu = (sem(n) for n in ("f1", "h1", "f2", "pre", "sum", "relu"))
        s_out = [sem(f"out{i}") for i in range(4)]

        def bc(a):
            return a.partition_broadcast(P)

        def following(i, l):
            return (i, l + 1) if l + 1 < GROUP_STEPS else (i + 1, 0)

        def is_first_group(i):
            return isinstance(i, int) and i == 0

        def is_last_group(i):
            return isinstance(i, int) and i == GROUPS_K - 1

        def two_on(i, u):
            return (i, u + 2) if u == 0 else (i + 1, u - 1)

        def beyond(i, u):
            return isinstance(i, int) and 3 * i + u >= K

        def steps(i):
            return B if is_last_group(i) else GROUP_STEPS

        def run(eng, group):
            group(0)
            with eng.Fori(1, GROUPS_K - 2) as i:
                group(i)
            for i in range(GROUPS_K - 2, GROUPS_K):
                group(i)

        with nc.Block() as block:
            @block.sync
            def _(sp):
                def load_unit(t):
                    b, j = divmod(t, B)
                    if t >= RING:
                        sp.wait_ge(s_z_mm, t - RING + 1)
                    for h in range(2):
                        sp.dma_start(xc[h * C:(h + 1) * C, t % RING, :].rearrange("c (p q) -> c p q", q=P),
                                     src["half"](b, h)[:, j * U_ROWS:(j + 1) * U_ROWS, :]).then_inc(s_unit[t % RING], 16)

                def load_x(k, u):
                    for b in range(B):
                        sp.dma_start(x[:, u, b], src["pcq"](b)[:, bass.ds(k * NB, NB), :]).then_inc(s_x_ld[u], 16)

                def load_z(k, u):
                    sp.dma_start(z[:, u], zd[:, k].rearrange("b p q -> p b q")).then_inc(s_z_ld[u], 16)

                with nc.allow_non_contiguous_dma("small parameters"):
                    for i, n in enumerate(("bn1_gamma", "bn1_var")):
                        sp.dma_start(bn1r[:, i, :], bc(w[n])).then_inc(s_par1, 16)
                    for h in range(2):
                        sp.dma_start(w1t[h * C:(h + 1) * C, :], w["w1"].rearrange("k c -> c k")).then_inc(s_par1, 16)
                    for t in range(UNITS):
                        load_unit(t)
                        if t == 11:
                            load_x(0, 0)
                    for b in range(B):
                        if b == B - 1:
                            load_x(1, 1)
                        for i in range(4):
                            sp.wait_ge(s_z_out[i], z_before + 16 * (b + 1))
                        sp.dma_start(z[:, 0, b, :], zd[b, 0]).then_inc(s_z_first[b], 16)
                    load_z(1, 1)
                    load_z(2, 2)
                    load_x(2, 2)

                def group(i):
                    for l in range(steps(i)):
                        u, b = divmod(l, B)
                        if b == 0 and not (is_first_group(i) and u == 0) and not beyond(i, u + 2):
                            sp.wait_ge(s_sum, i * GROUP_STEPS + l)
                            load_z(i * 3 + u + 2, (u + 2) % 3)
                            load_x(i * 3 + u + 2, (u + 2) % 3)
                        sp.wait_ge(s_relu, i * GROUP_STEPS + l + 1)
                        sp.dma_start(dst(b)[:, bass.ds((i * 3 + u) * NB, NB), :], o[:, l % 4]).then_inc(s_out[l % 4], 16)

                run(sp, group)
                for i in range(4):
                    sp.wait_ge(s_out[i], 16 * (K * B // 4))

            @block.gpsimd
            def _(pool):
                par = [(bn2[:, i, :], bc(w[n])) for i, n in enumerate(("bn2_gamma", "bn2_beta", "bn2_mean", "bn2_var"))]
                for ax, names in enumerate((("p_max", "p_min"), ("q_max", "q_min"))):
                    for m, n in enumerate(names):
                        par.append((edges[:, ax, m, :], bc(w[n].rearrange("k n -> (k n)"))))
                par += [(delta[:, 0, :], const[DELTA_Z]), (delta[:, 1, :], const[DELTA]), (ident[:], const[IDENT])]
                assert len(par) == N_PAR
                for a, d in par:
                    pool.dma_start(a, d).then_inc(s_par, 16)

                def store_unit(t):
                    b, part = divmod(t, UNITS // B)
                    pool.wait_ge((s_z_dve, s_z_act)[t % 2], t // 2 + 1)
                    to = zd[b].rearrange("k (t j r) q -> t j k (r q)", t=UNITS // B, j=2 * U_CHUNKS)[part]
                    pool.dma_start(to, zs[:, t % 4, :]).then_inc(s_z_out[t % 4], 16)

                def make_raw(i, u):
                    if not is_first_group(i):
                        pool.wait_ge(s_taps, i * 3 + u - 2)
                    for axis in range(2):
                        e = edges[:, axis, :, bass.ds((i * 3 + u) * NB, NB)]
                        d = delta[:, axis, None, None, :].broadcast_to([P, 2, NB, P])
                        ins = nc.gpsimd.tensor_tensor(raw[:, u, 2 * axis:2 * axis + 2], d,
                                                      e[:, :, :, None].broadcast_to([P, 2, NB, P]), ALU.add)
                    ins.then_inc(s_raw, 1)

                def group(i):
                    if is_first_group(i):
                        for t in range(UNITS):
                            store_unit(t)
                            if 2 <= t < 5:
                                if t == 2:
                                    pool.wait_ge(s_par, par_before + 16 * N_PAR)
                                make_raw(0, t - 2)
                    else:
                        for u in range(steps(i) // B):
                            make_raw(i, u)

                run(pool, group)
                for i in range(4):
                    pool.wait_ge(s_z_out[i], z_before + 16 * UNITS // 4)

            @block.vector
            def _(dve):
                n = [0]
                V = nc.vector

                def make_taps(i, u, part):
                    k = i * 3 + u
                    r = raw[:, u].rearrange("p (a m) n i -> p a m (n i)", a=2)
                    if part == 0:
                        dve.wait_ge(s_raw, k + 1)
                        V.tensor_scalar(raw[:, u], raw[:, u], 0.0, 1.0, ALU.max, ALU.min).then_inc(s_clip, 1)
                    elif part == 1:
                        dve.wait_ge(s_clip, k + 1)
                        if not is_first_group(i):
                            dve.wait_ge(s_f2, i * GROUP_STEPS + (u - 2) * B)
                        V.tensor_copy(affine_k[:, u], affine[:, :, bass.ds(k * NB, NB)])
                        V.tensor_tensor(taps[:, u].rearrange("p a n i -> p a (n i)"), r[:, :, 0], r[:, :, 1],
                                        ALU.subtract).then_inc(s_taps, 1)

                dve.wait_ge(s_par1, 16 * 4)
                V.memset(w1bd[:], 0.0)
                V.tensor_scalar(inv1[:], bn1r[:, 1, :], BN1_EPS, None, ALU.add).then_inc(s_var1, 1)
                dve.wait_ge(s_sqrt1, 1)
                chain(dve, s_step, n, V.reciprocal(inv1[:], inv1[:]))
                chain(dve, s_step, n, V.tensor_tensor(inv1[:], inv1[:], bn1r[:, 0, :], ALU.mult))
                for h in range(2):
                    V.tensor_tensor(w1bd[h * C:(h + 1) * C, h * K:(h + 1) * K], w1t[h * C:(h + 1) * C, :],
                                    inv1[h * C:(h + 1) * C, :], ALU.mult).then_inc(s_w1, 1)
                dve.wait_ge(s_par_c, 16 * 4)
                V.tensor_scalar(inv1c[:], bn1c[:, 0:1], BN1_EPS, None, ALU.add).then_inc(s_var, 1)
                dve.wait_ge(s_sqrt, 1)
                chain(dve, s_step, n, V.reciprocal(inv1c[:], inv1c[:]))
                chain(dve, s_step, n, V.tensor_tensor(inv1c[:], inv1c[:], bn1c[:, 1:2], ALU.mult))
                chain(dve, s_step, n, V.tensor_tensor(bias1[:, 0:1], inv1c[:], bn1c[:, 2:3], ALU.mult))
                V.tensor_tensor(bias1[:, 1:2], bn1c[:, 3:4], bias1[:, 0:1], ALU.subtract).then_inc(s_bias1, 1)

                def second_bn():
                    dve.wait_ge(s_par, par_before + 16 * N_PAR)
                    V.tensor_scalar(t2[:, 0, :], bn2[:, 3, :], BN2_EPS, None, ALU.add).then_inc(s_var, 1)
                    dve.wait_ge(s_sqrt, 2)
                    chain(dve, s_step, n, V.reciprocal(t2[:, 0, :], t2[:, 0, :]))
                    chain(dve, s_step, n, V.tensor_tensor(t2[:, 0, :], t2[:, 0, :], bn2[:, 0, :], ALU.mult))
                    V.tensor_tensor(bias2, t2[:, 0, :], bn2[:, 2, :], ALU.mult)
                    V.tensor_tensor(t2[:, 1, :], edges[:, 0, 0, :], edges[:, 0, 1, :], ALU.subtract)
                    chain(dve, s_step, n, V.tensor_tensor(t2[:, 2, :], edges[:, 1, 0, :], edges[:, 1, 1, :],
                                                          ALU.subtract))
                    V.tensor_tensor(bias2, bn2[:, 1, :], bias2, ALU.subtract)
                    chain(dve, s_step, n, V.tensor_tensor(t2[:, 1, :], t2[:, 1, :], t2[:, 2, :], ALU.mult))
                    chain(dve, s_step, n, V.reciprocal(t2[:, 2, :], t2[:, 1, :]))
                    V.tensor_tensor(scale2, t2[:, 0, :], t2[:, 2, :], ALU.mult).then_inc(s_bn2, 1)
                    dve.wait_ge(s_bn2, 1)

                dve.wait_ge(s_bias1, 1)
                for t in range(0, UNITS, 2):
                    dve.wait_ge(s_z_mm, t + 1)
                    if t >= 4:
                        dve.wait_ge(s_z_out[t % 4], z_before + 16 * (t // 4))
                    V.tensor_scalar(zs[:, t % 4, :], banks[z_banks[t % 4]][:], bias1[:, 1:2], None, ALU.add
                                    ).then_inc(s_z_dve, 1)
                    if t == 4:
                        second_bn()
                    if 6 <= t < 6 + 8:
                        make_taps(0, *divmod(t // 2 - 3, 2))

                def relu(i, l):
                    s = i * GROUP_STEPS + l
                    dve.wait_ge(s_sum, s + 1)
                    if not is_first_group(i) or l >= 4:
                        dve.wait_ge(s_out[l % 4], 16 * (i * 3 + l // 4))
                    V.tensor_scalar(o[:, l % 4], summed[:, l % 2], 0.0, None, ALU.max).then_inc(s_relu, 1)

                def group(i):
                    for l in range(steps(i)):
                        u, b = divmod(l, B)
                        s = i * GROUP_STEPS + l
                        if not turns and b == 0:
                            dve.wait_ge(s_x_ld[u], 16 * B * (i + 1))
                        dve.wait_ge(s_pre, s + 1)
                        res = (banks[5 + l % 3].rearrange("p (n i) -> p n i", n=NB) if turns else x[:, u, b])
                        V.tensor_tensor(summed[:, l % 2], pre[:, l % 2], res, ALU.add).then_inc(s_sum, 1)
                        if b < 2 and not beyond(i, u + 2):
                            make_taps(*two_on(i, u), b)
                        relu(i, l)

                run(dve, group)

            @block.scalar
            def _(act):
                with nc.allow_non_contiguous_dma("small parameters"):
                    for i, n in enumerate(("bn1_var", "bn1_gamma", "bn1_mean", "bn1_beta")):
                        act.dma_start(bn1c[:, i:i + 1], w[n].rearrange("(k a) -> k a", a=1).partition_broadcast(P // K)
                                      ).then_inc(s_par_c, 16)
                act.wait_ge(s_var1, 1)
                nc.scalar.activation(inv1[:], inv1[:], ACT.Sqrt).then_inc(s_sqrt1, 1)
                act.wait_ge(s_var, 1)
                nc.scalar.activation(inv1c[:], inv1c[:], ACT.Sqrt).then_inc(s_sqrt, 1)
                act.wait_ge(s_bias1, 1)
                for t in range(1, UNITS, 2):
                    act.wait_ge(s_z_mm, t + 1)
                    if t >= 4:
                        act.wait_ge(s_z_out[t % 4], z_before + 16 * (t // 4))
                    nc.scalar.activation(zs[:, t % 4, :], banks[z_banks[t % 4]][:], ACT.Identity, bias=bias1[:, 1:2]
                                         ).then_inc(s_z_act, 1)
                    if t == 5:
                        act.wait_ge(s_var, 2)
                        nc.scalar.activation(t2[:, 0, :], t2[:, 0, :], ACT.Sqrt).then_inc(s_sqrt, 1)

                def second_bn(i, l):
                    u, b = divmod(l, B)
                    s = i * GROUP_STEPS + l
                    act.wait_ge(s_f2, s + 1)
                    if not is_first_group(i) or l >= 2:
                        act.wait_ge(s_sum, s - 1)
                    for n in range(NB):
                        ins = nc.scalar.activation(pre[:, l % 2, n], banks[2 + l % 3][:, n * P:(n + 1) * P], ACT.Relu,
                                                   bias=affine_k[:, u, 1, n:n + 1], scale=affine_k[:, u, 0, n:n + 1])
                    ins.then_inc(s_pre, 1)

                def group(i):
                    for l in range(steps(i)):
                        s = i * GROUP_STEPS + l
                        act.wait_ge(s_f1, s + 1)
                        if not is_first_group(i) or l >= 2:
                            act.wait_ge(s_f2, s - 1)
                        nc.scalar.activation(half1[:, l % 2], banks[l % 2].rearrange("p (n i) -> p n i", n=NB),
                                             ACT.Copy).then_inc(s_h1, 1)
                        if l:
                            second_bn(i, l - 1)
                        elif not is_first_group(i):
                            second_bn(i - 1, GROUP_STEPS - 1)

                run(act, group)
                second_bn(GROUPS_K - 1, B - 1)

            @block.tensor
            def _(pe):
                pe.wait_ge(s_w1, 2)
                for t in range(UNITS):
                    pe.wait_ge(s_unit[t % RING], 32 * (t // RING + 1))
                    if t >= 4:
                        pe.wait_ge((s_z_dve, s_z_act)[t % 2], t // 2 - 1)
                    for j in range(U_CHUNKS):
                        mm = nc.tensor.matmul(banks[z_banks[t % 4]][j * 2 * K:(j + 1) * 2 * K, :], w1bd[:],
                                              xc[:, t % RING, j * BANK:(j + 1) * BANK], start=True, stop=True)
                    mm.then_inc(s_z_mm, 1)

                def first(i, l):
                    u, b = divmod(l, B)
                    if is_first_group(i) and u == 0:
                        pe.wait_ge(s_z_first[b], 16)
                    elif b == 0:
                        pe.wait_ge(s_z_ld[u], 16 * (i + (u > 0)))
                    if b == 0:
                        pe.wait_ge(s_x_ld[u], 16 * B * (i + 1))
                        pe.wait_ge(s_taps, i * 3 + u + 1)
                    if not is_first_group(i) or l >= 2:
                        pe.wait_ge(s_h1, i * GROUP_STEPS + l - 1)
                    nc.tensor.matmul(banks[l % 2][:], z[:, u, b, :], taps[:, u, 0].rearrange("p n i -> p (n i)"),
                                     start=True, stop=True).then_inc(s_f1, 1)

                def second(i, l):
                    u, b = divmod(l, B)
                    if is_first_group(i) and l == 1:
                        pe.wait_ge(s_z_dve, UNITS // 2)
                        pe.wait_ge(s_z_act, UNITS // 2)
                    if not is_first_group(i) or l >= 3:
                        pe.wait_ge(s_sum, i * GROUP_STEPS + l - 2)
                    if turns:
                        for j in range(NB):
                            nc.tensor.transpose(banks[5 + l % 3][:, j * P:(j + 1) * P], x[:, u, b, j, :], ident[:])
                    pe.wait_ge(s_h1, i * GROUP_STEPS + l + 1)
                    for j in range(NB):
                        h, t = half1[:, l % 2, j, :], taps[:, u, 1, j, :]
                        mm = nc.tensor.matmul(banks[2 + l % 3][:, j * P:(j + 1) * P], t if turns else h,
                                              h if turns else t, start=True, stop=True)
                    mm.then_inc(s_f2, 1)

                def group(i):
                    for l in range(steps(i)):
                        if l + 1 < steps(i) or not is_last_group(i):
                            first(*following(i, l))
                        second(i, l)

                pe.wait_ge(s_par, par_before + 16 * N_PAR)
                first(0, 0)
                run(pe, group)
        clear(nc, [s_par1, s_par_c, s_var1, s_sqrt1, s_w1, s_bias1, s_step, s_sqrt, s_var, s_z_mm, s_z_dve, s_z_act]
                  + s_unit + s_z_first + s_z_ld + s_x_ld
                  + [s_raw, s_clip, s_taps, s_bn2, s_f1, s_h1, s_f2, s_pre, s_sum, s_relu] + s_out)
        nc.all_engine_barrier()


GROUPS_K = (K + 2) // 3
GROUP_STEPS = 3 * B
PAIRS = 10
N_PAR = 4 + 4 + 3
N_CHUNK = 17
N_WLOAD_MIX = 11
N_WLOAD = 22
GROUPS = C // 4
HB = 8
BLOCKS = P // HB
STRIP = 2
SH = HB * STRIP
STRIPS = BLOCKS // STRIP
LOADS = 4
POOL_SHARE = 20
AHEAD = 3 * STRIP
W_SCALE = 64.0
ROOT_STEPS = 14
RSQRT_GUESS = 0x5F3759DF


def chunk(i):
    return 4 if i < N_CHUNK - 1 else 1


def inverse_bank(i):
    return (0, 1, 4, 5, 6, 7)[i] if i < AHEAD else 0


def inverse_before(i):
    return 0 if i == AHEAD else i - 1


def root_step(nc, dve, step, n, view, j):
    V = nc.vector
    total, total_sq, v, r, mean = (view(q) for q in range(5))
    if j:
        dve.wait_ge(step, n[0])
    if j == 0:
        V.tensor_scalar(mean, total, 1.0 / C, None, ALU.mult)
        ins = V.scalar_tensor_tensor(out=v, in0=total, scalar=-1.0 / (C * C), in1=total, op0=ALU.mult, op1=ALU.mult)
    elif j == 1:
        ins = V.scalar_tensor_tensor(out=v, in0=total_sq, scalar=1.0 / C, in1=v, op0=ALU.mult, op1=ALU.add)
    elif j == 2:
        ins = V.tensor_scalar(v, v, 0.0, LN_EPS, ALU.max, ALU.add)
    elif j == 3:
        ins = V.tensor_scalar(r.bitcast(I32), v.bitcast(I32), 1, None, ALU.logical_shift_right)
    elif j == 4:
        ins = V.tensor_scalar(r.bitcast(I32), r.bitcast(I32), -1.0, float(RSQRT_GUESS), ALU.mult, ALU.add)
    elif j % 3 == 2:
        ins = V.tensor_tensor(total, r, r, ALU.mult)
    elif j % 3 == 0:
        ins = V.scalar_tensor_tensor(out=total, in0=total, scalar=-0.5, in1=v, op0=ALU.mult, op1=ALU.mult)
    else:
        ins = V.scalar_tensor_tensor(out=r, in0=total, scalar=1.5, in1=r, op0=ALU.add, op1=ALU.mult)
    n[0] += 1
    return ins.then_inc(step, 1)


def inverse_std(nc, dve, step, n, view, between={}):
    for j in range(ROOT_STEPS):
        root_step(nc, dve, step, n, view, j)
        if j in between:
            between[j]()
    dve.wait_ge(step, n[0])


def root_count(kind, t):
    return t + (1 if kind == 1 else 5)


def square_count(kind, t):
    if kind == 2:
        return t + 2
    return {0: 1, 1: 1, 2: 2}.get(t, t)


def afno_layers(nc, const, w, src, dst):
    with ExitStack() as ctx:
        def sb(name, shape, dtype=F32):
            return ctx.enter_context(nc.sbuf_tensor(f"a_{name}", shape, dtype))

        def sem(name):
            s = ctx.enter_context(nc.semaphore(f"a_{name}"))
            sems.append(s)
            return s

        sems = []
        bank = [ctx.enter_context(nc.psum_tensor(f"a_bank{i}", [P, BANK], F32)) for i in range(8)]

        x = sb("x", [P, C, P])
        y = sb("y", [P, C, P])
        m1 = y
        m2 = sb("m2", [P, C, P])
        m2_flat = m2[:].rearrange("p c h -> p (c h)")
        hidden = m2_flat[:, 0:8 * BANK].rearrange("p (r i n) -> p r i n", r=2, i=4)
        delta = m2_flat[:, 8 * BANK:10 * BANK].rearrange("p (r n) -> p r n", r=2)
        sq = m2_flat[:, 10 * BANK:10 * BANK + 2 * C * SH].rearrange("p (k c h) -> p k c h", k=2, c=C)
        g = sb("g", [P, KW, 2, C])
        iy = g[:].rearrange("p k r c -> p (k r c)")[:, 0:C * P].rearrange("p (c h) -> p c h", c=C)
        upper = sb("upper", [P, 2, C, SH])
        xf = sb("xf", [P, 2, BANK])
        o1 = sb("o1", [P, 2, BANK])
        o2 = sb("o2", [P, 2, 4, 2, C])
        mag = sb("mag", [P, 2, 4, 2, C])
        top = sb("top", [P, 2, 4, C])
        im = sb("im", [P, 2, 4, C])
        xc = sb("xc", [P, 2, C, HB])
        y2 = sb("y2", [P, 2, HB, C])
        y2s = sb("y2s", [P, 2, HB, 2, C], F16)
        yc = sb("yc", [P, 2, HB * P], F16)
        squares = iy
        sums = sb("sums", [P, P, LOADS])
        whole = sb("whole", [P, 5, P])
        stat = sb("stat", [P, 5, 3, 2, SH])
        ident, dft_w, dft_h, cos, sin, idft_w, centre = (
            sb(n, [P, P]) for n in ("ident", "dft_w", "dft_h", "cos", "sin", "idft_w", "centre"))
        mix1, mix1_s, mix1_fold, mix2 = (sb(n, [P, P]) for n in ("mix1", "mix1_s", "mix1_fold", "mix2"))
        mix1_b, mix1_b0 = sb("mix1_b", [P, 1]), sb("mix1_b0", [P, 1])
        mix2_b = sb("mix2_b", [P, 2, C])
        ln1 = sb("ln1", [P, 2])
        ln2 = sb("ln2", [P, 2])
        up, up_s = sb("up", [P, HID]), sb("up_s", [P, HID])
        up_w = sb("up_w", [P, 2, HID], F16)
        ident16 = sb("ident16", [P, P], F16)
        up_b = sb("up_b", [P, 2 * HC])
        down = sb("down", [P, HC, C])
        down_b = sb("down_b", [P, 1])

        s_part, s_store = [sem(f"part{i}") for i in range(LOADS)], [sem(f"store{i}") for i in range(LOADS)]
        sems.clear()
        s_const, s_w_mix, s_w, s_sums, s_squares = (sem(n) for n in ("const", "w_mix", "w", "sums", "squares"))
        s_copied = [sem(f"copied{i}") for i in range(LOADS)]
        s_pe_sums, s_std, s_pool_std = sem("pe_sums"), sem("std"), sem("pool_std")
        s_step, s_act_step, s_pool_step = sem("step"), sem("act_step"), sem("pool_step")
        s_sq, s_sq_read, s_y = [sem("sq0"), sem("sq1")], [sem("sq_read0"), sem("sq_read1")], sem("y")
        s_wscaled, s_wsplit, s_wfold, s_wready = (sem(n) for n in ("wscaled", "wsplit", "wfold", "wready"))
        s_zero = sem("zero")
        s_fw, s_g_dve, s_g_act = sem("fw"), sem("g_dve"), sem("g_act")
        s_fh, s_xf, s_mix1, s_o1, s_mix2, s_o2 = (sem(n) for n in ("fh", "xf", "mix1", "o1", "mix2", "o2"))
        s_mag, s_top, s_masked, s_m, s_m_pool = (sem(n) for n in ("mag", "top", "masked", "m", "m_pool"))
        s_ih, s_iy = sem("ih"), [sem("iy_dve"), sem("iy_act")]
        s_iw, s_x = sem("iw"), sem("x")
        s_mean, s_root, s_xc, s_high = sem("mean"), sem("root"), sem("xc"), sem("high")
        s_low = [sem("low_dve"), sem("low_pool")]
        s_y2, s_tr, s_yc, s_up, s_hid, s_down, s_delta, s_back, s_res = (
            sem(n) for n in ("y2", "tr", "yc", "up", "hid", "down", "delta", "back", "res"))

        def four(a):
            return a.rearrange("p (a b) -> p a b", a=4)

        def fold(eng, cs, rows, temp):
            mirrored = slice(P - rows.start, P - rows.stop, -1)
            eng.tensor_tensor(y[:, cs, rows], y[:, cs, mirrored], temp, ALU.subtract)
            return eng.tensor_tensor(y[:, cs, mirrored], y[:, cs, mirrored], temp, ALU.add)

        def copy_spectrum(i, copy, negate, eng, step, count):
            ps, cs = four(bank[i % 4][:]), slice(4 * i, 4 * i + 4)
            re, im = ps[:, :, 0:KW].rearrange("p c k -> p k c"), ps[:, :, KW:P].rearrange("p c k -> p k c")
            copy(g[HALF:P, 1:KW - 1, 0, cs], im[HALF:P])
            chain(eng, step, count, negate(g[HALF:P, :, 1, cs], re[HALF:P]))
            copy(g[0:HALF + 1, :, 0, cs], re[0:HALF + 1])
            return copy(g[0:HALF + 1, 1:KW - 1, 1, cs], im[0:HALF + 1])

        def wait_low(eng, i):
            eng.wait_ge(s_low[i >= 2], i + 1 if i < 2 else i - 1)

        def low_part(eng, i):
            eng.wait_ge(s_y2, i + 1)
            eng.wait_ge(s_high, i + 1)
            eng.tensor_tensor(y2s[:, i % 2, :, 1, :], y2[:, i % 2], y2s[:, i % 2, :, 0, :], ALU.subtract
                              ).then_inc(s_low[i >= 2], 1)

        with nc.Block() as block:
            @block.sync
            def _(sp):
                for t, i in ((ident, IDENT), (dft_w, DFT_W), (dft_h, DFT_H), (cos, COS), (sin, SIN),
                             (idft_w, IDFT_W), (centre, CENTRE)):
                    sp.dma_start(t[:], const[i]).then_inc(s_const, 16)
                sp.wait_ge(s_const, 16 * 7)

            @block.vector
            def _(dve):
                dve.wait_ge(s_const, 16 * 7)
                nc.vector.tensor_copy(ident16[:], ident[:])
        clear(nc, (s_const,))
        nc.all_engine_barrier()

        parts = [slice(i * C // LOADS, (i + 1) * C // LOADS) for i in range(LOADS)]
        STORE_ORDER = (2, 3, 0, 1)

        def image_in():
            lower, higher = slice(0, HALF + 1), slice(HALF + 1, P)

            def normalised(eng, cs):
                for rows, to in ((lower, y), (higher, squares)):
                    ins = eng.tensor_tensor(
                        to[:, cs, rows], x[:, cs, rows],
                        whole[:, 3, None, rows].broadcast_to([P, cs.stop - cs.start, rows.stop - rows.start]), ALU.mult)
                return ins

            def fold_image(eng, cs):
                fold(eng, cs, higher, squares[:, cs, higher])

            with nc.Block() as block:
                @block.scalar
                def _(act):
                    for i, cs in enumerate(parts):
                        act.wait_ge(s_part[i], 16)
                        nc.scalar.activation(squares[:, cs, :], y[:, cs, :], ACT.Square).then_inc(s_squares, 1)
                    for i in STORE_ORDER[1:]:
                        act.wait_ge(s_store[i], 16)
                        nc.scalar.activation(x[:, parts[i], :], y[:, parts[i], :], ACT.Copy).then_inc(s_copied[i], 1)

                @block.gpsimd
                def _(pool):
                    i = STORE_ORDER[0]
                    pool.wait_ge(s_part[i], 16)
                    pool.wait_ge(s_store[i], 16)
                    nc.gpsimd.tensor_copy(x[:, parts[i], :], y[:, parts[i], :]).then_inc(s_copied[i], 1)
                    pool.wait_ge(s_std, 1)
                    pool.wait_ge(s_copied[2], 1)
                    pool.wait_ge(s_copied[3], 1)
                    normalised(nc.gpsimd, slice(C - POOL_SHARE, C)).then_inc(s_pool_std, 1)
                    pool.wait_ge(s_pool_std, 1)
                    fold_image(nc.gpsimd, slice(C - POOL_SHARE, C))

                @block.tensor
                def _(pe):
                    first, last = GROUPS // LOADS, GROUPS - 1
                    for i in range(first, GROUPS):
                        if i % (GROUPS // LOADS) == 0:
                            pe.wait_ge(s_part[i * LOADS // GROUPS], 16)
                        mm = nc.tensor.matmul(bank[0][:], ident[:], y[:, 4 * i:4 * i + 4, :].rearrange("p c h -> p (c h)"),
                                              start=i == first, stop=i == last)
                    mm.then_inc(s_pe_sums, 1)

                @block.vector
                def _(dve):
                    n = [0]
                    V = nc.vector
                    dve.wait_ge(s_part[0], 16)
                    V.tensor_reduce(whole[:, 0, :], y[:, parts[0], :].rearrange("p c h -> p h c"), AX.X, ALU.add
                                    ).then_inc(s_sums, 1)
                    for i, cs in enumerate(parts):
                        dve.wait_ge(s_squares, i + 1)
                        V.tensor_reduce(sums[:, :, i], squares[:, cs, :].rearrange("p c h -> p h c"), AX.X, ALU.add
                                        ).then_inc(s_sums, 1)
                    dve.wait_ge(s_pe_sums, 1)
                    chain(dve, s_step, n, V.tensor_reduce(whole[:, 2, :], four(bank[0][:]).rearrange("p a h -> p h a"),
                                                          AX.X, ALU.add))
                    dve.wait_ge(s_sums, LOADS + 1)
                    V.tensor_tensor(whole[:, 0, :], whole[:, 0, :], whole[:, 2, :], ALU.add)
                    chain(dve, s_step, n, V.tensor_reduce(whole[:, 1, :], sums[:], AX.X, ALU.add))
                    inverse_std(nc, dve, s_step, n, lambda q: whole[:, q, :])
                    dve.sem_inc(s_std, 1)
                    mine = slice(0, C - POOL_SHARE)
                    for i in range(3):
                        dve.wait_ge(s_copied[i], 1)
                    chain(dve, s_step, n, normalised(V, mine))
                    fold_image(V, mine)
            clear(nc, (*s_part, *s_store, *s_copied, s_squares, s_sums, s_pe_sums, s_std, s_pool_std, s_step))
            nc.all_engine_barrier()

        def afno_block(l, last):
            kinds_taken = (1,) if last else (1, 2)
            with nc.Block() as block:
                @block.sync
                def _(sp):
                    with nc.allow_non_contiguous_dma("small weights"):
                        loads = []
                        for t, n in ((mix1, "w1"), (mix2, "w2")):
                            for rows in range(2):
                                for cols in range(2):
                                    loads.append((t[rows * C:(rows + 1) * C, cols * C:(cols + 1) * C],
                                                  w[n][l, (rows + cols) % 2]))
                        for t, n in ((ln1, "ln1"), (ln2, "ln2")):
                            for i in range(2):
                                loads.append((t[i * C:(i + 1) * C, 0:1],
                                              w[n + "_w"][l].rearrange("(c a) -> c a", a=1)))
                            loads.append((t[0:C, 1:2], w[n + "_b"][l].rearrange("(c a) -> c a", a=1)))
                        loads.append((mix1_b[:], w["b1"][l].rearrange("r (c a) -> (r c) a", a=1)))
                        loads.append((mix2_b[:].rearrange("p r c -> p (r c)"),
                                      w["b2"][l].rearrange("r c -> (r c)").partition_broadcast(P)))
                        for i in range(2):
                            loads.append((up[i * C:(i + 1) * C, :], w["mlp_w1"][l]))
                        loads.append((up_b[:, 0:HC], w["mlp_b1"][l].rearrange("(j p) -> p j", p=P)))
                        loads.append((down[:], w["mlp_w2"][l].rearrange("(j p) c -> p j c", p=P)))
                        for i in range(2):
                            loads.append((down_b[i * C:(i + 1) * C, :],
                                          w["mlp_b2"][l].rearrange("(c a) -> c a", a=1)))
                        assert len(loads) == N_WLOAD
                        for j, (o, i) in enumerate(loads):
                            sp.dma_start(o, i).then_inc(s_w_mix if j < N_WLOAD_MIX else s_w, 16)
                    if last:
                        sp.wait_ge(s_ih, GROUPS)
                        for i, cs in enumerate(parts):
                            sp.dma_start(y[:, cs, :], src[(b + 1) % B][:, cs, :]).then_inc(s_part[i], 16)
                        sp.wait_ge(s_res, BLOCKS)
                        for i in STORE_ORDER:
                            sp.dma_start(dst[b][:, parts[i], :], x[:, parts[i], :]).then_inc(s_store[i], 16)

                @block.gpsimd
                def _(pool):
                    nc.gpsimd.memset(g[0:HALF, 0:KW:KW - 1, 1, :], 0.0)
                    nc.gpsimd.memset(g[HALF:P, 0:KW:KW - 1, 0, :], 0.0).then_inc(s_zero, 1)
                    G = nc.gpsimd
                    n = [0]
                    pool.wait_ge(s_w_mix, 16 * N_WLOAD_MIX)
                    G.tensor_scalar(mix2[C:P, 0:C], mix2[C:P, 0:C], -1.0, None, ALU.mult)
                    chain(pool, s_pool_step, n, G.tensor_scalar(mix1[C:P, 0:C], mix1[C:P, 0:C], -1.0, None, ALU.mult))
                    G.tensor_scalar(mix1_s[:], mix1[:], ln1[:, 0:1], None, ALU.mult).then_inc(s_wscaled, 1)
                    pool.wait_ge(s_g_dve, GROUPS // 2)
                    pool.wait_ge(s_g_act, GROUPS // 2)
                    pool.wait_ge(s_wscaled, 1)
                    nc.gpsimd.memset(g[HALF:HALF + 1, 0:KW:KW - 1, 1, :], 0.0).then_inc(s_zero, 1)
                    pool.wait_ge(s_zero, 2)
                    pool.wait_ge(s_w, 16 * (N_WLOAD - N_WLOAD_MIX))
                    chain(pool, s_pool_step, n, G.tensor_scalar(up_s[:], up[:], ln2[:, 0:1], W_SCALE, ALU.mult, ALU.mult))
                    chain(pool, s_pool_step, n, G.tensor_copy(up_w[:, 0, :], up_s[:]))
                    G.tensor_tensor(up_w[:, 1, :], up_s[:], up_w[:, 0, :], ALU.subtract).then_inc(s_wsplit, 1)
                    for j in range(N_CHUNK - 1):
                        pool.wait_ge(s_masked, j + 1)
                        lo, col = (1 if j == 0 else 0), 4 * j
                        G.tensor_copy(m2[:, :, HALF + col + lo:HALF + col + 4], m1[:, :, col + lo:col + 4]
                                      ).then_inc(s_m_pool, 1)

                    def centre(i):
                        hs, t = slice(i * HB, (i + 1) * HB), i // STRIP
                        if t < 2:
                            pool.wait_ge(s_mean, t + 1)
                        else:
                            pool.wait_ge(s_root, root_count(1, t))
                        if i >= 2:
                            pool.wait_ge(s_y2, i - 1)
                        mean = stat[:, 4, t % 3, 0, i % STRIP * HB:(i % STRIP + 1) * HB]
                        nc.gpsimd.tensor_tensor(xc[:, i % 2], x[:, :, hs], mean[:, None, :].broadcast_to([P, C, HB]),
                                                ALU.subtract).then_inc(s_xc, 1)

                    def next_y(t):
                        hs = slice(t * SH, (t + 1) * SH)
                        std = stat[:, 3, (t + 1) % 3, 1, :][:, None, :]
                        pool.wait_ge(s_root, root_count(2, t))
                        to = y[:, :, hs] if t < STRIPS // 2 else upper[:, t % 2]
                        if t == STRIPS // 2:
                            nc.gpsimd.tensor_tensor(y[:, :, HALF:HALF + 1], x[:, :, HALF:HALF + 1],
                                                    std[:, :, 0:1].broadcast_to([P, C, 1]), ALU.mult)
                        nc.gpsimd.tensor_tensor(to, x[:, :, hs], std.broadcast_to([P, C, SH]), ALU.mult
                                                ).then_inc(s_y, 1)
                        if t >= STRIPS // 2:
                            skip = 1 if t == STRIPS // 2 else 0
                            pool.wait_ge(s_y, t + 1)
                            fold(nc.gpsimd, slice(0, C), slice(t * SH + skip, (t + 1) * SH), upper[:, t % 2, :, skip:])

                    centre(0)
                    centre(1)
                    centre(2)
                    for p in range(PAIRS):
                        for i in (2 * p, 2 * p + 1):
                            if 2 <= i + 1 < BLOCKS:
                                low_part(nc.gpsimd, i + 1)
                            if i + 3 < BLOCKS:
                                centre(i + 3)
                        if not last and 3 <= p < STRIPS + 2:
                            next_y(p - 3)

                @block.vector
                def _(dve):
                    n = [0]
                    V = nc.vector

                    dve.wait_ge(s_zero, 1)
                    for i in range(0, GROUPS, 2):
                        dve.wait_ge(s_fw, i + 1)
                        copy_spectrum(i, V.tensor_copy, lambda o, a: V.tensor_scalar(o, a, -1.0, None, ALU.mult),
                                      dve, s_step, n).then_inc(s_g_dve, 1)
                    dve.wait_ge(s_wfold, 1)
                    V.tensor_copy(mix1_fold[:], bank[7][:, 0:P])
                    V.scalar_tensor_tensor(out=mix1_b0[:], in0=bank[5][:, 0:1], scalar=float(P), in1=mix1_b[:],
                                           op0=ALU.mult, op1=ALU.add)
                    V.tensor_tensor(up_b[:, HC:2 * HC], bank[5][:, 1:1 + HC], up_b[:, 0:HC], ALU.add
                                    ).then_inc(s_wready, 1)
                    for t in range(N_CHUNK + 3):
                        if t < N_CHUNK:
                            k = chunk(t)
                            dve.wait_ge(s_fh, t + 1)
                            if t >= 2:
                                dve.wait_ge(s_mix1, t - 1)
                            V.tensor_copy(xf[:, t % 2, 0:k * P], bank[2 + t % 2][:, 0:k * P]).then_inc(s_xf, 1)
                        j = t - 2
                        if 0 <= j < N_CHUNK:
                            k = chunk(j)
                            dve.wait_ge(s_mix2, j + 1)
                            if j >= 2:
                                dve.wait_ge(s_masked, j - 1)
                                dve.wait_ge(s_mag, j - 1)
                            V.tensor_tensor(o2[:, j % 2, 0:k].rearrange("p k r c -> p k (r c)"),
                                            four(bank[6 + j % 2][:])[:, 0:k],
                                            mix2_b[:].rearrange("p r c -> p (r c)")[:, None, :
                                            ].broadcast_to([P, k, P]), ALU.add).then_inc(s_o2, 1)
                        j = t - 3
                        if 0 <= j < N_CHUNK:
                            k = chunk(j)
                            dve.wait_ge(s_mag, j + 1)
                            V.tensor_tensor(top[:, j % 2, 0:k], mag[:, j % 2, 0:k, 0], mag[:, j % 2, 0:k, 1],
                                            ALU.max).then_inc(s_top, 1)
                            dve.wait_ge(s_top, j + 1)
                            col = 4 * j
                            V.scalar_tensor_tensor(
                                out=m1[:, :, col:col + k].rearrange("p c k -> p k c"),
                                in0=top[:, j % 2, 0:k], scalar=THR, in1=o2[:, j % 2, 0:k, 0],
                                op0=ALU.is_gt, op1=ALU.mult)
                            if j >= 2:
                                dve.wait_ge(s_m, j - 1)
                            V.scalar_tensor_tensor(
                                out=im[:, j % 2, 0:k], in0=top[:, j % 2, 0:k], scalar=THR,
                                in1=o2[:, j % 2, 0:k, 1], op0=ALU.is_gt, op1=ALU.mult).then_inc(s_masked, 1)
                    for i in range(0, GROUPS, 2):
                        dve.wait_ge(s_ih, i + 1)
                        V.tensor_copy(iy[:, 4 * i:4 * i + 4, :], four(bank[0][:])).then_inc(s_iy[0], 1)

                    def first_residual(i):
                        xb = x[:, :, i * HB:(i + 1) * HB]
                        dve.wait_ge(s_iw, i + 1)
                        V.tensor_tensor(xb, bank[inverse_bank(i)].rearrange("p (c h) -> p c h", h=HB), xb,
                                        ALU.add).then_inc(s_x, 1)

                    def normalise(i):
                        t = i // STRIP
                        dve.wait_ge(s_xc, i + 1)
                        if i >= 2:
                            dve.wait_ge(s_high, i - 1)
                            wait_low(dve, i - 2)
                        r = stat[:, 3, t % 3, 0, i % STRIP * HB:(i % STRIP + 1) * HB]
                        V.tensor_tensor(y2[:, i % 2].rearrange("p h c -> p c h"), xc[:, i % 2],
                                        r[:, None, :].broadcast_to([P, C, HB]), ALU.mult).then_inc(s_y2, 1)

                    def second_residual(i):
                        xb = x[:, :, i * HB:(i + 1) * HB].rearrange("p c (q k) -> p k q c", q=2)
                        dve.wait_ge(s_back, i + 1)
                        V.tensor_tensor(xb, bank[1].rearrange("p (k q c) -> p k q c", q=2, c=C), xb, ALU.add
                                        ).then_inc(s_res, 1)

                    def sum_up(kind, t, slot):
                        dve.wait_ge((s_x, s_res)[kind - 1], (t + 1) * STRIP)
                        if kind == 2 and t >= 3:
                            dve.wait_ge(s_y, t - 2)
                        V.tensor_reduce(stat[:, 0, slot, kind - 1], x[:, :, t * SH:(t + 1) * SH].rearrange(
                            "p c h -> p h c"), AX.X, ALU.add)

                    def sum_squares(kind, t, slot, buffer):
                        dve.wait_ge(s_sq[buffer], square_count(kind, t))
                        V.tensor_reduce(stat[:, 1, slot, kind - 1], sq[:, buffer].rearrange("p c h -> p h c"), AX.X,
                                        ALU.add).then_inc(s_sq_read[buffer], 1)
                        dve.wait_ge(s_sq_read[buffer], square_count(kind, t))

                    def mean_ready():
                        dve.wait_ge(s_step, n[0])
                        dve.sem_inc(s_mean, 1)

                    first_residual(0)
                    first_residual(1)
                    sum_up(1, 0, 0)
                    sum_squares(1, 0, 0, 0)
                    inverse_std(nc, dve, s_step, n, lambda q: stat[:, q, 0, 0, :],
                                {0: mean_ready, 2: lambda: first_residual(2), 5: lambda: first_residual(3),
                                 8: lambda: first_residual(4), 11: lambda: first_residual(5)})
                    normalise(0)
                    normalise(1)
                    low_part(nc.vector, 0)
                    sum_up(1, 1, 1)
                    low_part(nc.vector, 1)
                    sum_squares(1, 1, 1, 1)
                    inverse_std(nc, dve, s_step, n, lambda q: stat[:, q, 1, 0, :], {0: mean_ready})
                    dve.sem_inc(s_root, 2)
                    sum_up(1, 2, 2)
                    for p in range(PAIRS):
                        mine = [(kind, t) for kind, t in ((1, p + 2), (2, p - 2))
                                if 0 <= t < STRIPS and kind in kinds_taken]
                        slot = (p + 2) % 3
                        kinds = slice(mine[0][0] - 1, mine[-1][0]) if mine else None

                        def root(lo, hi):
                            for j in range(lo, hi):
                                if mine:
                                    root_step(nc, dve, s_step, n, lambda q: stat[:, q, slot, kinds, :], j)

                        for odd in range(2):
                            i = 2 * p + odd
                            if i + 2 < BLOCKS:
                                normalise(i + 2)
                            if odd:
                                root(5, 7)
                            if odd:
                                root(7, 9)
                            else:
                                for kind, t in mine:
                                    sum_squares(kind, t, slot, kind - 1)
                                root(0, 1)
                            if 0 <= i - 2 < BLOCKS:
                                second_residual(i - 2)
                            root(9, 11) if odd else root(1, 3)
                            if i + AHEAD < BLOCKS:
                                first_residual(i + AHEAD)
                            root(11, ROOT_STEPS) if odd else root(3, 5)
                        if mine:
                            dve.wait_ge(s_step, n[0])
                            dve.sem_inc(s_root, 1)
                        for kind, t in ((1, p + 3), (2, p - 1)):
                            if 0 <= t < STRIPS and kind in kinds_taken:
                                sum_up(kind, t, (p + 3) % 3)
                    if not last:
                        hs = slice((STRIPS - 1) * SH, P)
                        dve.wait_ge(s_y, STRIPS - 1)
                        chain(dve, s_step, n, V.tensor_tensor(
                            upper[:, 1], x[:, :, hs], stat[:, 3, STRIPS % 3, 1, :][:, None, :].broadcast_to([P, C, SH]),
                            ALU.mult))
                        fold(V, slice(0, C), hs, upper[:, 1])

                @block.scalar
                def _(act):
                    A = nc.scalar.activation

                    act.wait_ge(s_zero, 1)
                    n = [0]
                    for i in range(1, GROUPS, 2):
                        act.wait_ge(s_fw, i + 1)
                        copy_spectrum(i, lambda o, a: A(o, a, ACT.Copy), lambda o, a: A(o, a, ACT.Copy, scale=-1.0),
                                      act, s_act_step, n).then_inc(s_g_act, 1)
                    act.wait_ge(s_wready, 1)
                    for t in range(1, N_CHUNK + 3):
                        j = t - 1
                        if j < N_CHUNK:
                            cols = chunk(j) * P
                            act.wait_ge(s_mix1, j + 1)
                            if j >= 2:
                                act.wait_ge(s_mix2, j - 1)
                            first = 0
                            if j == 0:
                                A(o1[:, 0, 0:1], bank[4][:, 0:1], ACT.Relu, bias=mix1_b0[:])
                                first = 1
                            A(o1[:, j % 2, first:cols], bank[4 + j % 2][:, first:cols], ACT.Relu, bias=mix1_b[:]
                              ).then_inc(s_o1, 1)
                        j = t - 2
                        if 0 <= j < N_CHUNK:
                            k = chunk(j)
                            act.wait_ge(s_o2, j + 1)
                            if j >= 2:
                                act.wait_ge(s_top, j - 1)
                            A(mag[:, j % 2, 0:k], o2[:, j % 2, 0:k], ACT.Abs).then_inc(s_mag, 1)
                        j = t - 3
                        if 0 <= j < N_CHUNK:
                            k, col = chunk(j), 4 * j
                            act.wait_ge(s_masked, j + 1)
                            ins = A(m2[:, :, col:col + k].rearrange("p c k -> p k c"), im[:, j % 2, 0:k],
                                    ACT.Copy, scale=-1.0)
                            if j < N_CHUNK - 1:
                                lo = 1 if j == 0 else 0
                                to = slice(HALF + col + lo, HALF + col + 4)
                                ins = A(m1[:, :, to].rearrange("p c k -> p k c"), im[:, j % 2, lo:4], ACT.Copy)
                            ins.then_inc(s_m, 1)
                    for i in range(1, GROUPS, 2):
                        act.wait_ge(s_ih, i + 1)
                        A(iy[:, 4 * i:4 * i + 4, :], four(bank[1][:]), ACT.Copy).then_inc(s_iy[1], 1)

                    def square(kind, t, buffer):
                        act.wait_ge((s_x, s_res)[kind - 1], (t + 1) * STRIP)
                        if square_count(kind, t) > 1:
                            act.wait_ge(s_sq_read[buffer], square_count(kind, t) - 1)
                        A(sq[:, buffer], x[:, :, t * SH:(t + 1) * SH], ACT.Square).then_inc(s_sq[buffer], 1)

                    def transposed(i):
                        act.wait_ge(s_tr, i + 1)
                        if i >= 2:
                            act.wait_ge(s_up, 4 * (i - 1))
                        if i < 3:
                            for half in range(2):
                                cols = slice(half * BANK, (half + 1) * BANK)
                                A(yc[:, i % 2, cols], bank[2][:].bitcast(F16)[:, cols], ACT.Copy).then_inc(s_yc, 1)
                        else:
                            A(yc[:, i % 2, :], bank[2][:].bitcast(F16), ACT.Copy).then_inc(s_yc, 2)

                    def high_part(i):
                        act.wait_ge(s_y2, i + 1)
                        if i >= 2:
                            act.wait_ge(s_tr, i - 1)
                        A(y2s[:, i % 2, :, 0, :], y2[:, i % 2], ACT.Copy).then_inc(s_high, 1)

                    square(1, 0, 0)
                    square(1, 1, 1)
                    high_part(0)
                    square(1, 2, 0)
                    high_part(1)
                    transposed(0)
                    for i in range(2 * PAIRS):
                        if i < BLOCKS:
                            for j in range(4):
                                act.wait_ge(s_up, 4 * i + j + 1)
                                if i >= 2 and j == 0:
                                    act.wait_ge(s_down, i - 1)
                                A(hidden[:, i % 2, j, :], bank[4 + j][:], ACT.Gelu, scale=1.0 / W_SCALE,
                                  bias=up_b[:, HC + j % HC:HC + j % HC + 1]).then_inc(s_hid, 1)
                        if i + 1 < BLOCKS:
                            transposed(i + 1)
                        if i + 2 < BLOCKS:
                            high_part(i + 2)
                        if 0 <= i - 1 < BLOCKS:
                            act.wait_ge(s_down, i)
                            if i >= 3:
                                act.wait_ge(s_back, i - 2)
                            A(delta[:, (i - 1) % 2, :], bank[3][:], ACT.Identity, bias=down_b[:]
                              ).then_inc(s_delta, 1)
                        if i % 2:
                            for kind, t in ((1, i // 2 + 3), (2, i // 2 - 1)):
                                if 0 <= t < STRIPS and kind in kinds_taken:
                                    square(kind, t, kind - 1)

                @block.tensor
                def _(pe):
                    M = nc.tensor.matmul
                    for i in range(GROUPS):
                        if i >= 4:
                            pe.wait_ge((s_g_dve, s_g_act)[i % 2], i // 2 - 1)
                        for c in range(4):
                            mm = M(bank[i % 4][:, c * P:(c + 1) * P], y[:, 4 * i + c, :], dft_w[:], start=True,
                                   stop=True)
                        mm.then_inc(s_fw, 1)
                    pe.wait_ge(s_wscaled, 1)
                    M(bank[7][:, 0:P], centre[:], mix1_s[:], start=True, stop=True)
                    M(bank[5][:, 0:1], mix1[0:C, :], ln1[0:C, 1:2], start=True, stop=True)
                    pe.wait_ge(s_w, 16 * (N_WLOAD - N_WLOAD_MIX))
                    for j in range(HC):
                        mm = M(bank[5][:, 1 + j:2 + j], up[0:C, j * P:(j + 1) * P], ln2[0:C, 1:2], start=True,
                               stop=True)
                    mm.then_inc(s_wfold, 1)
                    for i in range(N_CHUNK + 2):
                        if i < N_CHUNK:
                            if i == 0:
                                pe.wait_ge(s_g_dve, GROUPS // 2)
                                pe.wait_ge(s_g_act, GROUPS // 2)
                                pe.wait_ge(s_zero, 2)
                            if i >= 2:
                                pe.wait_ge(s_xf, i - 1)
                            for k in range(chunk(i)):
                                kw = 4 * i + k
                                mm = M(bank[2 + i % 2][:, k * P:(k + 1) * P],
                                       g[:, kw].rearrange("p r c -> p (r c)"), dft_h[:], start=True, stop=True)
                            mm.then_inc(s_fh, 1)
                        j = i - 1
                        if 0 <= j < N_CHUNK:
                            if j == 0:
                                pe.wait_ge(s_wready, 1)
                            pe.wait_ge(s_xf, j + 1)
                            if j >= 2:
                                pe.wait_ge(s_o1, j - 1)
                            cols = chunk(j) * P
                            M(bank[4 + j % 2][:, 0:cols], mix1_fold[:], xf[:, j % 2, 0:cols], start=True, stop=True
                              ).then_inc(s_mix1, 1)
                        j = i - 2
                        if 0 <= j < N_CHUNK:
                            pe.wait_ge(s_o1, j + 1)
                            if j >= 2:
                                pe.wait_ge(s_o2, j - 1)
                            for k in range(chunk(j)):
                                mm = M(bank[6 + j % 2][:, k * P:(k + 1) * P], o1[:, j % 2, k * P:(k + 1) * P],
                                       mix2[:], start=True, stop=True)
                            mm.then_inc(s_mix2, 1)
                    pe.wait_ge(s_m, N_CHUNK)
                    pe.wait_ge(s_m_pool, N_CHUNK - 1)
                    for i in range(GROUPS):
                        if i >= 2:
                            pe.wait_ge(s_iy[i % 2], i // 2)
                        for c in range(4):
                            to = bank[i % 2][:, c * P:(c + 1) * P]
                            M(to, m1[:, 4 * i + c, :], cos[:], start=True, stop=False)
                            mm = M(to, m2[:, 4 * i + c, :], sin[:], start=False, stop=True)
                        mm.then_inc(s_ih, 1)
                    pe.wait_ge(s_iy[0], GROUPS // 2)
                    pe.wait_ge(s_iy[1], GROUPS // 2)

                    def inverse(i):
                        if i >= AHEAD:
                            pe.wait_ge(s_x, inverse_before(i) + 1)
                        M(bank[inverse_bank(i)][:], idft_w[:], iy[:, :, i * HB:(i + 1) * HB], start=True, stop=True
                          ).then_inc(s_iw, 1)

                    def turn(i):
                        wait_low(pe, i)
                        if i >= 1:
                            pe.wait_ge(s_yc, 2 * i)
                        for h in range(HB):
                            mm = nc.tensor.transpose(bank[2][:].bitcast(F16)[:, h * P:(h + 1) * P],
                                                     y2s[:, i % 2, h].rearrange("p r c -> p (r c)"), ident16[:])
                        mm.then_inc(s_tr, 1)

                    def mlp_up(i):
                        if i == 0:
                            pe.wait_ge(s_wsplit, 1)
                        for j in range(4):
                            if j % HC == 0:
                                pe.wait_ge(s_yc, 2 * i + j // HC + 1)
                            if i >= 1:
                                pe.wait_ge(s_hid, 4 * (i - 1) + j + 1)
                            else:
                                pe.wait_ge(s_x, j + 3)
                            for part in range(2):
                                mm = M(bank[4 + j][:], up_w[:, part, j % HC * P:(j % HC + 1) * P],
                                       yc[:, i % 2, j // HC * BANK:(j // HC + 1) * BANK], start=part == 0,
                                       stop=part == 1)
                            mm.then_inc(s_up, 1)

                    def mlp_down(i):
                        pe.wait_ge(s_hid, 4 * (i + 1))
                        if i >= 1:
                            pe.wait_ge(s_delta, i)
                        for j in range(4):
                            chunk, half = divmod(j, 2)
                            mm = M(bank[3][half * C:(half + 1) * C, :], down[:, chunk, :],
                                   hidden[:, i % 2, half * HC + chunk, :], start=chunk == 0, stop=chunk == HC - 1)
                        mm.then_inc(s_down, 1)

                    def turn_back(i):
                        pe.wait_ge(s_delta, i + 1)
                        pe.wait_ge(s_x, 2)
                        if i >= 1:
                            pe.wait_ge(s_res, i)
                        for k in range(HB // 2):
                            mm = nc.tensor.transpose(bank[1][:, k * P:(k + 1) * P],
                                                     delta[:, i % 2, k * P:(k + 1) * P], ident[:])
                        mm.then_inc(s_back, 1)

                    for i in range(AHEAD):
                        inverse(i)
                    turn(0)
                    for i in range(BLOCKS + 2):
                        if i < BLOCKS:
                            mlp_up(i)
                        if 0 <= i - 2 < BLOCKS:
                            turn_back(i - 2)
                        if i + AHEAD < BLOCKS:
                            inverse(i + AHEAD)
                        if i == 1:
                            mlp_down(0)
                        if i + 1 < BLOCKS:
                            turn(i + 1)
                        if 1 <= i - 1 < BLOCKS:
                            mlp_down(i - 1)
            clear(nc, sems)
            nc.all_engine_barrier()

        with nc.Block() as block:
            @block.sync
            def _(sp):
                for i, cs in enumerate(parts):
                    sp.dma_start(y[:, cs, :], src[0][:, cs, :]).then_inc(s_part[i], 16)
                    sp.sem_inc(s_store[i], 16)
        with nc.Fori(0, B) as b:
            image_in()
            with nc.Fori(0, L - 1) as l:
                afno_block(l, False)
            afno_block(L - 1, True)
        with nc.Block() as block:
            @block.sync
            def _(sp):
                for i in range(LOADS):
                    sp.wait_ge(s_store[i], 16)
                    sp.wait_ge(s_part[i], 16)
        clear(nc, (*s_part, *s_store))
        nc.all_engine_barrier()


LAYER_INPUTS = {
    "L0_conv": ["w1", "bn1_gamma", "bn1_beta", "bn1_mean", "bn1_var", "x_min", "x_max", "y_min", "y_max",
                "bn2_gamma", "bn2_beta", "bn2_mean", "bn2_var"],
    "L1_conv": ["ln1_w", "ln1_b", "ln2_w", "ln2_b", "w1", "w2", "b1", "b2", "mlp_w1", "mlp_b1", "mlp_w2", "mlp_b2"],
}
LAYER_INPUTS["L2_conv"] = LAYER_INPUTS["L3_conv"] = LAYER_INPUTS["L0_conv"]


def build(nc, ins, out):
    const = ins["constants"]
    part = {t: {n: ins[f"{t}_{n}"] for n in names} for t, names in LAYER_INPUTS.items()}

    def scratch(name, shape):
        return nc.dram_tensor(name, shape, F32, kind="Internal").ap()

    turned = [scratch(f"turned{i}", [B, P, C, P]) for i in range(3)]
    z = [scratch(f"z{i}", [B, K, P, P]) for i in range(3)]
    x = ins["x"]

    def edges(w, p, q):
        return w | {"p_max": w[p + "_max"], "p_min": w[p + "_min"], "q_max": w[q + "_max"], "q_min": w[q + "_min"]}

    def from_turned(t):
        return {"pcq": lambda b: t[b], "half": lambda b, h: t[b, h * HALF:(h + 1) * HALF].rearrange("w c h -> c w h")}

    with nc.semaphore("par") as s_par, ExitStack() as ctx:
        s_z_out = [ctx.enter_context(nc.semaphore(f"z_out{i}")) for i in range(4)]
        box_layer(nc, 0, const, edges(part["L0_conv"], "x", "y"), True,
                  {"pcq": lambda b: x[b].rearrange("c h w -> h c w"), "half": lambda b, h: x[b, :, h * HALF:(h + 1) * HALF]},
                  lambda b: turned[0][b], z[0], s_par, s_z_out)
        afno_layers(nc, const, part["L1_conv"], turned[0], turned[1])
        box_layer(nc, 1, const, edges(part["L2_conv"], "y", "x"), False, from_turned(turned[1]),
                  lambda b: turned[2][b], z[1], s_par, s_z_out)
        box_layer(nc, 2, const, edges(part["L3_conv"], "y", "x"), True, from_turned(turned[2]),
                  lambda b: out[b].rearrange("c h w -> h c w"), z[2], s_par, s_z_out)


def kernel(**inputs):
    import concourse.bacc as bacc
    from concourse.bass_utils import run_bass_kernel_spmd

    nc = bacc.Bacc("TRN2", target_bir_lowering=False, num_devices=1)
    names = ["x"] + [f"{t}_{n}" for t, ns in LAYER_INPUTS.items() for n in ns]
    arrays = {n: np.ascontiguousarray(inputs[n]) for n in names}
    arrays["constants"] = constants()
    aps = {n: nc.dram_tensor(f"in_{n}", a.shape, mybir.dt.from_np(a.dtype), kind="ExternalInput").ap()
           for n, a in arrays.items()}
    out = nc.dram_tensor("out", (B, C, P, P), F32, kind="ExternalOutput").ap()
    build(nc, aps, out)
    r = run_bass_kernel_spmd(nc, [{f"in_{n}": a for n, a in arrays.items()}], core_ids=[0])
    return r.results[0]["out"]
```
